# Optimizing a Trainium2 kernel written in Bass

```python
import numpy as np
import jax
import jax.numpy as jnp

def _softmax(x, axis=-1):
    return jax.nn.softmax(x, axis=axis)

def _gelu(x):
    return jax.nn.gelu(x, approximate=True)

def _silu(x):
    return jax.nn.silu(x)

def _sigmoid(x):
    return jax.nn.sigmoid(x)

def _layernorm(x, axis=-1, eps=1e-05):
    m = jnp.mean(x, axis=axis, keepdims=True)
    v = jnp.var(x, axis=axis, keepdims=True)
    return (x - m) / jnp.sqrt(v + eps)

def _scatter_add(tgt, idx, src, axis=0):
    return tgt.at[idx].add(src)

def _segment_sum(src, seg, n):
    return jax.ops.segment_sum(src, seg, n)
kernel_name = 'mk_gnn_ffn_d2_gnn_r8_d11566'

def setup_inputs(seed: int=0):
    np.random.seed(seed)
    _w = jnp.asarray

    def _rec_inputs():
        import jax
        import jax.numpy as jnp
        _gk = jax.random.key(seed)
        x = -0.0002117 + 1 * jax.random.normal(jax.random.fold_in(_gk, 1), (6250, 512), jnp.float32)
        src = jax.random.randint(jax.random.fold_in(_gk, 2), (100000,), 0, 6250, jnp.int32)
        dst = jax.random.randint(jax.random.fold_in(_gk, 3), (100000,), 0, 6250, jnp.int32)
        _o = jnp.argsort(dst, stable=True)
        src = src[_o]
        dst = dst[_o]
        node_vec1 = jax.random.uniform(jax.random.fold_in(_gk, 12), (6250, 1), jnp.float32, 0.0, 1.49996)
        return (x, src, dst, node_vec1)
    x, src, dst, node_vec1 = _rec_inputs()

    def _L0_gnn_setup():
        import jax, jax.numpy as jnp
        import numpy as np
        N = 6250
        E = 100000
        D = 512
        H = D // 64
        LN_EPS = 1e-05

        def _gcn_conv(x, W, b, src, dst, norm):
            h = x @ W
            msg = h[src] * norm[:, None]
            out = jax.ops.segment_sum(msg, dst, num_segments=N)
            return out + b
        key = jax.random.key(seed)
        ks = jax.random.split(key, 6)
        x = jax.random.normal(ks[0], (N, D), dtype=jnp.float32)
        edge_index = jax.random.randint(ks[1], (2, E), 0, N, dtype=jnp.int64)
        size_factors = jax.random.uniform(ks[2], (N, 1), dtype=jnp.float32) + 0.5
        s1 = float(1.0 / np.sqrt(D))
        W1 = jax.random.uniform(ks[3], (D, H), jnp.float32, -s1, s1)
        b1 = jnp.zeros((H,), jnp.float32)
        gamma = jnp.ones((H,), jnp.float32)
        beta = jnp.zeros((H,), jnp.float32)
        s2 = float(1.0 / np.sqrt(H))
        W2 = jax.random.uniform(ks[4], (H, D), jnp.float32, -s2, s2)
        b2 = jnp.zeros((D,), jnp.float32)
        return {'x': x, 'size_factors': size_factors, 'W1': W1, 'b1': b1, 'gamma': gamma, 'beta': beta, 'W2': W2, 'b2': b2, 'edge_index': edge_index}
    _L0_gnn_all = _L0_gnn_setup()
    _L0_gnn_in = {k: v for k, v in _L0_gnn_all.items() if k in ('W1', 'b1', 'gamma', 'beta', 'W2', 'b2')}
    del _L0_gnn_all

    def _L0_ffn_setup():
        import jax, jax.numpy as jnp
        import numpy as np
        DIM = 512
        FFN_DIM = 1408
        GROUP = 128
        EPS = 1e-05

        def _quantize_weight(w, group_size):
            o, i = w.shape
            wg = w.reshape(o, i // group_size, group_size)
            scale = jnp.mean(jnp.abs(wg), axis=-1, keepdims=True) + EPS
            wq = jnp.clip(jnp.round(wg / scale), -1.0, 1.0) * scale
            return wq.reshape(o, i)

        def _bitlinear(x, w, group_size=GROUP):
            wq = w + jax.lax.stop_gradient(_quantize_weight(w, group_size) - w)
            return jnp.einsum('bsd,fd->bsf', x, wq)
        key = jax.random.key(seed)
        k_x, k_g, k_u, k_d = jax.random.split(key, 4)
        x = jax.random.normal(k_x, (8, 512, DIM), dtype=jnp.float32)
        sd_in = 1.0 / np.sqrt(DIM)
        sd_ffn = 1.0 / np.sqrt(FFN_DIM)
        w_gate = jax.random.normal(k_g, (FFN_DIM, DIM), dtype=jnp.float32) * sd_in
        w_up = jax.random.normal(k_u, (FFN_DIM, DIM), dtype=jnp.float32) * sd_in
        w_down = jax.random.normal(k_d, (DIM, FFN_DIM), dtype=jnp.float32) * sd_ffn
        return {'x': x, 'w_gate': w_gate, 'w_up': w_up, 'w_down': w_down}
    _L0_ffn_all = _L0_ffn_setup()
    _L0_ffn_in = {k: v for k, v in _L0_ffn_all.items() if k in ('w_gate', 'w_up', 'w_down')}
    del _L0_ffn_all

    def _L1_gnn_setup():
        import jax, jax.numpy as jnp
        import numpy as np
        N = 6250
        DIM = 512
        E = 18750
        key = jax.random.key(seed)
        k_x, k_src, k_dst, k_w, k_b = jax.random.split(key, 5)
        x = jax.random.normal(k_x, (N, DIM), dtype=jnp.float32)
        src = jax.random.randint(k_src, (E,), 0, N)
        dst = jax.random.randint(k_dst, (E,), 0, N)
        edge_index = jnp.stack([src, dst], axis=0)
        bound = 1.0 / np.sqrt(DIM)
        W = jax.random.uniform(k_w, (DIM, DIM), minval=-bound, maxval=bound, dtype=jnp.float32)
        b = jax.random.uniform(k_b, (DIM,), minval=-bound, maxval=bound, dtype=jnp.float32)
        alpha = jnp.float32(0.5)
        return {'x': x, 'edge_index': edge_index, 'num_nodes': N, 'alpha': alpha, 'W': W, 'b': b}
    _L1_gnn_all = _L1_gnn_setup()
    _L1_gnn_in = {k: v for k, v in _L1_gnn_all.items() if k in ('alpha', 'W', 'b')}
    del _L1_gnn_all

    def _L1_ffn_setup():
        import jax, jax.numpy as jnp
        import numpy as np
        CAPACITY_FACTOR = 1.2
        key = jax.random.key(seed)
        k1, k2, k3 = jax.random.split(key, 3)
        B, S, D, E = (8, 512, 512, 16)
        x = jax.random.normal(k1, (B, S, D), dtype=jnp.float32)
        switch_w = jax.random.normal(k2, (E, D), dtype=jnp.float32) * 0.02
        switch_b = jnp.zeros((E,), dtype=jnp.float32)
        expert_w = jax.random.normal(k3, (E, D, D), dtype=jnp.float32) * 0.02
        expert_b = jnp.zeros((E, D), dtype=jnp.float32)
        return {'x': x, 'switch_w': switch_w, 'switch_b': switch_b, 'expert_w': expert_w, 'expert_b': expert_b}
    _L1_ffn_all = _L1_ffn_setup()
    _L1_ffn_in = {k: v for k, v in _L1_ffn_all.items() if k in ('switch_w', 'switch_b', 'expert_w', 'expert_b')}
    del _L1_ffn_all
    return {'x': x, 'src': src, 'dst': dst, 'node_vec1': node_vec1, 'L0_gnn_W1': _L0_gnn_in['W1'], 'L0_gnn_b1': _L0_gnn_in['b1'], 'L0_gnn_gamma': _L0_gnn_in['gamma'], 'L0_gnn_beta': _L0_gnn_in['beta'], 'L0_gnn_W2': _L0_gnn_in['W2'], 'L0_gnn_b2': _L0_gnn_in['b2'], 'L0_ffn_w_gate': _L0_ffn_in['w_gate'], 'L0_ffn_w_up': _L0_ffn_in['w_up'], 'L0_ffn_w_down': _L0_ffn_in['w_down'], 'L1_gnn_alpha': _L1_gnn_in['alpha'], 'L1_gnn_W': _L1_gnn_in['W'], 'L1_gnn_b': _L1_gnn_in['b'], 'L1_ffn_switch_w': _L1_ffn_in['switch_w'], 'L1_ffn_switch_b': _L1_ffn_in['switch_b'], 'L1_ffn_expert_w': _L1_ffn_in['expert_w'], 'L1_ffn_expert_b': _L1_ffn_in['expert_b']}

def reference(x, src, dst, node_vec1, L0_gnn_W1, L0_gnn_b1, L0_gnn_gamma, L0_gnn_beta, L0_gnn_W2, L0_gnn_b2, L0_ffn_w_gate, L0_ffn_w_up, L0_ffn_w_down, L1_gnn_alpha, L1_gnn_W, L1_gnn_b, L1_ffn_switch_w, L1_ffn_switch_b, L1_ffn_expert_w, L1_ffn_expert_b):
    import jax
    import jax.numpy as jnp

    def _L0_gnn_ref(x, size_factors, W1, b1, gamma, beta, W2, b2, edge_index):
        import jax, jax.numpy as jnp
        import numpy as np
        N = 6250
        E = 100000
        D = 512
        H = D // 64
        LN_EPS = 1e-05

        def _gcn_conv(x, W, b, src, dst, norm):
            h = x @ W
            msg = h[src] * norm[:, None]
            out = jax.ops.segment_sum(msg, dst, num_segments=N)
            return out + b
        loops = jnp.arange(N, dtype=edge_index.dtype)
        src = jnp.concatenate([edge_index[0], loops])
        dst = jnp.concatenate([edge_index[1], loops])
        deg = jax.ops.segment_sum(jnp.ones_like(src, dtype=x.dtype), dst, num_segments=N)
        dinv = jax.lax.rsqrt(deg)
        norm = dinv[src] * dinv[dst]
        h = _gcn_conv(x, W1, b1, src, dst, norm)
        mu = jnp.mean(h, axis=-1, keepdims=True)
        var = jnp.var(h, axis=-1, keepdims=True)
        h = (h - mu) * jax.lax.rsqrt(var + LN_EPS) * gamma + beta
        h = jax.nn.relu(h)
        out = jax.nn.relu(_gcn_conv(h, W2, b2, src, dst, norm))
        return out * size_factors

    def _L0_ffn_ref(x, w_gate, w_up, w_down):
        import jax, jax.numpy as jnp
        import numpy as np
        DIM = 512
        FFN_DIM = 1408
        GROUP = 128
        EPS = 1e-05

        def _quantize_weight(w, group_size):
            o, i = w.shape
            wg = w.reshape(o, i // group_size, group_size)
            scale = jnp.mean(jnp.abs(wg), axis=-1, keepdims=True) + EPS
            wq = jnp.clip(jnp.round(wg / scale), -1.0, 1.0) * scale
            return wq.reshape(o, i)

        def _bitlinear(x, w, group_size=GROUP):
            wq = w + jax.lax.stop_gradient(_quantize_weight(w, group_size) - w)
            return jnp.einsum('bsd,fd->bsf', x, wq)
        gate = _bitlinear(x, w_gate)
        up = _bitlinear(x, w_up)
        h = jax.nn.silu(gate) * up
        return _bitlinear(h, w_down)

    def _L1_gnn_ref(x, edge_index, num_nodes, alpha, W, b):
        import jax, jax.numpy as jnp
        import numpy as np
        N = 6250
        DIM = 512
        E = 18750
        src = edge_index[0]
        dst = edge_index[1]
        agg = jax.ops.segment_sum(x[src], dst, num_segments=num_nodes)
        deg = jax.ops.segment_sum(jnp.ones_like(dst, dtype=x.dtype), dst, num_segments=num_nodes)
        deg = jnp.maximum(deg, 1.0)
        agg = agg / deg[:, None]
        return x + alpha * (agg @ W.T + b)

    def _L1_ffn_ref(x, switch_w, switch_b, expert_w, expert_b):
        import jax, jax.numpy as jnp
        import numpy as np
        CAPACITY_FACTOR = 1.2
        B, S, D = x.shape
        E = switch_w.shape[0]
        N = B * S
        xf = x.reshape(N, D)
        logits = xf @ switch_w.T + switch_b
        probs = jax.nn.softmax(logits, axis=-1)
        route_probs = jnp.max(probs, axis=-1)
        routes = jnp.argmax(probs, axis=-1)
        oh = jax.nn.one_hot(routes, E, dtype=jnp.int32)
        pos = jnp.take_along_axis(jnp.cumsum(oh, axis=0), routes[:, None], axis=1)[:, 0] - 1
        capacity = int(CAPACITY_FACTOR * N / E)
        keep = pos < capacity
        buf = jnp.zeros((E, capacity, D), dtype=xf.dtype).at[routes, pos].set(xf)
        y = jnp.einsum('ecd,efd->ecf', buf, expert_w) + expert_b[:, None, :]
        gathered = y[routes, jnp.minimum(pos, capacity - 1)]
        out = jnp.where(keep[:, None], gathered, xf) * route_probs[:, None]
        return out.reshape(B, S, D)
    edge_index = jnp.stack([src, dst])
    x = x + _L0_gnn_ref(_layernorm(x, axis=-1), node_vec1, L0_gnn_W1, L0_gnn_b1, L0_gnn_gamma, L0_gnn_beta, L0_gnn_W2, L0_gnn_b2, edge_index)
    x = x + _L0_ffn_ref(_layernorm(x, axis=-1)[None], L0_ffn_w_gate, L0_ffn_w_up, L0_ffn_w_down)[0]
    x = x + _L1_gnn_ref(_layernorm(x, axis=-1), edge_index, 6250, L1_gnn_alpha, L1_gnn_W, L1_gnn_b)
    x = x + _L1_ffn_ref(_layernorm(x, axis=-1)[None], L1_ffn_switch_w, L1_ffn_switch_b, L1_ffn_expert_w, L1_ffn_expert_b)[0]
    return x

_drawn_inputs = setup_inputs


def setup_inputs(seed=0):
    import zlib

    import numpy as np

    out = dict(_drawn_inputs(seed))
    spreads = {'L0_gnn_b1': (0.0, 0.1),
     'L0_gnn_gamma': (1.0, 0.2),
     'L0_gnn_beta': (0.0, 0.296),
     'L0_gnn_b2': (0.0, 0.1),
     'L1_ffn_switch_b': (0.0, 0.34),
     'L1_ffn_expert_b': (0.0, 0.8)}
    factors = {'L1_gnn_b': 7.547}
    for name, (base, spread) in spreads.items():
        noise = np.random.default_rng([zlib.crc32(name.encode()), seed]).standard_normal(out[name].shape)
        drawn = base * np.exp(spread * noise) if base else spread * noise
        out[name] = jnp.asarray(drawn.astype(out[name].dtype))
    for name, factor in factors.items():
        out[name] = (out[name] * factor).astype(out[name].dtype)
    return out
```

```python
import concourse.bass as bass
from concourse import mybir
from contextlib import ExitStack

F32 = mybir.dt.float32
F32R = mybir.dt.float32r
BF16 = mybir.dt.bfloat16
F16 = mybir.dt.float16
I32 = mybir.dt.int32
I16 = mybir.dt.int16
U32 = mybir.dt.uint32
ALU = mybir.AluOpType
ACT = mybir.ActivationFunctionType
AX = mybir.AxisListType.X
ds = bass.ds

P = 128
N = 6250
D = 512
DK = D // P
NT = -(-N // P)
LAST = N - (NT - 1) * P
G = 7
E = 100000
EB = 7
EP = 112
C = EB * EP
U = 8
CU = C // U
CX = C + U
Q = 4
CQ = C // Q
UQ = CQ + NT + 3
FAR = NT * P
H = 8
H3 = 3 * H
F = 1408
FB = F // P
NX = 16
CAP = int(1.2 * N / NX)
ET = -(-CAP // P)
SLOTS = NX * CAP
SX = (UQ + 2) * Q
EPS = 1e-5


def lag(k):
    return {0: 1, 1: 3}.get(k, 2)


FREE = 3


class Steps:

    def __init__(self, eng, sem):
        self.eng, self.sem, self.n, self.i, self.per = eng, sem, 0, None, 0

    def body(self, i, per, first=0):
        self.i, self.per, self.start, self.k = i - first, per, self.n, 0

    def end(self, times):
        assert self.k == self.per, (self.k, self.per)
        self.n, self.i = self.start + times * self.per, None

    def step(self, ins):
        ins.then_inc(self.sem, 1)
        if self.i is None:
            self.n += 1
            self.eng.wait_ge(self.sem, self.n)
        else:
            self.k += 1
            self.eng.wait_ge(self.sem, self.i * self.per + (self.start + self.k))


def bc(ap, shape):
    return ap.to_broadcast(list(shape))



def wait_alone(eng, sem, value, fence):
    eng.wait_ge(sem, value)
    eng.sem_inc(fence, 1)


def gather_units(nc, pool, table, srcT, idx, stage, msg, landed, idx_ready, msg_ready, fence):

    def issue(u, h):
        nc.gpsimd.tensor_copy(idx[:, h, :], srcT[:, ds(u * U, U)]).then_inc(idx_ready, 1)
        pool.wait_ge(idx_ready, u + 1)
        pool.sem_inc(fence, 1)
        for k in range(U):
            nc.gpsimd.indirect_dma_start(
                stage[:, h, k, :], None, table,
                bass.IndirectOffsetOnAxis(ap=idx[:, h, k:k + 1], axis=0)).then_inc(landed[h][k], 16)

    def place(u, h, times):
        for k in range(U):
            pool.wait_ge(landed[h][k], times * 16)
        pool.sem_inc(fence, 1)
        nc.gpsimd.tensor_copy(msg[:, ds(u * U, U), :], stage[:, h, :, :]).then_inc(msg_ready, 1)
        pool.wait_ge(msg_ready, u + 1)

    issue(0, 0)
    with pool.Fori(0, CU // 2 - 1) as i:
        issue(i * 2 + 1, 1)
        place(i * 2, 0, i + 1)
        issue(i * 2 + 2, 0)
        place(i * 2 + 1, 1, i + 1)
    issue(CU - 1, 1)
    place(CU - 2, 0, CU // 2)
    place(CU - 1, 1, CU // 2)


def tile_range(eng, ranges, t, rows):
    top = {0: (0, C - 1), 1: (1, CU + 1), 2: (1, CU + 1), 3: (0, NT * (CU + 1))}
    return [eng.value_load(ranges[0:1, j, ds(t, 1)], min_val=top[j][0], max_val=top[j][1]) for j in rows]


def chunk_at(nc, first, b, k, size):
    at = nc.s_assert_within(first + b * U + k, 0, CX - size, skip_runtime_bounds_check_because=
                            "first + units * U <= CX, as block A computes the ranges")
    return ds(at, size)


def build_onehots(nc, dve, t, ranges, dstT, tiota, onehot, ready, used):
    c0, units, before = tile_range(dve, ranges, t, (0, 1, 3))
    with dve.Fori(0, units) as b:
        for h in range(2):
            dve.wait_ge(used, (before + b) * 2 + (h + 1))
            nc.vector.tensor_tensor(onehot[:, h, :, :], bc(tiota[:].unsqueeze(1), (P, U // 2, P)),
                                    bc(dstT[:, chunk_at(nc, c0, b, h * (U // 2), U // 2)].unsqueeze(2), (P, U // 2, P)),
                                    ALU.is_equal).then_inc(ready, 1)


def sum_messages(nc, pe, t, ranges, hid, msg, identb, zerob, acc, onehot, ready, used, msg_ready):
    c0, units, rows, before = tile_range(pe, ranges, t, (0, 1, 2, 3))
    nc.tensor.matmul(acc, identb[:], hid[:, ds(t, 1), :].rearrange("p a b -> p (a b)"), start=True, stop=False)
    with pe.Fori(0, units) as b:
        pe.wait_ge(msg_ready, rows + b)
        for h in range(2):
            pe.wait_ge(ready, (before + b) * 2 + (h + 1))
            for k in range(U // 2):
                last = nc.tensor.matmul(acc, onehot[:, h, k, :],
                                        msg[:, chunk_at(nc, c0, b, h * (U // 2) + k, 1), :].rearrange("p a b -> p (a b)"),
                                        start=False, stop=False)
            last.then_inc(used, 1)
    return nc.tensor.matmul(acc, zerob[:], zerob[:, 0:H3], start=False, stop=True)


GROUPS = ((0, 1, 2, 3), (4, 5, 6))


def groups(loop, part):

    def group(i, g, after, before):
        for f in range(FB):
            part.gate(i, g, f)
            if before is not None:
                ks = GROUPS[before[1]]
                if f == 0:
                    part.residual(*before)
                if f == 1:
                    part.scale_rows(*before)
                for k in {1: ks[0:2], 2: ks[2:4]}.get(f, ()):
                    part.rows(before[0], k, ks.index(k))
            if after is not None and f == 7:
                part.stats(*after)
            part.up(i, g, f)
            if after is not None:
                ks = GROUPS[after[1]]
                if 1 <= f <= len(ks):
                    part.sums(after[0], ks[f - 1], f - 1)
                for first, step in ((5, part.layer1), (9, part.turn)):
                    if f in (first, first + 1) and 2 * (f - first) < len(ks):
                        step(after[0], ks[2 * (f - first)], 2 * (f - first))
            if f > 0:
                part.down(i, g, f - 1)
            if after is not None:
                if f == 8:
                    part.scale(*after)
                for first, step in ((5, part.layer1), (9, part.turn)):
                    if f in (first, first + 1) and 2 * (f - first) + 1 < len(ks):
                        step(after[0], ks[2 * (f - first) + 1], 2 * (f - first) + 1)
        part.down(i, g, FB - 1)

    ks = GROUPS[0]
    for step in (part.sums, part.layer1):
        for j, k in enumerate(ks):
            step(0, k, j)
    part.stats(0, 0)
    part.scale(0, 0)
    for j, k in enumerate(ks):
        part.turn(0, k, j)
    group(0, 0, (0, 1), None)
    group(0, 1, (1, 0), (0, 0))
    with loop(1, G - 1) as i:
        part.enter(i)
        group(i, 0, (i, 1), (i - 1, 1))
        group(i, 1, (i + 1, 0), (i, 0))
    part.leave()
    group(G - 1, 0, (G - 1, 1), (G - 2, 1))
    group(G - 1, 1, None, (G - 1, 0))
    part.residual(G - 1, 1)
    part.scale_rows(G - 1, 1)
    for j, k in enumerate(GROUPS[1]):
        part.rows(G - 1, k, j)


def nothing(*args):
    pass


class Part:

    def __init__(self, gate=nothing, up=nothing, down=nothing, sums=nothing, layer1=nothing, stats=nothing,
                 scale=nothing, turn=nothing, residual=nothing, scale_rows=nothing, rows=nothing,
                 enter=nothing, leave=nothing):
        self.gate, self.up, self.down = gate, up, down
        self.sums, self.layer1, self.stats, self.scale, self.turn = sums, layer1, stats, scale, turn
        self.residual, self.scale_rows, self.rows = residual, scale_rows, rows
        self.enter, self.leave = enter, leave


def program(nc, x, src, dst, node_vec, W1, b1, gamma, beta, W2, b2, w_gate, w_up, w_down,
            alpha, Wg, bg, switch_w, switch_b, expert_w, expert_b, out):
    with ExitStack() as whole:
        def sb(ctx, name, shape, dt):
            return ctx.enter_context(nc.sbuf_tensor(name, shape, dt))

        def pb(ctx, name, shape, dt):
            return ctx.enter_context(nc.psum_tensor(name, shape, dt))

        stage_sems = []

        def sem(name):
            stage_sems.append(nc.alloc_semaphore(name=name))
            return stage_sems[-1]

        def next_stage():
            nc.clear_and_free_semaphores(stage_sems)
            stage_sems.clear()
            nc.all_engine_barrier()

        def dram(name, shape, dt):
            return nc.dram_tensor(name, shape, dt, kind="Internal").ap()

        whole.enter_context(nc.allow_non_contiguous_dma(reason="small vectors and tables"))

        extremes = dram("extremes", (2, C), F32)
        units_row = dram("units_row", (1, 3, UQ), I32)
        turns_row = dram("turns_row", (1, 3, NT), I32)
        lasts = dram("lasts", (1, NT), F32)
        expert_rows = dram("expert_rows", (SLOTS + P, D), F32)
        y_rows = dram("y_rows", (SLOTS, D), F32)
        z_rows = dram("z_rows", (NT * P, D), F32)
        hid1_rows = dram("hid1_rows", (NT * P, H3), BF16)
        hid2_rows = dram("hid2_rows", (NT * P, H3), BF16)
        x2_rows = dram("x2_rows", (NT * P, D), F32)
        xn2_rows = dram("xn2_rows", (NT * P, 2 * D), F16)
        wd_rows = dram("wd_rows", (FB, P, 2, D), F32)

        ident = sb(whole, "ident", [P, P], F32)
        identb = sb(whole, "identb", [P, P], BF16)
        iota = sb(whole, "iota", [P, P], F32)
        srcT = sb(whole, "srcT", [P, SX], I16)
        dstT = sb(whole, "dstT", [P, CX], I16)
        ranges = sb(whole, "ranges", [1, 4, NT], I32)
        dinv = sb(whole, "dinv", [P, NT], F32)
        invdeg = sb(whole, "invdeg", [P, NT], F32)
        hid = sb(whole, "hid", [P, NT, H3], BF16)
        zerob = sb(whole, "zerob", [P, P], BF16)

        s = {n: sem("a_" + n) for n in (
            "ext_out const cleared src_in dst_in w1_in stats xn xT_ps xT h_ps h_used "
            "xT_used dve lists_f lists_ps lists_used lo_hi ol oh hist_used hist minmax "
            "span var std degs degs_std fence span_ps spanr row_ps ranges pool hid1 stored act".split())}
        x_in = [sem(f"a_x_in{k}") for k in range(G)]
        with ExitStack() as ctx:
            src_em = sb(ctx, "src_em", [EP, EB * P], I32)
            dst_em = sb(ctx, "dst_em", [EP, EB * P], I32)
            src_f = sb(ctx, "src_f", [EP, EB * P], F32)
            dst_f = sb(ctx, "dst_f", [EP, EB * P], F32)
            hi_i = sb(ctx, "hi_i", [EP, EB * P], I32)
            hi_f = sb(ctx, "hi_f", [EP, EB, P], F32)
            lohi_i = sb(ctx, "lohi_i", [P, 3, C], I32)
            lo_f = sb(ctx, "lo_f", [P, C], F32)
            hiT_f = sb(ctx, "hiT_f", [P, C], F32)
            mm = sb(ctx, "mm", [EP, 2, EB], F32)
            pres = sb(ctx, "pres", [EP, 3, EB, NT], F32)
            cid = sb(ctx, "cid", [EP, 2, EB], F32)
            span = sb(ctx, "span", [EP, 2, NT], F32)
            spanr = sb(ctx, "spanr", [2 * NT, 1], F32)
            row = sb(ctx, "row", [1, 8, NT], F32)
            rowi = sb(ctx, "rowi", [1, 3, NT], I32)
            w1 = sb(ctx, "w1", [P, DK, H], F32)
            xt = sb(ctx, "xt", [P, G, D], F32)
            st = sb(ctx, "st", [P, G, 6], F32)
            sig = sb(ctx, "sig", [P, 8], F32)
            var = sb(ctx, "var", [P, G], F32)
            nw = sb(ctx, "nw", [P, G], F32)
            degs = sb(ctx, "degs", [P, NT], F32)
            nwd = sb(ctx, "nwd", [P, NT], F32)
            mv = sb(ctx, "mv", [P, G, 2], F32)
            rs = sb(ctx, "rs", [P, G, 2], F32)
            xT = sb(ctx, "xT", [P, 2, D], F32)
            h1 = sb(ctx, "h1", [P, NT, H], F32)
            r1 = sb(ctx, "r1", [P, 2, NT * H], F32)
            HU = 14
            ol = sb(ctx, "ol", [P, 2, HU, P], BF16)
            oh = sb(ctx, "oh", [P, 2, HU, NT], BF16)
            pT = [pb(ctx, f"pT{i}", [P, D], F32) for i in range(2)]
            pH = [pb(ctx, f"pH{i}", [P, 512], F32) for i in range(2)]
            pD = pb(ctx, "pD", [P, 512], F32)
            pL = [pb(ctx, f"pL{i}", [P, 512], F32) for i in range(2)]
            block = ctx.enter_context(nc.Block())

            @block.sync
            def _(sp):
                sp.dma_start(w1[:], W1.rearrange("(k p) h -> p k h", p=P)).then_inc(s["w1_in"], 16)
                sp.wait_ge(s["cleared"], 2)
                full = (EP - 1) * EB * P
                for lst, em, done in ((src, src_em, "src_in"), (dst, dst_em, "dst_in")):
                    sp.dma_start(em[0:EP - 1, :], lst[0:full].rearrange("(p c) -> p c", p=EP - 1)).then_inc(s[done], 16)
                    sp.dma_start(em[EP - 1:EP, 0:E - full], lst[full:E].rearrange("(p c) -> p c", p=1)).then_inc(s[done], 16)

                def load(i, k, rows=P):
                    sp.dma_start(xt[0:rows, k, :], x[ds((i * G + k) * P, rows), :]).then_inc(x_in[k], 16)

                for k in range(G):
                    load(0, k)
                with sp.Fori(1, G - 1) as i:
                    for k in range(G):
                        sp.wait_ge(s["xT_ps"], (i - 1) * G + (k + 1))
                        load(i, k)
                for k in range(G):
                    sp.wait_ge(s["xT_ps"], (G - 2) * G + k + 1)
                    load(G - 1, k, P if k < G - 1 else LAST)
                sp.wait_ge(s["row_ps"], 1)
                sp.dma_start(extremes.rearrange("m (p b) -> p m b", p=EP), mm[:]).then_inc(s["ext_out"], 16)
                sp.wait_ge(s["ranges"], 1)
                sp.dma_start(lasts, row[0:1, 0, :]).then_inc(s["ext_out"], 16)
                sp.wait_ge(s["ext_out"], 32)
                sp.wait_ge(s["hid1"], 1)
                sp.dma_start(hid1_rows.rearrange("(t p) f -> p t f", p=P), hid[:]).then_inc(s["stored"], 16)
                sp.wait_ge(s["stored"], 16)

            @block.gpsimd
            def _(pool):
                own = Steps(pool, s["pool"])
                own.step(nc.gpsimd.memset(ident[:], 0.0))
                own.step(nc.gpsimd.affine_select(out=ident[:], in_=ident[:], compare_op=ALU.not_equal, fill=1.0,
                                                 base=0, pattern=[[-1, P]], channel_multiplier=1))
                nc.gpsimd.tensor_copy(identb[:], ident[:])
                nc.gpsimd.memset(zerob[:], 0.0)
                nc.gpsimd.iota(iota[:], [[1, P]], base=0, channel_multiplier=0,
                               allow_small_or_imprecise_dtypes=True)
                nc.gpsimd.iota(cid[:, 0, :], [[1, EB]], base=1, channel_multiplier=EB,
                               allow_small_or_imprecise_dtypes=True)
                nc.gpsimd.iota(cid[:, 1, :], [[-1, EB]], base=1000, channel_multiplier=-EB,
                               allow_small_or_imprecise_dtypes=True)
                nc.gpsimd.memset(srcT[:, C:SX], 0)
                nc.gpsimd.memset(dstT[:, C:CX], FAR).then_inc(s["const"], 1)

            @block.vector
            def _(dve):
                own = Steps(dve, s["dve"])
                nc.vector.memset(src_em[:], 0).then_inc(s["cleared"], 1)
                nc.vector.memset(dst_em[:], FAR).then_inc(s["cleared"], 1)
                dve.wait_ge(s["dst_in"], 32)
                nc.vector.tensor_copy(dst_f[:], dst_em[:]).then_inc(s["lists_f"], 1)
                dve.wait_ge(s["src_in"], 32)
                nc.vector.tensor_copy(src_f[:], src_em[:]).then_inc(s["lists_f"], 1)
                own.step(nc.vector.tensor_single_scalar(hi_i[:], dst_em[:], 7, ALU.arith_shift_right))
                own.step(nc.vector.tensor_copy(hi_f[:].rearrange("p a b -> p (a b)"), hi_i[:]))
                own.step(nc.vector.tensor_reduce(mm[:, 0, :], hi_f[:], AX, ALU.min))
                own.step(nc.vector.tensor_reduce(mm[:, 1, :], hi_f[:], AX, ALU.max))
                dve.wait_ge(s["const"], 1)
                full = (EP, EB, NT)
                tiles = bc(iota[0:EP, 0:NT].unsqueeze(1), full)
                own.step(nc.vector.tensor_tensor(pres[:, 0], bc(mm[:, 0, :].unsqueeze(2), full), tiles, ALU.is_le))
                own.step(nc.vector.tensor_tensor(pres[:, 1], bc(mm[:, 1, :].unsqueeze(2), full), tiles, ALU.is_ge))
                own.step(nc.vector.tensor_tensor(pres[:, 2], pres[:, 0], pres[:, 1], ALU.mult))
                for j in range(2):
                    own.step(nc.vector.tensor_tensor(pres[:, 0], pres[:, 2], bc(cid[:, j, :].unsqueeze(2), full), ALU.mult))
                    own.step(nc.vector.tensor_reduce(span[:, j, :], pres[:, 0].rearrange("p e t -> p t e"), AX, ALU.max))
                nc.vector.tensor_copy(pres[:, 1, 0, 0:1], pres[:, 0, 0, 0:1]).then_inc(s["span"], 1)
                for j in range(2 * EB):
                    lst, b = (dstT[:, 0:C], j) if j < EB else (srcT[:, 0:C], j - EB)
                    dve.wait_ge(s["lists_ps"], j + 1)
                    nc.vector.tensor_copy(lst.rearrange("q (p b) -> q b p", b=EB)[:, b, :],
                                          pL[j % 2][:, 0:EP]).then_inc(s["lists_used"], 1)
                dve.wait_ge(s["lists_used"], 2 * EB)
                own.step(nc.vector.tensor_copy(lohi_i[:, 0, :], dstT[:, 0:C]))
                own.step(nc.vector.tensor_single_scalar(lohi_i[:, 1, :], lohi_i[:, 0, :], P - 1, ALU.bitwise_and))
                own.step(nc.vector.tensor_single_scalar(lohi_i[:, 2, :], lohi_i[:, 0, :], 7, ALU.arith_shift_right))
                own.step(nc.vector.tensor_copy(lo_f[:], lohi_i[:, 1, :]))
                nc.vector.tensor_copy(hiT_f[:], lohi_i[:, 2, :]).then_inc(s["lo_hi"], 1)
                dve.wait_ge(s["span_ps"], 1)
                nc.vector.tensor_reduce(spanr[:], pL[0][0:2 * NT, 0:EP], AX, ALU.max).then_inc(s["spanr"], 1)
                dve.wait_ge(s["row_ps"], 1)
                r = [row[0:1, j, :] for j in range(8)]
                own.step(nc.vector.tensor_copy(row[0:1, 0:2, :].rearrange("p a b -> p (a b)"), pL[1][0:1, 0:2 * NT]))
                own.step(nc.vector.tensor_scalar(r[2], r[1], -1.0, 1000.0, ALU.mult, ALU.add))
                own.step(nc.vector.tensor_scalar_min(r[2], r[2], float(C - 1)))
                own.step(nc.vector.tensor_sub(r[3], r[0], r[2]))
                own.step(nc.vector.tensor_scalar(r[3], r[3], 1.0, float(U - 1), ALU.max, ALU.add))
                own.step(nc.vector.tensor_scalar_add(r[4], r[2], float(2 * U - 1)))
                own.step(nc.vector.tensor_copy(ranges[0:1, 0, :], r[2]))
                own.step(nc.vector.tensor_copy(rowi[0:1, 0:2, :], row[0:1, 3:5, :]))
                own.step(nc.vector.tensor_single_scalar(ranges[0:1, 1:3, :], rowi[0:1, 0:2, :], 3, ALU.arith_shift_right))
                own.step(nc.vector.tensor_copy(r[5], ranges[0:1, 1, :]))
                own.step(nc.vector.tensor_copy(r[7], r[5]))
                a, b = 5, 6
                d = 1
                while d < NT:
                    own.step(nc.vector.tensor_copy(r[b], r[a]))
                    own.step(nc.vector.tensor_add(r[b][:, d:NT], r[a][:, d:NT], r[a][:, 0:NT - d]))
                    a, b, d = b, a, 2 * d
                own.step(nc.vector.tensor_sub(r[b], r[a], r[7]))
                own.step(nc.vector.tensor_copy(ranges[0:1, 3, :], r[b]))
                dve.sem_inc(s["ranges"], 1)
                with dve.Fori(0, G) as i:
                    own.body(i, 3 + NEWTON)
                    dve.wait_ge(s["xn"], i * G + G)
                    for k in range(G):
                        dve.wait_ge(x_in[k], (i + 1) * 16)
                        last = nc.vector.bn_stats(st[:, k, :], xt[:, k, :])
                    own.step(last)
                    dve.sem_inc(s["fence"], 1)
                    for k in range(G):
                        last = nc.vector.bn_aggr(mv[:, k, :], st[:, k, :])
                    own.step(last)
                    own.step(nc.vector.tensor_scalar_add(var[:], mv[:, :, 1], EPS))
                    nc.vector.tensor_copy(sig[:, 0:1], var[:, 0:1]).then_inc(s["var"], 1)
                    dve.wait_ge(s["std"], i + 1)
                    newton(nc, own, rs[:, :, 0], var[:], nw[:])
                    nc.vector.scalar_tensor_tensor(rs[:, :, 1], mv[:, :, 0], -1.0, rs[:, :, 0],
                                                   ALU.mult, ALU.mult).then_inc(s["stats"], 1)
                own.end(G)
                with dve.Fori(0, C // (2 * HU)) as i:
                    for h in range(2):
                        dve.wait_ge(s["hist_used"], i * 2 + (h + 1))
                        nc.vector.tensor_tensor(
                            ol[:, h, :, :], bc(iota[:].unsqueeze(1), (P, HU, P)),
                            bc(lo_f[:, ds((i * 2 + h) * HU, HU)].unsqueeze(2), (P, HU, P)),
                            ALU.is_equal).then_inc(s["ol"], 1)
                        nc.vector.tensor_tensor(
                            oh[:, h, :, :], bc(iota[:, 0:NT].unsqueeze(1), (P, HU, NT)),
                            bc(hiT_f[:, ds((i * 2 + h) * HU, HU)].unsqueeze(2), (P, HU, NT)),
                            ALU.is_equal).then_inc(s["oh"], 1)
                dve.wait_ge(s["hist"], 1)
                own.step(nc.vector.tensor_scalar_add(degs[:], pD[:, 0:NT], 1.0))
                nc.vector.tensor_copy(sig[:, 0:1], degs[:, 0:1]).then_inc(s["degs"], 1)
                dve.wait_ge(s["degs_std"], 1)
                newton(nc, own, dinv[:], degs[:], nwd[:])
                own.step(nc.vector.tensor_scalar_max(invdeg[:], pD[:, 0:NT], 1.0))
                own.step(nc.vector.reciprocal(invdeg[:], invdeg[:]))
                dve.wait_ge(s["h_used"], NT)
                own.step(nc.vector.tensor_tensor(h1[:], h1[:], bc(dinv[:].unsqueeze(2), (P, NT, H)), ALU.mult))
                split3(nc, own, hid, h1, r1)
                nc.vector.tensor_copy(sig[:, 0:1], r1[:, 0, 0:1]).then_inc(s["hid1"], 1)

            @block.scalar
            def _(act):
                act.sem_inc(s["xn"], G)
                with act.Fori(0, G) as i:
                    act.wait_ge(s["var"], i + 1)
                    nc.scalar.activation(rs[:, :, 0], var[:], ACT.Sqrt).then_inc(s["std"], 1)
                    act.wait_ge(s["stats"], i + 1)
                    for k in range(G):
                        T = i * G + k
                        nc.scalar.activation(xt[:, k, :], xt[:, k, :], ACT.Identity,
                                             bias=rs[:, k, 1:2], scale=rs[:, k, 0:1]).then_inc(s["xn"], 1)
                        act.wait_ge(s["xT_ps"], T + 1)
                        nc.scalar.copy(xT[:, k % 2, :], pT[k % 2][:]).then_inc(s["xT"], 1)
                        act.wait_ge(s["h_ps"], T + 1)
                        nc.scalar.copy(h1[:, ds(T, 1), :].rearrange("p a b -> p (a b)"), pH[k % 2][:, 0:H]).then_inc(s["h_used"], 1)
                act.wait_ge(s["degs"], 1)
                nc.scalar.activation(dinv[:], degs[:], ACT.Sqrt).then_inc(s["degs_std"], 1)

            @block.tensor
            def _(pe):
                pe.wait_ge(s["const"], 1)
                pe.sem_inc(s["hist_used"], 1)
                for j in range(2 * EB):
                    lst, b = (dst_f, j) if j < EB else (src_f, j - EB)
                    pe.wait_ge(s["lists_f"], j // EB + 1)
                    if j >= 2:
                        pe.wait_ge(s["lists_used"], j - 1)
                    nc.tensor.transpose(pL[j % 2][:, 0:EP], lst[:, b * P:(b + 1) * P], ident[0:EP, 0:EP]).then_inc(s["lists_ps"], 1)
                pe.wait_ge(s["span"], 1)
                pe.wait_ge(s["lists_used"], 2 * EB)
                nc.tensor.transpose(pL[0][0:2 * NT, 0:EP], span[:].rearrange("p a b -> p (a b)"),
                                    ident[0:EP, 0:EP]).then_inc(s["span_ps"], 1)
                pe.wait_ge(s["spanr"], 1)
                nc.tensor.transpose(pL[1][0:1, 0:2 * NT], spanr[:], ident[0:2 * NT, 0:2 * NT]).then_inc(s["row_ps"], 1)
                pe.wait_ge(s["w1_in"], 16)
                with pe.Fori(0, G) as i:
                    for k in range(G):
                        T = i * G + k
                        pe.wait_ge(s["xn"], T + (G + 1))
                        for c in range(DK):
                            last = nc.tensor.transpose(pT[k % 2][:, c * P:(c + 1) * P], xt[:, k, c * P:(c + 1) * P], ident[:])
                        last.then_inc(s["xT_ps"], 1)
                        pe.wait_ge(s["xT"], T + 1)
                        for c in range(DK):
                            last = nc.tensor.matmul(pH[k % 2][:, 0:H], xT[:, k % 2, c * P:(c + 1) * P], w1[:, c, :],
                                                    start=(c == 0), stop=(c == DK - 1))
                        last.then_inc(s["h_ps"], 1)
                nc.tensor.matmul(pD[:, 0:NT], zerob[:], zerob[:, 0:NT], start=True, stop=False)
                with pe.Fori(0, C // (2 * HU)) as i:
                    for h in range(2):
                        pe.wait_ge(s["ol"], i * 2 + (h + 1))
                        pe.wait_ge(s["oh"], i * 2 + (h + 1))
                        for c in range(HU):
                            last = nc.tensor.matmul(pD[:, 0:NT], ol[:, h, c, :], oh[:, h, c, :], start=False, stop=False)
                        last.then_inc(s["hist_used"], 1)
                nc.tensor.matmul(pD[:, 0:NT], zerob[:], zerob[:, 0:NT], start=False, stop=True).then_inc(s["hist"], 1)


        ffn = whole.enter_context(ExitStack())
        wgu = [sb(ffn, f"wgu_{n}", [P, 2 * FB, DK, P], F32R) for n in ("hi", "lo")]
        msg = sb(ffn, "msg", [P, CX, H3], BF16)
        onehot = sb(ffn, "onehot", [P, 2, U // 2, P], BF16)
        tiota = sb(ffn, "tiota", [P, P], F32)
        idx = sb(ffn, "idx", [P, 2, U], I32)
        stage = sb(ffn, "stage", [P, 2, U, H3], BF16)
        next_stage()
        s = {n: sem("b_" + n) for n in (
            "tables tables_out zero zeroed ext_in fence fence_sp fence_pe fence_dve small_in wq ps hi lo_done dve idx msg onehot used agg agg_used var std hid2 stored "
            "d_wq d_ps d_hi d_lo d_out".split())}
        w_in = [sem(f"b_w_in{j}") for j in range(2)]
        wd_in = sem("b_wd_in")
        landed = [[sem(f"b_landed{h}_{k}") for k in range(U)] for h in range(2)]
        with ExitStack() as ctx:
            wraw = sb(ctx, "wraw", [P, 2, DK, P], F32)
            wq = sb(ctx, "wq", [P, 2, 2, DK, P], F32)
            wdraw = sb(ctx, "wdraw", [P, FB, P], F32)
            wdq = sb(ctx, "wdq", [P, 2, FB, P], F32)
            wdT = sb(ctx, "wdT", [P, 2, FB, P], F32R)
            sc = sb(ctx, "sc", [P, 3, FB], F32)
            vec = sb(ctx, "vec", [P, 3, H], F32)
            agg = sb(ctx, "agg", [P, NT, H], F32)
            sq = sb(ctx, "sq", [P, NT, H], F32)
            mean = sb(ctx, "mean", [P, NT], F32)
            var = sb(ctx, "bvar", [P, NT], F32)
            rstd = sb(ctx, "rstd", [P, NT], F32)
            nw = sb(ctx, "bnw", [P, NT], F32)
            rest = sb(ctx, "rest", [P, 2, NT * H], F32)
            sig = sb(ctx, "bsig", [P, 1], F32)
            zeros = sb(ctx, "zeros", [P, D], F32)
            units = sb(ctx, "units", [1, 3, UQ], I32)
            turns = sb(ctx, "turns", [1, 3, NT], I32)
            ext = sb(ctx, "ext", [1, 2, C], F32)
            ur = sb(ctx, "ur", [1, 5, UQ], F32)
            tr = sb(ctx, "tr", [1, 6, NT], F32)
            ti = sb(ctx, "ti", [1, 2, NT], I32)
            pW = [pb(ctx, f"pW{i}", [P, DK, P], F32) for i in range(2)]
            pA = pb(ctx, "pA", [P, 512], F32)
            acc = pA[:, 0:H3]
            block = ctx.enter_context(nc.Block())

            @block.sync
            def _(sp):
                sp.wait_ge(s["zero"], 1)
                with sp.Fori(0, (SLOTS + P) // P) as i:
                    sp.dma_start(expert_rows[ds(i * P, P), :], zeros[:]).then_inc(s["zeroed"], 16)
                rest_rows = (SLOTS + P) % P
                sp.dma_start(expert_rows[SLOTS + P - rest_rows:SLOTS + P, :], zeros[0:rest_rows, :]).then_inc(s["zeroed"], 16)
                sp.dma_start(ext[0:1, :, :], extremes.rearrange("(a m) c -> a m c", a=1)).then_inc(s["ext_in"], 16)
                sp.dma_start(tr[0:1, 0, :], lasts).then_inc(s["ext_in"], 16)
                for j, v in enumerate((b1, gamma, beta)):
                    sp.dma_start(vec[:, j, :], v.partition_broadcast(P)).then_inc(s["small_in"], 16)
                with sp.Fori(0, FB) as i:
                    for j, w in enumerate((w_gate, w_up)):
                        wait_alone(sp, s["wq"], i * 2 + (j + 1), s["fence_sp"])
                        sp.dma_start(wraw[:, j, :, :].rearrange("p a b -> p (a b)"), w[ds(i * P, P), :]).then_inc(w_in[j], 16)
                with sp.Fori(0, DK) as i:
                    wait_alone(sp, s["d_wq"], i + 1, s["fence_sp"])
                    sp.dma_start(wdraw[:].rearrange("p a b -> p (a b)"), w_down[ds(i * P, P), :]).then_inc(wd_in, 16)
                    wait_alone(sp, s["d_lo"], (i + 1) * 3 + 1, s["fence_sp"])
                    for j in range(2):
                        sp.dma_start(wd_rows[:, :, j, ds(i * P, P)].rearrange("b f o -> f b o"),
                                     wdT[:, j, :, :].bitcast(F32)).then_inc(s["d_out"], 16)
                    wait_alone(sp, s["d_out"], (i + 1) * 32, s["fence_sp"])
                sp.wait_ge(s["tables"], 1)
                sp.dma_start(units_row, units[:]).then_inc(s["tables_out"], 16)
                sp.dma_start(turns_row, turns[:]).then_inc(s["tables_out"], 16)
                sp.wait_ge(s["tables_out"], 32)
                sp.wait_ge(s["zeroed"], ((SLOTS + P) // P + 1) * 16)
                sp.wait_ge(s["hid2"], 1)
                sp.dma_start(hid2_rows.rearrange("(t p) f -> p t f", p=P), hid[:]).then_inc(s["stored"], 16)
                sp.wait_ge(s["stored"], 16)

            @block.gpsimd
            def _(pool):
                nc.gpsimd.memset(msg[:, C:CX, :], 0.0)
                gather_units(nc, pool, hid1_rows, srcT, idx, stage, msg, landed, s["idx"], s["msg"], s["fence"])
                pool.sem_inc(s["msg"], 1)

            @block.vector
            def _(dve):
                own = Steps(dve, s["dve"])
                own.step(nc.vector.memset(zeros[:], 0.0))
                dve.sem_inc(s["zero"], 1)
                dve.sem_inc(s["wq"], 2)
                dve.sem_inc(s["d_wq"], 1)

                def quantize(w, q, n):
                    full = (P, n, P)
                    scale, over, under = (sc[:, j, 0:n] for j in range(3))
                    own.step(nc.vector.tensor_reduce(scale, w, AX, ALU.add, apply_absolute_value=True))
                    own.step(nc.vector.tensor_scalar(scale, scale, 1.0 / P, EPS, ALU.mult, ALU.add))
                    own.step(nc.vector.tensor_scalar_mul(over, scale, 0.5))
                    own.step(nc.vector.tensor_scalar_mul(under, scale, -0.5))
                    own.step(nc.vector.tensor_tensor(q[0], w, bc(over.unsqueeze(2), full), ALU.is_gt))
                    own.step(nc.vector.tensor_tensor(q[1], w, bc(under.unsqueeze(2), full), ALU.is_lt))
                    own.step(nc.vector.tensor_tensor(q[0], q[0], q[1], ALU.subtract))
                    return nc.vector.tensor_tensor(q[0], q[0], bc(scale.unsqueeze(2), full), ALU.mult)

                with dve.Fori(0, FB) as i:
                    own.body(i, 14)
                    for j in range(2):
                        dve.wait_ge(w_in[j], (i + 1) * 16)
                        quantize(wraw[:, j], [wq[:, j, 0], wq[:, j, 1]], DK).then_inc(s["wq"], 1)
                        dve.wait_ge(s["wq"], i * 2 + (j + 3))
                    for j in range(2):
                        dve.wait_ge(s["hi"], i * 2 + (j + 1))
                        at = wgu[1][:, ds(i + j * FB, 1)].rearrange("p a b c -> p (a b) c")
                        hi = wgu[0][:, ds(i + j * FB, 1)].rearrange("p a b c -> p (a b) c").bitcast(F32)
                        nc.vector.tensor_tensor(at, pW[j][:], hi, ALU.subtract).then_inc(s["lo_done"], 1)
                own.end(FB)
                with dve.Fori(0, DK) as i:
                    own.body(i, 7)
                    dve.wait_ge(wd_in, (i + 1) * 16)
                    quantize(wdraw[:], [wdq[:, 0], wdq[:, 1]], FB).then_inc(s["d_wq"], 1)
                    dve.wait_ge(s["d_wq"], i + 2)
                    for m in range(3):
                        g = slice(4 * m, min(4 * m + 4, FB))
                        dve.wait_ge(s["d_hi"], i * 3 + (m + 1))
                        nc.vector.tensor_tensor(wdT[:, 1, g, :], pW[m % 2][:, 0:g.stop - g.start, :],
                                                wdT[:, 0, g, :].bitcast(F32), ALU.subtract).then_inc(s["d_lo"], 1)
                own.end(DK)
                dve.wait_ge(s["ext_in"], 32)
                u = [ur[0:1, j, :] for j in range(5)]
                own.step(nc.vector.memset(ur[:], float(NT - 1)))
                own.step(nc.vector.tensor_reduce(u[0][:, 0:CQ], ext[0:1, 0, :].rearrange("a (u q) -> a u q", q=Q), AX, ALU.min))
                own.step(nc.vector.tensor_reduce(u[1][:, 0:CQ], ext[0:1, 1, :].rearrange("a (u q) -> a u q", q=Q), AX, ALU.max))
                own.step(nc.vector.tensor_scalar_min(ur[0:1, 0:2, :], ur[0:1, 0:2, :], float(NT - 1)))
                own.step(nc.vector.tensor_sub(u[1], u[1], u[0]))
                own.step(nc.vector.tensor_scalar_add(u[1], u[1], 1.0))
                own.step(nc.vector.tensor_copy(units[0:1, 0:2, :], ur[0:1, 0:2, :]))
                own.step(nc.vector.tensor_copy(u[2], u[1]))
                a, b = scan(nc, own, u, 2, 3, UQ, ALU.add)
                own.step(nc.vector.tensor_sub(u[b], u[a], u[1]))
                own.step(nc.vector.tensor_copy(units[0:1, 2, :], u[b]))
                r = [tr[0:1, j, :] for j in range(6)]
                own.step(nc.vector.tensor_scalar(r[0], r[0], float(Q - 1), float(Q), ALU.add, ALU.max))
                own.step(nc.vector.tensor_copy(ti[0:1, 0, :], r[0]))
                own.step(nc.vector.tensor_single_scalar(ti[0:1, 1, :], ti[0:1, 0, :], Q.bit_length() - 1, ALU.arith_shift_right))
                own.step(nc.vector.tensor_copy(r[0], ti[0:1, 1, :]))
                own.step(nc.vector.tensor_sub(r[1], r[0], iota[0:1, 0:NT]))
                a, b = scan(nc, own, r, 1, 2, NT, ALU.max)
                own.step(nc.vector.tensor_add(r[3], r[a], iota[0:1, 0:NT]))
                own.step(nc.vector.tensor_copy(ti[0:1, 0, :], r[3]))
                own.step(nc.vector.tensor_scalar_add(r[4], r[3], float(Q - 1)))
                own.step(nc.vector.tensor_copy(ti[0:1, 1, :], r[4]))
                own.step(nc.vector.tensor_single_scalar(turns[0:1, 2, :], ti[0:1, 1, :], Q.bit_length() - 1, ALU.arith_shift_right))
                own.step(nc.vector.tensor_copy(turns[0:1, 2, 0:1], turns[0:1, 2, NT - 1:NT]))
                own.step(nc.vector.tensor_copy(r[5], turns[0:1, 2, :]))
                own.step(nc.vector.tensor_scalar_mul(r[3][:, NT - 1:NT], r[5][:, NT - 1:NT], float(Q)))
                own.step(nc.vector.memset(r[4], 0.0))
                own.step(nc.vector.tensor_copy(r[4][:, 1:NT], r[3][:, 0:NT - 1]))
                own.step(nc.vector.tensor_sub(r[5], r[3], r[4]))
                own.step(nc.vector.tensor_copy(turns[0:1, 0:2, :], tr[0:1, 4:6, :]))
                dve.sem_inc(s["tables"], 1)
                own.step(nc.vector.tensor_copy(tiota[:], iota[:]))
                with dve.Fori(0, NT) as t:
                    own.body(t, 1)
                    build_onehots(nc, dve, t, ranges, dstT, tiota, onehot, s["onehot"], s["used"])
                    dve.wait_ge(s["agg"], t + 1)
                    own.step(nc.vector.tensor_scalar_add(tiota[:], tiota[:], float(P)))
                    nc.vector.tensor_reduce(agg[:, ds(t, 1), :].rearrange("p a b -> p (a b)"),
                                            acc.rearrange("p (a f) -> p f a", f=H), AX, ALU.add).then_inc(s["agg_used"], 1)
                own.end(NT)
                dve.wait_ge(s["agg_used"], NT + 1)
                dve.wait_ge(s["small_in"], 48)
                full = (P, NT, H)
                b1_, gamma_, beta_ = (bc(vec[:, j, :].unsqueeze(1), full) for j in range(3))

                def tt(o, a, b, op):
                    own.step(nc.vector.tensor_tensor(o, a, b, op))

                per_node = lambda v: bc(v[:].unsqueeze(2), full)
                tt(agg[:], agg[:], per_node(dinv), ALU.mult)
                tt(agg[:], agg[:], b1_, ALU.add)
                own.step(nc.vector.tensor_reduce(mean[:], agg[:], AX, ALU.add))
                own.step(nc.vector.tensor_scalar_mul(mean[:], mean[:], 1.0 / H))
                tt(agg[:], agg[:], per_node(mean), ALU.subtract)
                tt(sq[:], agg[:], agg[:], ALU.mult)
                own.step(nc.vector.tensor_reduce(var[:], sq[:], AX, ALU.add))
                own.step(nc.vector.tensor_scalar(var[:], var[:], 1.0 / H, EPS, ALU.mult, ALU.add))
                nc.vector.memset(sig[:], 0.0).then_inc(s["var"], 1)
                dve.wait_ge(s["std"], 1)
                newton(nc, own, rstd[:], var[:], nw[:])
                tt(agg[:], agg[:], per_node(rstd), ALU.mult)
                tt(agg[:], agg[:], gamma_, ALU.mult)
                tt(agg[:], agg[:], beta_, ALU.add)
                own.step(nc.vector.tensor_scalar_max(agg[:], agg[:], 0.0))
                tt(agg[:], agg[:], per_node(dinv), ALU.mult)
                split3(nc, own, hid, agg, rest)
                nc.vector.memset(sig[:], 0.0).then_inc(s["hid2"], 1)

            @block.scalar
            def _(act):
                with act.Fori(0, FB) as i:
                    for j in range(2):
                        act.wait_ge(s["ps"], i * 2 + (j + 1))
                        nc.scalar.copy(wgu[0][:, ds(i + j * FB, 1)].rearrange("p a b c -> p (a b) c"), pW[j][:]).then_inc(s["hi"], 1)
                with act.Fori(0, DK) as i:
                    act.wait_ge(s["d_wq"], i + 2)
                    for m in range(3):
                        g = slice(4 * m, min(4 * m + 4, FB))
                        act.wait_ge(s["d_ps"], i * 3 + (m + 1))
                        nc.scalar.copy(wdT[:, 0, g, :], pW[m % 2][:, 0:g.stop - g.start, :]).then_inc(s["d_hi"], 1)
                act.wait_ge(s["var"], 1)
                nc.scalar.activation(rstd[:], var[:], ACT.Sqrt).then_inc(s["std"], 1)

            @block.tensor
            def _(pe):
                pe.sem_inc(s["used"], 2)
                pe.sem_inc(s["agg_used"], 1)
                pe.sem_inc(s["lo_done"], 2)
                with pe.Fori(0, FB) as i:
                    for j in range(2):
                        pe.wait_ge(s["wq"], i * 2 + (j + 3))
                        pe.wait_ge(s["lo_done"], i * 2 + (j + 1))
                        for k in range(DK):
                            last = nc.tensor.transpose(pW[j][:, k, :], wq[:, j, 0, k, :], ident[:])
                        last.then_inc(s["ps"], 1)
                pe.wait_ge(s["lo_done"], 2 * FB + 2)
                pe.sem_inc(s["d_lo"], 1)
                with pe.Fori(0, DK) as i:
                    pe.wait_ge(s["d_wq"], i + 2)
                    for m in range(3):
                        pe.wait_ge(s["d_lo"], i * 3 + (1 if m < 2 else 2))
                        for k in range(4 * m, min(4 * m + 4, FB)):
                            last = nc.tensor.transpose(pW[m % 2][:, k - 4 * m, :], wdq[:, 0, k, :], ident[:])
                        last.then_inc(s["d_ps"], 1)
                with pe.Fori(0, NT) as t:
                    pe.wait_ge(s["agg_used"], t + 1)
                    sum_messages(nc, pe, t, ranges, hid, msg, identb, zerob, acc, onehot,
                                 s["onehot"], s["used"], s["msg"]).then_inc(s["agg"], 1)


        next_stage()
        s = {n: sem("c_" + n) for n in (
            "small_in nv_clear idx msg fence fence_sp fence_pe fence_dve onehot used agg agg_used aggd aggT_ps aggT conv relu "
            "x1 var std rs xn xT_ps xT_hi xT_lo gate_ps up_ps silu hmul h_hi h_lo down x2 var2 std2 rs2 "
            "xn2 row_hi row_lo row_stored dve".split())}
        landed = [[sem(f"c_landed{h}_{k}") for k in range(U)] for h in range(2)]
        x_in = [sem(f"c_x_in{k}") for k in range(G)]
        x2_out = [sem(f"c_x2_out{k}") for k in range(G)]
        row_out = sem("c_row_out")
        wd_in = [sem(f"c_wd_in{j}") for j in range(2)]
        with ExitStack() as ctx:
            xr = sb(ctx, "xr", [P, G, D], F32)
            xn = sb(ctx, "xn", [P, 2, D], F32)
            xT = [sb(ctx, f"xT{g}", [P, 2, DK, len(ks) * P], F32R) for g, ks in enumerate(GROUPS)]
            hT = sb(ctx, "hT", [P, 2, 2, 4 * P], F32R)
            sil = sb(ctx, "sil", [P, 4 * P], F32)
            wd = sb(ctx, "wd", [P, 2, 2, D], F32R)
            w2b = sb(ctx, "w2b", [H + 1, D], F32)
            nv = sb(ctx, "nv", [P, NT], F32)
            pair = sb(ctx, "pair", [P, 2, D], F16)
            sums8 = sb(ctx, "sums8", [P, H], F32)
            aggd = sb(ctx, "aggd", [P, 4, H + 1], F32)
            aggT = sb(ctx, "aggT", [H + 1, P], F32)
            st = sb(ctx, "cst", [P, 4, 6], F32)
            mv = sb(ctx, "cmv", [P, 2, 4, 2], F32)
            var = sb(ctx, "cvar", [P, 2, 4], F32)
            rs = sb(ctx, "crs", [P, 2, 4, 2], F32)
            nw = sb(ctx, "cnw", [P, 4], F32)
            sig = sb(ctx, "csig", [P, 1], F32)
            acc4 = [pb(ctx, f"acc{j}", [P, D], F32) for j in range(4)]
            pG = pb(ctx, "pG", [P, 4 * P], F32)
            pU = pb(ctx, "pU", [P, 4 * P], F32)
            pA = pb(ctx, "pAc", [P, 512], F32)
            pB = pb(ctx, "pB", [P, DK, P], F32)
            pB_flat = pB[:].rearrange("p a b -> p (a b)")
            acc = pA[:, 0:H3]
            pAT = pB[0:H + 1, 0, :]
            block = ctx.enter_context(nc.Block())

            def steps_before(i, g, f):
                return i * (2 * FB) + (g * FB + f)

            @block.gpsimd
            def _(pool):
                gather_units(nc, pool, hid2_rows, srcT, idx, stage, msg, landed, s["idx"], s["msg"], s["fence"])
                pool.sem_inc(s["msg"], 1)

            @block.sync
            def _(sp):
                def load_x(i, k):
                    last = isinstance(i, int) and i * G + k == NT - 1
                    rows = LAST if last else P
                    sp.dma_start(xr[0:rows, k, :], x[ds((i * G + k) * P, rows), :]).then_inc(x_in[k], 16)

                sp.dma_start(w2b[0:H, :], W2).then_inc(s["small_in"], 16)
                sp.dma_start(w2b[H:H + 1, :], b2.rearrange("(a n) -> a n", a=1)).then_inc(s["small_in"], 16)
                full = (NT - 1) * P
                sp.wait_ge(s["nv_clear"], 1)
                sp.dma_start(nv[:, 0:NT - 1], node_vec[0:full, :].rearrange("(t p) a -> p (t a)", p=P)).then_inc(s["small_in"], 16)
                sp.dma_start(nv[0:LAST, NT - 1:NT], node_vec[full:N, :]).then_inc(s["small_in"], 16)
                for k in range(G):
                    load_x(0, k)

                def gate(i, g, f):
                    step, slot = steps_before(i, g, f), (g * FB + f) % 2
                    wait_alone(sp, s["down"], step + 1, s["fence_sp"])
                    sp.dma_start(wd[:, slot, :, :].bitcast(F32), wd_rows[f]).then_inc(wd_in[slot], 16)

                def rows(i, k, j):
                    T = i * G + k
                    wait_alone(sp, s["x2"], T + 2, s["fence_sp"])
                    sp.dma_start(x2_rows[ds(T * P, P), :], xr[:, k, :]).then_inc(x2_out[k], 16)
                    wait_alone(sp, s["row_lo"], T + 2, s["fence_sp"])
                    sp.dma_start(xn2_rows[ds(T * P, P), :], pair[:].rearrange("p a b -> p (a b)")).then_inc(row_out, 16)
                    wait_alone(sp, row_out, T * 16 + 16, s["fence_sp"])
                    sp.sem_inc(s["row_stored"], 1)
                    if not isinstance(i, int) or i < G - 1:
                        wait_alone(sp, x2_out[k], (i + 1) * 16, s["fence_sp"])
                        load_x(i + 1, k)

                groups(sp.Fori, Part(gate=gate, rows=rows))
                for k in range(G):
                    sp.wait_ge(x2_out[k], G * 16)

            @block.tensor
            def _(pe):
                pe.sem_inc(s["used"], 2)
                for n in ("agg_used", "silu", "hmul", "xT_lo"):
                    pe.sem_inc(s[n], 1)
                pe.sem_inc(s["down"], 2)
                pe.wait_ge(s["small_in"], 64)

                def sums(i, k, j):
                    T = i * G + k
                    wait_alone(pe, s["agg_used"], T + 1, s["fence_pe"])
                    sum_messages(nc, pe, T, ranges, hid, msg, identb, zerob, acc, onehot,
                                 s["onehot"], s["used"], s["msg"]).then_inc(s["agg"], 1)

                def layer1(i, k, j):
                    T = i * G + k
                    wait_alone(pe, s["relu"] if j else s["xT_lo"], T if j else T + 1, s["fence_pe"])
                    wait_alone(pe, s["aggd"], T + 1, s["fence_pe"])
                    nc.tensor.transpose(pAT, aggd[:, j, :], ident[:]).then_inc(s["aggT_ps"], 1)
                    wait_alone(pe, s["aggT"], T + 1, s["fence_pe"])
                    nc.tensor.matmul(pB_flat, aggT[:], w2b[:], start=True, stop=True).then_inc(s["conv"], 1)

                def turn(i, k, j):
                    T = i * G + k
                    wait_alone(pe, s["xn"], T + 1, s["fence_pe"])
                    wait_alone(pe, s["xT_lo"], T + 1, s["fence_pe"])
                    for c in range(DK):
                        last = nc.tensor.transpose(pB[:, c, :], xn[:, j % 2, c * P:(c + 1) * P], ident[:])
                    last.then_inc(s["xT_ps"], 1)

                def hidden(ps, i, g, f, which):
                    hi, lo = (w[:, which * FB + f] for w in wgu)
                    x_hi, x_lo = xT[g][:, 0], xT[g][:, 1]
                    n = len(GROUPS[g]) * P
                    terms = [(w, v, c) for c in range(DK) for w, v in ((hi, x_hi), (hi, x_lo), (lo, x_hi))]
                    for m, (w, v, c) in enumerate(terms):
                        last = nc.tensor.matmul(ps[:, 0:n], w[:, c, :], v[:, c, :], start=(m == 0), stop=(m == len(terms) - 1))
                    return last

                def gate(i, g, f):
                    if f == 0:
                        wait_alone(pe, s["xT_lo"], i * G + (GROUPS[g][-1] + 2), s["fence_pe"])
                    wait_alone(pe, s["silu"], steps_before(i, g, f) + 1, s["fence_pe"])
                    hidden(pG, i, g, f, 0).then_inc(s["gate_ps"], 1)

                def up(i, g, f):
                    wait_alone(pe, s["hmul"], steps_before(i, g, f) + 1, s["fence_pe"])
                    hidden(pU, i, g, f, 1).then_inc(s["up_ps"], 1)

                def down(i, g, f):
                    step = steps_before(i, g, f)
                    slot = (g * FB + f) % 2
                    if f == 0:
                        wait_alone(pe, s["x2"], i * G + GROUPS[g][0] + 1, s["fence_pe"])
                    wait_alone(pe, wd_in[slot], (i * FB + ((g * FB + f) // 2 + 1)) * 16, s["fence_pe"])
                    wait_alone(pe, s["h_lo"], step + 2, s["fence_pe"])
                    for j in range(len(GROUPS[g])):
                        h_hi, h_lo = (hT[:, slot, m, j * P:(j + 1) * P] for m in range(2))
                        for m, (h, w) in enumerate(((h_hi, 0), (h_hi, 1), (h_lo, 0))):
                            last = nc.tensor.matmul(acc4[j][:], h, wd[:, slot, w, :], start=(f == 0 and m == 0),
                                                    stop=(f == FB - 1 and m == 2))
                    last.then_inc(s["down"], 1)

                groups(pe.Fori, Part(sums=sums, layer1=layer1, turn=turn, gate=gate, up=up, down=down))

            @block.scalar
            def _(act):
                act.sem_inc(s["h_lo"], 1)
                act.sem_inc(s["x2"], 1)
                act.sem_inc(s["row_stored"], 1)
                act.sem_inc(s["row_lo"], 1)

                def layer1(i, k, j):
                    T = i * G + k
                    act.wait_ge(s["aggT_ps"], T + 1)
                    nc.scalar.copy(aggT[:], pAT).then_inc(s["aggT"], 1)
                    act.wait_ge(s["conv"], T + 1)
                    if j >= 2:
                        act.wait_ge(s["x1"], T - 1)
                    elif not (isinstance(i, int) and i == 0 and k < 4):
                        act.wait_ge(s["row_lo"], T - j - (2 if k < 4 else 3))
                    nc.scalar.activation(xn[:, j % 2, :], pB_flat, ACT.Relu).then_inc(s["relu"], 1)

                def scale(i, g):
                    n = len(GROUPS[g])
                    act.wait_ge(s["var"], i * 2 + (g + 1))
                    nc.scalar.activation(rs[:, 0, 0:n, 0], var[:, 0, 0:n], ACT.Sqrt).then_inc(s["std"], 1)

                def turn(i, k, j):
                    T, g = i * G + k, int(k >= 4)
                    act.wait_ge(s["rs"], i * 2 + (g + 1))
                    if j >= 2:
                        act.wait_ge(s["xT_ps"], T - 1)
                    nc.scalar.activation(xn[:, j % 2, :], xr[:, k, :], ACT.Identity, bias=rs[:, 0, j, 1:2],
                                         scale=rs[:, 0, j, 0:1]).then_inc(s["xn"], 1)
                    act.wait_ge(s["xT_ps"], T + 1)
                    nc.scalar.copy(xT[g][:, 0, :, j * P:(j + 1) * P], pB[:]).then_inc(s["xT_hi"], 1)

                def gate(i, g, f):
                    step, n = steps_before(i, g, f), len(GROUPS[g]) * P
                    act.wait_ge(s["h_lo"], step + 1)
                    act.wait_ge(s["gate_ps"], step + 1)
                    nc.scalar.activation(sil[:, 0:n], pG[:, 0:n], ACT.Silu).then_inc(s["silu"], 1)

                def up(i, g, f):
                    step, n, slot = steps_before(i, g, f), len(GROUPS[g]) * P, (g * FB + f) % 2
                    act.wait_ge(s["hmul"], step + 2)
                    act.wait_ge(s["down"], step + 1)
                    nc.scalar.copy(hT[:, slot, 0, 0:n], sil[:, 0:n]).then_inc(s["h_hi"], 1)

                def scale_rows(i, g):
                    n = len(GROUPS[g])
                    act.wait_ge(s["var2"], i * 2 + (g + 1))
                    nc.scalar.activation(rs[:, 1, 0:n, 0], var[:, 1, 0:n], ACT.Sqrt).then_inc(s["std2"], 1)

                def rows(i, k, j):
                    T, g = i * G + k, int(k >= 4)
                    act.wait_ge(s["rs2"], i * 2 + (g + 1))
                    act.wait_ge(s["row_lo"], T + 1)
                    act.wait_ge(s["row_stored"], T + 1)
                    nc.scalar.activation(xn[:, j % 2, :], xr[:, k, :], ACT.Identity, bias=rs[:, 1, j, 1:2],
                                         scale=rs[:, 1, j, 0:1]).then_inc(s["xn2"], 1)
                    act.wait_ge(s["xn2"], T + 1)
                    nc.scalar.copy(pair[:, 0, :], xn[:, j % 2, :]).then_inc(s["row_hi"], 1)

                groups(act.Fori, Part(layer1=layer1, scale=scale, turn=turn, gate=gate, up=up,
                                      scale_rows=scale_rows, rows=rows))

            @block.vector
            def _(dve):
                own = Steps(dve, s["dve"])
                own.step(nc.vector.tensor_copy(tiota[:], iota[:]))
                own.step(nc.vector.memset(aggd[:], 1.0))
                nc.vector.memset(nv[:], 0.0).then_inc(s["nv_clear"], 1)

                def sums(i, k, j):
                    T = i * G + k
                    build_onehots(nc, dve, T, ranges, dstT, tiota, onehot, s["onehot"], s["used"])
                    dve.wait_ge(s["agg"], T + 1)
                    own.step(nc.vector.tensor_scalar_add(tiota[:], tiota[:], float(P)))
                    own.step(nc.vector.tensor_reduce(sums8[:], acc.rearrange("p (a f) -> p f a", f=H), AX, ALU.add))
                    dve.sem_inc(s["agg_used"], 1)
                    nc.vector.tensor_scalar(aggd[:, j, 0:H], sums8[:], dinv[:, ds(T, 1)], None, ALU.mult).then_inc(s["aggd"], 1)
                    dve.wait_ge(s["aggd"], T + 1)

                def layer1(i, k, j):
                    T = i * G + k
                    if isinstance(i, int) and i == 0:
                        dve.wait_ge(s["small_in"], 64)
                    dve.wait_ge(s["relu"], T + 1)
                    dve.wait_ge(x_in[k], (i + 1) * 16)
                    nc.vector.scalar_tensor_tensor(xr[:, k, :], xn[:, j % 2, :], nv[:, ds(T, 1)], xr[:, k, :],
                                                   ALU.mult, ALU.add).then_inc(s["x1"], 1)

                def stats_of(g, m, ready):
                    ks = GROUPS[g]
                    for j, k in enumerate(ks):
                        last = nc.vector.bn_stats(st[:, j, :], xr[:, k, :])
                    own.step(last)
                    dve.sem_inc(s["fence_dve"], 1)
                    for j, k in enumerate(ks):
                        last = nc.vector.bn_aggr(mv[:, m, j, :], st[:, j, :])
                    own.step(last)
                    own.step(nc.vector.tensor_scalar_add(var[:, m, 0:len(ks)], mv[:, m, 0:len(ks), 1], EPS))
                    dve.sem_inc(ready, 1)

                def scales_of(g, m, done):
                    n = len(GROUPS[g])
                    newton(nc, own, rs[:, m, 0:n, 0], var[:, m, 0:n], nw[:, 0:n])
                    own.step(nc.vector.scalar_tensor_tensor(rs[:, m, 0:n, 1], mv[:, m, 0:n, 0], -1.0, rs[:, m, 0:n, 0],
                                                            ALU.mult, ALU.mult))
                    dve.sem_inc(done, 1)

                def stats(i, g):
                    dve.wait_ge(s["x1"], i * G + (GROUPS[g][-1] + 1))
                    dve.wait_ge(s["xT_lo"], i * G + (GROUPS[g][0] + 1))
                    stats_of(g, 0, s["var"])

                def scale(i, g):
                    dve.wait_ge(s["std"], i * 2 + (g + 1))
                    scales_of(g, 0, s["rs"])

                def turn(i, k, j):
                    T, g = i * G + k, int(k >= 4)
                    dve.wait_ge(s["xT_hi"], T + 1)
                    nc.vector.tensor_tensor(xT[g][:, 1, :, j * P:(j + 1) * P], pB[:],
                                            xT[g][:, 0, :, j * P:(j + 1) * P].bitcast(F32), ALU.subtract).then_inc(s["xT_lo"], 1)

                def up(i, g, f):
                    step, n, slot = steps_before(i, g, f), len(GROUPS[g]) * P, (g * FB + f) % 2
                    dve.wait_ge(s["silu"], step + 2)
                    dve.wait_ge(s["up_ps"], step + 1)
                    nc.vector.tensor_tensor(sil[:, 0:n], pU[:, 0:n], sil[:, 0:n], ALU.mult).then_inc(s["hmul"], 1)
                    dve.wait_ge(s["hmul"], step + 2)
                    dve.wait_ge(s["h_hi"], step + 1)
                    nc.vector.tensor_tensor(hT[:, slot, 1, 0:n], sil[:, 0:n], hT[:, slot, 0, 0:n].bitcast(F32),
                                            ALU.subtract).then_inc(s["h_lo"], 1)

                def residual(i, g):
                    dve.wait_ge(s["down"], steps_before(i, g, FB) + 2)
                    for j, k in enumerate(GROUPS[g]):
                        last = nc.vector.tensor_tensor(xr[:, k, :], xr[:, k, :], acc4[j][:], ALU.add).then_inc(s["x2"], 1)
                    dve.wait_ge(s["x2"], i * G + (GROUPS[g][-1] + 2))
                    stats_of(g, 1, s["var2"])

                def scale_rows(i, g):
                    dve.wait_ge(s["std2"], i * 2 + (g + 1))
                    scales_of(g, 1, s["rs2"])

                def rows(i, k, j):
                    T = i * G + k
                    dve.wait_ge(s["row_hi"], T + 1)
                    nc.vector.tensor_tensor(pair[:, 1, :], xn[:, j % 2, :], pair[:, 0, :], ALU.subtract).then_inc(s["row_lo"], 1)

                groups(dve.Fori, Part(sums=sums, layer1=layer1, stats=stats, scale=scale, turn=turn, up=up,
                                      residual=residual, scale_rows=scale_rows, rows=rows,
                                      enter=lambda i: own.body(i, 2 * (3 + 6) * 2 + 2 * G, 1),
                                      leave=lambda: own.end(G - 2)))

        ffn.close()

        next_stage()
        s = {n: sem("d_" + n) for n in (
            "tables_in w_in small_in idx fence fence_sp fence_pe fence_dve rows_ready rows_used oh_ready mm_done added loaded loads "
            "const wT_ps wT scaled aT_ps aT conv x3 var std rs xf xf2 xT_ps xT logits lg_done lg expd onehot cum "
            "z stores stored base dve pool aggz".split())}
        landed = [[sem(f"d_landed{h}_{k}") for k in range(Q)] for h in range(4)]
        route = whole.enter_context(ExitStack())
        agg = sb(route, "agg3", [P, NT + 1, D], F32)
        gidx = sb(route, "gidx", [P, NT], I32)
        sidx = sb(route, "sidx", [P, NT], I32)
        pkeep = sb(route, "pkeep", [P, NT], F32)
        with ExitStack() as ctx:
            rows = sb(ctx, "rows", [P, 4, Q, 2 * D], F16)
            units = sb(ctx, "units3", [1, 3, UQ], I32)
            turns = sb(ctx, "turns3", [1, 3, NT], I32)
            idx = sb(ctx, "idx3", [P, 4, Q], I32)
            oh = sb(ctx, "oh3", [P, 2, Q, P], F16)
            iotah = sb(ctx, "iotah", [P, P], F16)
            bases = sb(ctx, "bases", [P, NT], F32)
            dstF = sb(ctx, "dstF", [P, UQ * Q], F32)
            zeroh = sb(ctx, "zeroh", [P, D], F16)
            wg = sb(ctx, "wg", [P, DK, D], F32)
            wgT = sb(ctx, "wgT", [P, DK, D], F32)
            bgb = sb(ctx, "bgb", [P, D], F32)
            alp = sb(ctx, "alp", [P, 1], F32)
            sw = sb(ctx, "sw", [NX, D], F32)
            swT = sb(ctx, "swT", [P, DK, NX], F32)
            swb = sb(ctx, "swb", [P, NX], F32)
            tri = sb(ctx, "tri", [P, 2, P], BF16)
            trash = sb(ctx, "trash", [P, 1], F32)
            scaled = sb(ctx, "scaled", [P, D], F32)
            aT = sb(ctx, "aT", [P, DK, P], F32)
            xf = sb(ctx, "xf", [P, D], F32)
            xfT = sb(ctx, "xfT", [P, DK, P], F32)
            x2l = sb(ctx, "x2l", [P, 3, D], F32)
            pl = sb(ctx, "pl", [P, 3, 2 * D], F16)
            res = sb(ctx, "res", [P, D], F32)
            x3 = sb(ctx, "x3", [P, 6, D], F32)
            st = sb(ctx, "dst", [P, 6], F32)
            mv = sb(ctx, "dmv", [P, 2], F32)
            var = sb(ctx, "dvar", [P, 1], F32)
            rs = sb(ctx, "drs", [P, 2], F32)
            nw = sb(ctx, "dnw", [P, 1], F32)
            lg = sb(ctx, "lg", [P, NX], F32)
            ex = sb(ctx, "ex", [P, NX], F32)
            top = sb(ctx, "top", [P, 8], F32)
            topi = sb(ctx, "topi", [P, 8], U32)
            ntop = sb(ctx, "ntop", [P, 1], F32)
            esum = sb(ctx, "esum", [P, 1], F32)
            rt = sb(ctx, "rt", [P, 1], F32)
            oh16 = sb(ctx, "oh16", [P, NX], F32)
            oh16b = sb(ctx, "oh16b", [P, NX], BF16)
            base = sb(ctx, "base", [P, NX], F32)
            w16 = sb(ctx, "w16", [P, 2, NX], F32)
            c1 = sb(ctx, "c1", [P, 8], F32)
            pV = pb(ctx, "pV", [P, 2, D], F32)
            pT = pb(ctx, "pT3", [P, DK, P], F32)
            pX = pb(ctx, "pX3", [P, DK, P], F32)
            pW = pb(ctx, "pW3", [P, D], F32)
            pR = pb(ctx, "pR3", [P, 512], F32)
            pC = pb(ctx, "pC3", [P, 512], F32)
            block = ctx.enter_context(nc.Block())
            LAGS = 5

            def tiles_in_turn(loop, part, enter, leave):
                def turn(t):
                    for lag_, step in part:
                        if not isinstance(t, int) or 0 <= t - lag_ < NT:
                            step(t - lag_)
                for t in range(LAGS):
                    turn(t)
                with loop(LAGS, NT) as t:
                    enter(t)
                    turn(t)
                leave()
                for t in range(NT, NT + LAGS):
                    turn(t)

            def turn_of(eng, t):
                return (eng.value_load(turns[0:1, 0, ds(t, 1)], min_val=0, max_val=UQ - 1),
                        eng.value_load(turns[0:1, 1, ds(t, 1)], min_val=1, max_val=UQ))

            def unit_at(eng, first, b):
                u = nc.s_assert_within(first + b, 0, UQ - 1, skip_runtime_bounds_check_because="block B's tables end at UQ")
                return (u, eng.value_load(units[0:1, 0, ds(u, 1)], min_val=0, max_val=NT - 1),
                        eng.value_load(units[0:1, 1, ds(u, 1)], min_val=1, max_val=NT),
                        eng.value_load(units[0:1, 2, ds(u, 1)], min_val=0, max_val=UQ * NT))

            @block.gpsimd
            def _(pool):
                own = Steps(pool, s["pool"])
                nc.gpsimd.iota(iotah[:], [[1, P]], base=0, channel_multiplier=0, allow_small_or_imprecise_dtypes=True)
                nc.gpsimd.iota(bases[:], [[P, NT]], base=0, channel_multiplier=0, allow_small_or_imprecise_dtypes=True)
                nc.gpsimd.iota(trash[:], [[0, 1]], base=SLOTS, channel_multiplier=1, allow_small_or_imprecise_dtypes=True)
                nc.gpsimd.memset(zeroh[:], 0.0)
                own.step(nc.gpsimd.memset(tri[:], 1.0))
                nc.gpsimd.affine_select(out=tri[:, 0, :], in_=tri[:, 0, :], compare_op=ALU.is_ge, fill=0.0,
                                        base=0, pattern=[[1, P]], channel_multiplier=-1).then_inc(s["const"], 1)
                pool.wait_ge(s["tables_in"], 32)
                bodies = pool.value_load(turns[0:1, 2, 0:1], min_val=1, max_val=UQ // Q)

                def issue(u, h):
                    wait_alone(pool, s["rows_used"], u + 1, s["fence"])
                    nc.gpsimd.tensor_copy(idx[:, h, :], srcT[:, ds(u * Q, Q)]).then_inc(s["idx"], 1)
                    wait_alone(pool, s["idx"], u + 1, s["fence"])
                    for k in range(Q):
                        nc.gpsimd.indirect_dma_start(
                            rows[:, h, k, :], None, xn2_rows,
                            bass.IndirectOffsetOnAxis(ap=idx[:, h, k:k + 1], axis=0)).then_inc(landed[h][k], 16)

                def drain(h, times):
                    for k in range(Q):
                        pool.wait_ge(landed[h][k], times * 16)
                    pool.sem_inc(s["rows_ready"], 1)

                issue(0, 0)
                issue(1, 1)
                with pool.Fori(0, bodies) as i:
                    for h in range(4):
                        issue(i * 4 + (h + 2), (h + 2) % 4)
                        drain(h, i + 1)
                for h in range(2):
                    drain(h, bodies + 1)

            @block.sync
            def _(sp):
                sp.dma_start(units[:], units_row).then_inc(s["tables_in"], 16)
                sp.dma_start(turns[:], turns_row).then_inc(s["tables_in"], 16)
                sp.dma_start(wg[:], Wg.rearrange("(m p) d -> p m d", p=P)).then_inc(s["w_in"], 16)
                sp.dma_start(bgb[:], bg.partition_broadcast(P)).then_inc(s["small_in"], 16)
                sp.dma_start(alp[:], alpha.partition_broadcast(P)).then_inc(s["small_in"], 16)
                sp.dma_start(sw[:], switch_w).then_inc(s["small_in"], 16)
                sp.dma_start(swb[:], switch_b.partition_broadcast(P)).then_inc(s["small_in"], 16)

                def load(T):
                    wait_alone(sp, s["x3"], T + 1, s["fence_sp"])
                    sp.dma_start(x2l[:, ds(T % 3, 1), :].rearrange("p a b -> p (a b)"), x2_rows[ds(T * P, P), :]).then_inc(s["loads"], 16)
                    sp.dma_start(pl[:, ds(T % 3, 1), :].rearrange("p a b -> p (a b)"), xn2_rows[ds(T * P, P), :]).then_inc(s["loads"], 16)
                    wait_alone(sp, s["loads"], (T + 1) * 32, s["loaded"])

                def store(T):
                    wait_alone(sp, s["z"], T + 1, s["fence_sp"])
                    sp.dma_start(z_rows[ds(T * P, P), :], x3[:, ds(T % 6, 1), :].rearrange("p a b -> p (a b)")).then_inc(s["stores"], 16)
                    wait_alone(sp, s["stores"], (T + 1) * 16, s["stored"])

                tiles_in_turn(sp.Fori, ((0, load), (5, store)), lambda t: None, lambda: None)

            @block.tensor
            def _(pe):
                pe.wait_ge(s["w_in"], 16)
                for c in range(DK):
                    if c > 0:
                        pe.wait_ge(s["wT"], c)
                    for m in range(DK):
                        last = nc.tensor.transpose(pW[:, m * P:(m + 1) * P], wg[:, m, c * P:(c + 1) * P], ident[:])
                    last.then_inc(s["wT_ps"], 1)
                pe.wait_ge(s["small_in"], 64)
                for c in range(DK):
                    last = nc.tensor.transpose(pR[:, c * NX:(c + 1) * NX], sw[:, c * P:(c + 1) * P], ident[0:NX, 0:NX])
                last.then_inc(s["wT_ps"], 1)
                pe.wait_ge(s["wT"], DK + 1)
                pe.wait_ge(s["const"], 1)
                pe.wait_ge(s["tables_in"], 32)
                nc.tensor.matmul(pV[:, 1, :], zeroh[:, 0:P], zeroh[:], start=True, stop=True).then_inc(s["mm_done"], 2)

                def cumulate(T):
                    wait_alone(pe, s["onehot"], T + 1, s["fence_pe"])
                    for m in range(2):
                        last = nc.tensor.matmul(pC[:, m * NX:(m + 1) * NX], tri[:, m, :], oh16b[:], start=True, stop=True)
                    last.then_inc(s["cum"], 1)

                def visit(t):
                    first, n = turn_of(pe, t)
                    with pe.Fori(0, n) as b:
                        u, tile, tiles, before = unit_at(pe, first, b)
                        wait_alone(pe, s["rows_ready"], u + 1, s["fence_pe"])
                        with pe.Fori(0, tiles) as k:
                            v = before + k
                            wait_alone(pe, s["added"], v + 1, s["fence_pe"])
                            wait_alone(pe, s["oh_ready"], v + 1, s["fence_pe"])
                            out_ = pV[:, ds(v % 2, 1), :].rearrange("p a b -> p (a b)")
                            for c in range(Q):
                                w = oh[:, ds(v % 2, 1), c, :].rearrange("p a b -> p (a b)")
                                for m in range(2):
                                    last = nc.tensor.matmul(
                                        out_, w, rows[:, ds(u % 4, 1), c, m * D:(m + 1) * D].rearrange("p a b -> p (a b)"),
                                        start=(c == 0 and m == 0), stop=(c == Q - 1 and m == 1))
                            last.then_inc(s["mm_done"], 1)

                def turn_sums(T):
                    wait_alone(pe, s["scaled"], T + 1, s["fence_pe"])
                    for c in range(DK):
                        last = nc.tensor.transpose(pT[:, c, :], scaled[:, c * P:(c + 1) * P], ident[:])
                    last.then_inc(s["aT_ps"], 1)

                def turn_rows(T):
                    wait_alone(pe, s["xf"], T + 1, s["fence_pe"])
                    for c in range(DK):
                        last = nc.tensor.transpose(pX[:, c, :], xf[:, c * P:(c + 1) * P], ident[:])
                    last.then_inc(s["xT_ps"], 1)

                def convolve(T):
                    wait_alone(pe, s["aT"], T + 1, s["fence_pe"])
                    wait_alone(pe, s["x3"], T + 3, s["fence_pe"])
                    for c in range(DK):
                        last = nc.tensor.matmul(pW[:], aT[:, c, :], wgT[:, c, :], start=(c == 0), stop=(c == DK - 1))
                    last.then_inc(s["conv"], 1)

                def logits(T):
                    wait_alone(pe, s["xT"], T + 1, s["fence_pe"])
                    wait_alone(pe, s["lg"], T + 1, s["fence_pe"])
                    for c in range(DK):
                        last = nc.tensor.matmul(pR[:, 0:NX], xfT[:, c, :], swT[:, c, :], start=(c == 0), stop=(c == DK - 1))
                    last.then_inc(s["logits"], 1)

                tiles_in_turn(pe.Fori, ((5, cumulate), (0, visit), (1, turn_sums), (3, turn_rows), (1, convolve),
                                        (3, logits)), lambda t: None, lambda: None)

            @block.scalar
            def _(act):
                for c in range(DK):
                    act.wait_ge(s["wT_ps"], c + 1)
                    nc.scalar.copy(wgT[:, c, :], pW[:]).then_inc(s["wT"], 1)
                act.wait_ge(s["wT_ps"], DK + 1)
                nc.scalar.copy(swT[:].rearrange("p a b -> p (a b)"), pR[:, 0:DK * NX]).then_inc(s["wT"], 1)

                def normalize(T):
                    act.wait_ge(s["rs"], T + 1)
                    if not isinstance(T, int) or T > 0:
                        act.wait_ge(s["xT_ps"], T)
                    at = x3[:, ds(T % 6, 1), :].rearrange("p a b -> p (a b)")
                    nc.scalar.activation(xf[:], at, ACT.Identity, bias=rs[:, 1:2], scale=rs[:, 0:1]).then_inc(s["xf"], 1)
                    nc.scalar.activation(agg[:, ds(T, 1), :].rearrange("p a b -> p (a b)"), at, ACT.Identity,
                                         bias=rs[:, 1:2], scale=rs[:, 0:1]).then_inc(s["xf2"], 1)

                def sums_out(T):
                    act.wait_ge(s["aT_ps"], T + 1)
                    nc.scalar.copy(aT[:], pT[:]).then_inc(s["aT"], 1)

                def rows_out(T):
                    act.wait_ge(s["xT_ps"], T + 1)
                    nc.scalar.copy(xfT[:], pX[:]).then_inc(s["xT"], 1)

                def root(T):
                    act.wait_ge(s["var"], T + 1)
                    nc.scalar.activation(rs[:, 0:1], var[:], ACT.Sqrt).then_inc(s["std"], 1)

                def exps(T):
                    act.wait_ge(s["lg_done"], T + 1)
                    nc.scalar.activation(ex[:], lg[:], ACT.Exp, bias=ntop[:], accum_out=esum[:]).then_inc(s["expd"], 1)

                tiles_in_turn(act.Fori, ((3, normalize), (1, sums_out), (3, rows_out), (2, root), (4, exps)),
                              lambda t: None, lambda: None)

            @block.vector
            def _(dve):
                own = Steps(dve, s["dve"])
                dve.sem_inc(s["rows_used"], 3)
                dve.sem_inc(s["x3"], 3)
                dve.sem_inc(s["lg"], 1)
                dve.sem_inc(s["stored"], 6)
                own.step(nc.vector.memset(base[:], 0.0))
                own.step(nc.vector.memset(dstF[:], float(FAR)))
                own.step(nc.vector.tensor_copy(dstF[:, 0:C], dstT[:, 0:C]))
                own.step(nc.vector.memset(agg[:], 0.0))
                dve.sem_inc(s["added"], 1)
                dve.wait_ge(s["small_in"], 64)
                own.step(nc.vector.tensor_scalar(bgb[:], bgb[:], alp[:], None, ALU.mult))
                dve.wait_ge(s["const"], 1)
                dve.wait_ge(s["tables_in"], 32)
                pending = dve.alloc_register("pending")
                dve.reg_mov(pending, NT)

                def add_pending(v):
                    tile = nc.s_assert_within(dve.snap(pending), 0, NT, skip_runtime_bounds_check_because="a tile, or NT")
                    wait_alone(dve, s["mm_done"], v + 2, s["fence_dve"])
                    wait_alone(dve, s["added"], v + 1, s["fence_dve"])
                    at = agg[:, ds(tile, 1), :].rearrange("p a b -> p (a b)")
                    nc.vector.tensor_tensor(at, at, pV[:, ds((v + 1) % 2, 1), :].rearrange("p a b -> p (a b)"),
                                            ALU.add).then_inc(s["added"], 1)

                def visit(t):
                    first, n = turn_of(dve, t)
                    with dve.Fori(0, n) as b:
                        u, tile0, tiles, before = unit_at(dve, first, b)
                        with dve.Fori(0, tiles) as k:
                            v = before + k
                            tile = nc.s_assert_within(tile0 + k, 0, NT - 1, skip_runtime_bounds_check_because="block B's tables")
                            wait_alone(dve, s["mm_done"], v + 1, s["fence_dve"])
                            for c in range(Q):
                                last = nc.vector.tensor_scalar(
                                    oh[:, ds(v % 2, 1), c, :].rearrange("p a b -> p (a b)"), iotah[:], bases[:, ds(tile, 1)],
                                    dstF[:, ds(u * Q + c, 1)], ALU.add, ALU.is_equal)
                            last.then_inc(s["oh_ready"], 1)
                            add_pending(v)
                            dve.reg_mov(pending, tile)
                        dve.sem_inc(s["rows_used"], 1)

                def scale(T):
                    if isinstance(T, int) and T == NT - 1:
                        last_unit = nc.s_assert_within(dve.value_load(turns[0:1, 0, NT - 1:NT], min_val=0, max_val=UQ) +
                                                       dve.value_load(turns[0:1, 1, NT - 1:NT], min_val=1, max_val=UQ) - 1, 0, UQ - 1,
                                                       skip_runtime_bounds_check_because="block B's tables")
                        _, _, tiles, before = unit_at(dve, last_unit, 0)
                        add_pending(before + tiles)
                        wait_alone(dve, s["added"], before + tiles + 2, s["fence_dve"])
                    else:
                        first, _ = turn_of(dve, T + 1)
                        _, _, _, before = unit_at(dve, first, 0)
                        wait_alone(dve, s["added"], before + 2, s["fence_dve"])
                    if not isinstance(T, int) or T > 0:
                        wait_alone(dve, s["aT_ps"], T, s["fence_dve"])
                    nc.vector.tensor_scalar(scaled[:], agg[:, ds(T, 1), :].rearrange("p a b -> p (a b)"),
                                            invdeg[:, ds(T, 1)], None, ALU.mult).then_inc(s["scaled"], 1)

                def residual(T):
                    wait_alone(dve, s["loaded"], T + 1, s["fence_dve"])
                    parts = pl[:, ds(T % 3, 1), :].rearrange("p a (m d) -> p (a m) d", m=2)
                    own.step(nc.vector.tensor_tensor(res[:], parts[:, 0, :], parts[:, 1, :], ALU.add))
                    own.step(nc.vector.tensor_tensor(res[:], res[:], x2l[:, ds(T % 3, 1), :].rearrange("p a b -> p (a b)"), ALU.add))
                    own.step(nc.vector.tensor_tensor(res[:], res[:], bgb[:], ALU.add))
                    wait_alone(dve, s["conv"], T + 1, s["fence_dve"])
                    wait_alone(dve, s["stored"], T + 1, s["fence_dve"])
                    at = x3[:, ds(T % 6, 1), :].rearrange("p a b -> p (a b)")
                    own.step(nc.vector.scalar_tensor_tensor(at, pW[:], alp[:], res[:], ALU.mult, ALU.add))
                    dve.sem_inc(s["x3"], 1)
                    own.step(nc.vector.bn_stats(st[:], at))
                    dve.sem_inc(s["fence_dve"], 1)
                    own.step(nc.vector.bn_aggr(mv[:], st[:]))
                    if not isinstance(T, int) or T > 0:
                        wait_alone(dve, s["xf2"], T, s["fence_dve"])
                    own.step(nc.vector.tensor_scalar_add(var[:], mv[:, 1:2], EPS))
                    dve.sem_inc(s["var"], 1)

                def scales(T):
                    wait_alone(dve, s["std"], T + 1, s["fence_dve"])
                    newton(nc, own, rs[:, 0:1], var[:], nw[:])
                    own.step(nc.vector.scalar_tensor_tensor(rs[:, 1:2], mv[:, 0:1], -1.0, rs[:, 0:1], ALU.mult, ALU.mult))
                    dve.sem_inc(s["rs"], 1)

                def routes(T):
                    wait_alone(dve, s["logits"], T + 1, s["fence_dve"])
                    if not isinstance(T, int) or T > 0:
                        wait_alone(dve, s["expd"], T, s["fence_dve"])
                    own.step(nc.vector.tensor_tensor(lg[:], pR[:, 0:NX], swb[:], ALU.add))
                    dve.sem_inc(s["lg"], 1)
                    own.step(nc.vector.max(top[:], lg[:]))
                    own.step(nc.vector.tensor_scalar_mul(ntop[:], top[:, 0:1], -1.0))
                    dve.sem_inc(s["lg_done"], 1)
                    own.step(nc.vector.max_index(topi[:], top[:], lg[:]))
                    own.step(nc.vector.tensor_copy(rt[:], topi[:, 0:1]))
                    own.step(nc.vector.tensor_scalar(oh16[:], iota[:, 0:NX], rt[:], None, ALU.is_equal))
                    own.step(nc.vector.tensor_copy(oh16b[:], oh16[:]))
                    dve.sem_inc(s["onehot"], 1)

                def place(T):
                    col = [c1[:, j:j + 1] for j in range(8)]
                    wait_alone(dve, s["cum"], T + 1, s["fence_dve"])
                    own.step(nc.vector.tensor_tensor(w16[:, 0, :], pC[:, 0:NX], base[:], ALU.add))
                    own.step(nc.vector.tensor_tensor(base[:], pC[:, NX:2 * NX], base[:], ALU.add))
                    own.step(nc.vector.tensor_tensor(w16[:, 1, :], w16[:, 0, :], oh16[:], ALU.mult))
                    own.step(nc.vector.tensor_reduce(col[0], w16[:, 1, :], AX, ALU.add))
                    own.step(nc.vector.tensor_scalar(col[1], col[0], float(CAP), None, ALU.is_le))
                    own.step(nc.vector.scalar_tensor_tensor(col[2], rt[:], float(CAP), col[0], ALU.mult, ALU.add))
                    own.step(nc.vector.tensor_scalar_add(col[2], col[2], -1.0))
                    nc.vector.tensor_scalar(gidx[:, ds(T, 1)], col[2], col[1], None, ALU.mult)
                    own.step(nc.vector.tensor_sub(col[3], col[2], trash[:]))
                    nc.vector.tensor_scalar(sidx[:, ds(T, 1)], col[3], col[1], trash[:], ALU.mult, ALU.add)
                    wait_alone(dve, s["expd"], T + 1, s["fence_dve"])
                    own.step(nc.vector.reciprocal(col[4], esum[:]))
                    own.step(nc.vector.tensor_mul(col[5], col[4], col[1]))
                    nc.vector.tensor_copy(pkeep[:, ds(T, 1)], col[5])
                    own.step(nc.vector.tensor_sub(col[6], col[4], col[5]))
                    wait_alone(dve, s["xf2"], T + 1, s["fence_dve"])
                    at = x3[:, ds(T % 6, 1), :].rearrange("p a b -> p (a b)")
                    own.step(nc.vector.scalar_tensor_tensor(at, agg[:, ds(T, 1), :].rearrange("p a b -> p (a b)"), col[6], at,
                                                            ALU.mult, ALU.add))
                    dve.sem_inc(s["z"], 1)

                tiles_in_turn(dve.Fori, ((3, scales), (0, visit), (1, scale), (2, residual), (5, place), (4, routes)),
                              lambda t: own.body(t, 6 + 7 + 7 + 12, LAGS), lambda: own.end(NT - LAGS))

        next_stage()
        s = {n: sem("e_" + n) for n in (
            "scattered_all y_free y_stored wT_ps wT xT_ps xT y y_ps fence_sp fence_pe fence_dve".split())}
        sc_out = sem("e_sc")
        w_in = [sem(f"e_w_in{j}") for j in range(2)]
        b_in = [sem(f"e_b_in{j}") for j in range(2)]
        r_in = [sem(f"e_r_in{j}") for j in range(ET)]
        y_out = [sem(f"e_y_out{j}") for j in range(ET)]
        with ExitStack() as ctx:
            we = sb(ctx, "we", [P, 2, DK, D], F32)
            weT = sb(ctx, "weT", [P, DK, D], F32)
            be = sb(ctx, "be", [P, 2, D], F32)
            er = sb(ctx, "er", [P, ET, D], F32)
            erT = sb(ctx, "erT", [P, 2, DK, P], F32)
            ye = sb(ctx, "ye", [P, ET, D], F32)
            pWT = [pb(ctx, f"pWT{j}", [P, DK, P], F32) for j in range(2)]
            pXT = [pb(ctx, f"pXT{j}", [P, DK, P], F32) for j in range(2)]
            pY = [pb(ctx, f"pY{j}", [P, D], F32) for j in range(2)]
            block = ctx.enter_context(nc.Block())
            sizes = [min(P, CAP - j * P) for j in range(ET)]

            @block.gpsimd
            def _(pool):
                for t in range(NT):
                    if t > 0:
                        pool.wait_ge(sc_out, t * 16)
                    nc.gpsimd.indirect_dma_start(expert_rows, bass.IndirectOffsetOnAxis(ap=sidx[:, t:t + 1], axis=0),
                                                 agg[:, t, :], None).then_inc(sc_out, 16)
                pool.wait_ge(sc_out, NT * 16)
                pool.sem_inc(s["scattered_all"], 1)

            @block.sync
            def _(sp):
                def load_w(e, j):
                    sp.dma_start(we[:, j, :, :], expert_w[ds(e, 1), :, :].rearrange("a (m p) d -> p (a m) d", p=P)).then_inc(w_in[j], 16)
                    sp.dma_start(be[:, j, :], expert_b[ds(e, 1), :].rearrange("a b -> (a b)").partition_broadcast(P)).then_inc(b_in[j], 16)

                sp.sem_inc(s["y_stored"], ET)
                load_w(0, 0)
                load_w(1, 1)
                sp.wait_ge(s["scattered_all"], 1)
                with sp.Fori(0, NX // 2) as i:
                    for j in range(2):
                        e = i * 2 + j
                        for m, n in enumerate(sizes):
                            wait_alone(sp, s["xT_ps"], e * ET + (m + 1), s["fence_sp"])
                            sp.dma_start(er[0:n, m, :], expert_rows[ds(e * CAP + m * P, n), :]).then_inc(r_in[m], 16)
                        for m, n in enumerate(sizes):
                            wait_alone(sp, s["y"], e * ET + (m + 3), s["fence_sp"])
                            sp.dma_start(y_rows[ds(e * CAP + m * P, n), :], ye[0:n, m, :]).then_inc(y_out[m], 16)
                        for m in range(ET):
                            wait_alone(sp, y_out[m], (e + 1) * 16, s["y_stored"])
                        nxt = nc.s_assert_within(i * 2 + (j + 2), 0, NX + 1, skip_runtime_bounds_check_because="i < NX / 2")
                        nxt = (e + 2) % NX
                        load_w(nxt, j)
                for j in range(2):
                    sp.wait_ge(w_in[j], (NX // 2 + 1) * 16)
                    sp.wait_ge(b_in[j], (NX // 2 + 1) * 16)
                for m in range(ET):
                    sp.wait_ge(y_out[m], NX * 16)

            @block.tensor
            def _(pe):
                pe.sem_inc(s["xT_ps"], ET)
                pe.sem_inc(s["wT"], 2)
                pe.sem_inc(s["xT"], 2)
                pe.sem_inc(s["y"], 2)
                with pe.Fori(0, NX // 2) as i:
                    for j in range(2):
                        e = i * 2 + j
                        wait_alone(pe, w_in[j], (i + 1) * 16, s["fence_pe"])
                        for c in range(DK):
                            wait_alone(pe, s["wT"], e * DK + (c + 1), s["fence_pe"])
                            for m in range(DK):
                                last = nc.tensor.transpose(pWT[c % 2][:, m, :], we[:, j, m, c * P:(c + 1) * P], ident[:])
                            last.then_inc(s["wT_ps"], 1)

                        def product(m):
                            n = sizes[m]
                            wait_alone(pe, s["xT"], e * ET + (m + 3), s["fence_pe"])
                            if m == 0:
                                wait_alone(pe, s["wT"], e * DK + (DK + 2), s["fence_pe"])
                            wait_alone(pe, s["y"], e * ET + (m + 1), s["fence_pe"])
                            for c in range(DK):
                                last = nc.tensor.matmul(pY[m % 2][0:n, :], erT[:, m % 2, c, 0:n], weT[:, c, :],
                                                        start=(c == 0), stop=(c == DK - 1))
                            last.then_inc(s["y_ps"], 1)

                        for m, n in enumerate(sizes):
                            wait_alone(pe, r_in[m], (e + 1) * 16, s["fence_pe"])
                            wait_alone(pe, s["xT"], e * ET + (m + 1), s["fence_pe"])
                            for c in range(DK):
                                last = nc.tensor.transpose(pXT[m % 2][:, c, 0:n], er[0:n, m, c * P:(c + 1) * P], ident[0:n, 0:n])
                            last.then_inc(s["xT_ps"], 1)
                            if m > 0:
                                product(m - 1)
                        product(ET - 1)

            @block.scalar
            def _(act):
                act.sem_inc(s["y_free"], 1)
                with act.Fori(0, NX // 2) as i:
                    for j in range(2):
                        e = i * 2 + j
                        for c in range(DK):
                            act.wait_ge(s["wT_ps"], e * DK + (c + 1))
                            act.wait_ge(s["y_free"], e * ET + 1)
                            nc.scalar.copy(weT[:, c, :], pWT[c % 2][:].rearrange("p a b -> p (a b)")).then_inc(s["wT"], 1)
                        for m, n in enumerate(sizes):
                            act.wait_ge(s["xT_ps"], e * ET + (m + 1 + ET))
                            if m >= 2:
                                act.wait_ge(s["y_ps"], e * ET + (m - 1))
                            nc.scalar.copy(erT[:, m % 2, :, 0:n], pXT[m % 2][:, :, 0:n]).then_inc(s["xT"], 1)

            @block.vector
            def _(dve):
                with dve.Fori(0, NX // 2) as i:
                    for j in range(2):
                        e = i * 2 + j
                        wait_alone(dve, b_in[j], (i + 1) * 16, s["fence_dve"])
                        for m, n in enumerate(sizes):
                            wait_alone(dve, s["y_ps"], e * ET + (m + 1), s["fence_dve"])
                            dve.sem_inc(s["y_free"], 1)
                            wait_alone(dve, s["y_stored"], e * ET + (m + 1), s["fence_dve"])
                            nc.vector.tensor_tensor(ye[0:n, m, :], pY[m % 2][0:n, :], be[0:n, j, :], ALU.add).then_inc(s["y"], 1)

        next_stage()
        s = {n: sem("f_" + n) for n in "idx fence fence_sp fence_dve done out_free".split()}
        y_in, z_in, o_out = ([sem(f"f_{n}{k}") for k in range(G)] for n in ("y_in", "z_in", "o_out"))
        with ExitStack() as ctx:
            idx = sb(ctx, "idx4", [P, G], I32)
            yl = sb(ctx, "yl", [P, G, D], F32)
            zl = sb(ctx, "zl", [P, G, D], F32)
            ol = sb(ctx, "ol4", [P, G, D], F32)
            block = ctx.enter_context(nc.Block())

            @block.gpsimd
            def _(pool):
                with pool.Fori(0, G) as i:
                    wait_alone(pool, s["done"], i * G + 1, s["fence"])
                    nc.gpsimd.tensor_copy(idx[:], gidx[:, ds(i * G, G)]).then_inc(s["idx"], 1)
                    wait_alone(pool, s["idx"], i + 1, s["fence"])
                    for k in range(G):
                        nc.gpsimd.indirect_dma_start(yl[:, k, :], None, y_rows,
                                                     bass.IndirectOffsetOnAxis(ap=idx[:, k:k + 1], axis=0)).then_inc(y_in[k], 16)

            @block.sync
            def _(sp):
                def load(i, k):
                    sp.dma_start(zl[:, k, :], z_rows[ds((i * G + k) * P, P), :]).then_inc(z_in[k], 16)

                def store(i, k, rows=P):
                    wait_alone(sp, s["done"], i * G + (k + 2), s["fence_sp"])
                    sp.dma_start(out[ds((i * G + k) * P, rows), :], ol[0:rows, k, :]).then_inc(o_out[k], 16)

                for k in range(G):
                    load(0, k)
                with sp.Fori(0, G - 1) as i:
                    for k in range(G):
                        store(i, k)
                        load(i + 1, k)
                    for k in range(G):
                        wait_alone(sp, o_out[k], (i + 1) * 16, s["out_free"])
                for k in range(G):
                    store(G - 1, k, P if k < G - 1 else LAST)
                for k in range(G):
                    sp.wait_ge(o_out[k], G * 16)

            @block.vector
            def _(dve):
                dve.sem_inc(s["done"], 1)
                dve.sem_inc(s["out_free"], G)
                with dve.Fori(0, G) as i:
                    for k in range(G):
                        T = i * G + k
                        wait_alone(dve, y_in[k], (i + 1) * 16, s["fence_dve"])
                        wait_alone(dve, z_in[k], (i + 1) * 16, s["fence_dve"])
                        wait_alone(dve, s["out_free"], T + 1, s["fence_dve"])
                        nc.vector.scalar_tensor_tensor(ol[:, k, :], yl[:, k, :], pkeep[:, ds(T, 1)], zl[:, k, :],
                                                       ALU.mult, ALU.add).then_inc(s["done"], 1)
        route.close()



def scan(nc, own, rows, a, b, n, op):
    d = 1
    while d < n:
        own.step(nc.vector.tensor_copy(rows[b], rows[a]))
        own.step(nc.vector.tensor_tensor(rows[b][:, d:n], rows[a][:, d:n], rows[a][:, 0:n - d], op))
        a, b, d = b, a, 2 * d
    return a, b


NEWTON = 5


def newton(nc, own, r, v, t):
    own.step(nc.vector.reciprocal(r, r))
    own.step(nc.vector.tensor_mul(t, v, r))
    own.step(nc.vector.tensor_mul(t, t, r))
    own.step(nc.vector.tensor_scalar(t, t, -0.5, 1.5, ALU.mult, ALU.add))
    own.step(nc.vector.tensor_mul(r, r, t))


def split3(nc, own, out3, val, rest):
    parts = [out3[:, :, j * H:(j + 1) * H] for j in range(3)]
    r = [rest[:, j, :].rearrange("p (t f) -> p t f", f=H) for j in range(2)]
    own.step(nc.vector.tensor_copy(parts[0], val[:]))
    own.step(nc.vector.tensor_tensor(r[0], val[:], parts[0], ALU.subtract))
    own.step(nc.vector.tensor_copy(parts[1], r[0]))
    own.step(nc.vector.tensor_tensor(r[1], r[0], parts[1], ALU.subtract))
    own.step(nc.vector.tensor_copy(parts[2], r[1]))


_INS = ['x', 'src', 'dst', 'node_vec1', 'L0_gnn_W1', 'L0_gnn_b1', 'L0_gnn_gamma', 'L0_gnn_beta', 'L0_gnn_W2',
        'L0_gnn_b2', 'L0_ffn_w_gate', 'L0_ffn_w_up', 'L0_ffn_w_down', 'L1_gnn_alpha', 'L1_gnn_W', 'L1_gnn_b',
        'L1_ffn_switch_w', 'L1_ffn_switch_b', 'L1_ffn_expert_w', 'L1_ffn_expert_b']


def kernel(**inputs):
    import numpy as np
    import concourse.bacc as bacc
    from concourse.bass_utils import run_bass_kernel_spmd

    nc = bacc.Bacc("TRN2", target_bir_lowering=False, num_devices=1)
    arrays, args = {}, []
    for name in _INS:
        a = np.ascontiguousarray(inputs[name])
        if a.ndim == 0:
            a = a.reshape(1)
        arrays[f"in_{name}"] = a
        args.append(nc.dram_tensor(f"in_{name}", a.shape, mybir.dt.from_np(a.dtype), kind="ExternalInput").ap())
    args.append(nc.dram_tensor("out_0", (N, D), F32, kind="ExternalOutput").ap())
    program(nc, *args)
    r = run_bass_kernel_spmd(nc, [arrays], core_ids=[0])
    return r.results[0]["out_0"]
```

```python
import concourse.bass as bass
from concourse import mybir
from contextlib import ExitStack

F32 = mybir.dt.float32
F32R = mybir.dt.float32r
BF16 = mybir.dt.bfloat16
F16 = mybir.dt.float16
I32 = mybir.dt.int32
I16 = mybir.dt.int16
U32 = mybir.dt.uint32
ALU = mybir.AluOpType
ACT = mybir.ActivationFunctionType
AX = mybir.AxisListType.X
ds = bass.ds

P = 128
N = 6250
D = 512
DK = D // P
NT = -(-N // P)
LAST = N - (NT - 1) * P
G = 7
E = 100000
EB = 7
EP = 112
C = EB * EP
U = 16
V = 8
CU = -(-C // U)
CV = C // V
CX = C + U - 1
Q = 4
CQ = C // Q
FAR = NT * P
H = 8
H3 = 3 * H
F = 1408
FB = F // P
NX = 16
CAP = int(1.2 * N / NX)
ET = -(-CAP // P)
SLOTS = NX * CAP
EPS = 1e-5


def lag(k):
    return {0: 1, 1: 3}.get(k, 2)


FREE = 3


class Steps:

    def __init__(self, eng, sem):
        self.eng, self.sem, self.n, self.i, self.per = eng, sem, 0, None, 0

    def body(self, i, per, first=0):
        self.i, self.per, self.start, self.k = i - first, per, self.n, 0

    def end(self, times):
        assert self.k == self.per, (self.k, self.per)
        self.n, self.i = self.start + times * self.per, None

    def step(self, ins):
        ins.then_inc(self.sem, 1)
        if self.i is None:
            self.n += 1
            self.eng.wait_ge(self.sem, self.n)
        else:
            self.k += 1
            self.eng.wait_ge(self.sem, self.i * self.per + (self.start + self.k))


def bc(ap, shape):
    return ap.to_broadcast(list(shape))


def wait_alone(eng, sem, value, fence):
    eng.wait_ge(sem, value)
    eng.sem_inc(fence, 1)


def gather_units(nc, pool, table, srcT, idx, stage, msg, landed, idx_ready, msg_ready, fence):

    def issue(u, h):
        nc.gpsimd.tensor_copy(idx[:, h, :], srcT[:, ds(u * V, V)]).then_inc(idx_ready, 1)
        pool.wait_ge(idx_ready, u + 1)
        pool.sem_inc(fence, 1)
        for k in range(V):
            nc.gpsimd.indirect_dma_start(
                stage[:, h, k, :], None, table,
                bass.IndirectOffsetOnAxis(ap=idx[:, h, k:k + 1], axis=0)).then_inc(landed[h][k], 16)

    def place(u, h, times):
        for k in range(V):
            pool.wait_ge(landed[h][k], times * 16)
        pool.sem_inc(fence, 1)
        nc.gpsimd.tensor_copy(msg[:, ds(u * V, V), :], stage[:, h, :, :]).then_inc(msg_ready, 1)
        pool.wait_ge(msg_ready, u + 1)

    issue(0, 0)
    with pool.Fori(0, CV // 2 - 1) as i:
        issue(i * 2 + 1, 1)
        place(i * 2, 0, i + 1)
        issue(i * 2 + 2, 0)
        place(i * 2 + 1, 1, i + 1)
    issue(CV - 1, 1)
    place(CV - 2, 0, CV // 2)
    place(CV - 1, 1, CV // 2)


def tile_range(eng, ranges, t, rows):
    top = {0: (0, C - 1), 1: (1, CU + 1), 2: (1, CV + U // V), 3: (0, NT * (CU + 1))}
    return [eng.value_load(ranges[0:1, j, ds(t, 1)], min_val=top[j][0], max_val=top[j][1]) for j in rows]


def chunk_at(nc, first, b, k, size):
    at = nc.s_assert_within(first + b * U + k, 0, CX - size, skip_runtime_bounds_check_because=
                            "first + units * U <= CX, as block A computes the ranges")
    return ds(at, size)


def build_onehots(nc, dve, t, ranges, dstT, tiota, onehot, ready, used):
    c0, units, before = tile_range(dve, ranges, t, (0, 1, 3))
    with dve.Fori(0, units) as b:
        for h in range(2):
            dve.wait_ge(used, (before + b) * 2 + (h + 1))
            nc.vector.tensor_tensor(onehot[:, h, :, :], bc(tiota[:].unsqueeze(1), (P, U // 2, P)),
                                    bc(dstT[:, chunk_at(nc, c0, b, h * (U // 2), U // 2)].unsqueeze(2), (P, U // 2, P)),
                                    ALU.is_equal).then_inc(ready, 1)


def sum_messages(nc, pe, t, ranges, hid, msg, identb, zerob, acc, onehot, ready, used, msg_ready):
    c0, units, rows, before = tile_range(pe, ranges, t, (0, 1, 2, 3))
    nc.tensor.matmul(acc, identb[:], hid[:, ds(t, 1), :].rearrange("p a b -> p (a b)"), start=True, stop=False)
    with pe.Fori(0, units) as b:
        pe.wait_ge(msg_ready, rows + b * (U // V))
        unit = msg[:, chunk_at(nc, c0, b, 0, U), :]
        for h in range(2):
            pe.wait_ge(ready, (before + b) * 2 + (h + 1))
            for k in range(U // 2):
                last = nc.tensor.matmul(acc, onehot[:, h, k, :], unit[:, h * (U // 2) + k, :],
                                        start=False, stop=False)
            last.then_inc(used, 1)
    return nc.tensor.matmul(acc, identb[:], zerob[:], start=False, stop=True)


GROUPS = ((0, 1, 2, 3), (4, 5, 6))


def groups(loop, part):

    def run(steps, body, g):
        ks = GROUPS[g]
        for step, j in steps:
            if j is None:
                step(body, g)
            elif j < len(ks):
                step(body, ks[j], j)

    ahead = {(j, 2): [(part.build, j)] for j in range(4)} | {
        (1 + j, 1): [(part.sums, j)] for j in range(4)} | {
        (5, 1): [(part.agg_turn, 0)],
        (5, 2): [(part.layer1, 0), (part.agg_turn, 1)],
        (6, 0): [(part.layer1, 1), (part.agg_turn, 2)],
        (6, 1): [(part.layer1, 2), (part.agg_turn, 3)],
        (6, 2): [(part.layer1, 3)],
        (7, 0): [(part.stats, None)],
        (8, 0): [(part.scale, None)],
        (8, 2): [(part.norm, 0), (part.norm, 1)],
        (9, 0): [(part.turn, 0), (part.norm, 2)],
        (9, 1): [(part.turn, 1), (part.norm, 3)],
        (9, 2): [(part.turn, 2)],
        (10, 0): [(part.turn, 3)]}
    behind = {(1 + j, 0): [(part.rows, j)] for j in range(4)} | {
        (0, 0): [(part.residual, None)],
        (0, 2): [(part.scale_rows, None)]}

    def group(i, g, after, before):
        def beside(*place):
            if before is not None:
                run(behind.get(place, ()), *before)
            if after is not None:
                run(ahead.get(place, ()), *after)

        for f in range(FB):
            part.gate(i, g, f)
            beside(f, 0)
            part.up(i, g, f)
            beside(f, 1)
            if f > 0:
                part.down(i, g, f - 1)
            beside(f, 2)
        part.down(i, g, FB - 1)

    for place in sorted(ahead):
        run(ahead[place], 0, 0)
    group(0, 0, (0, 1), None)
    group(0, 1, (1, 0), (0, 0))
    with loop(1, G - 1) as i:
        part.enter(i)
        group(i, 0, (i, 1), (i - 1, 1))
        group(i, 1, (i + 1, 0), (i, 0))
    part.leave()
    group(G - 1, 0, (G - 1, 1), (G - 2, 1))
    group(G - 1, 1, None, (G - 1, 0))
    for place in sorted(behind):
        run(behind[place], G - 1, 1)


def nothing(*args):
    pass


class Part:

    def __init__(self, gate=nothing, up=nothing, down=nothing, build=nothing, sums=nothing, agg_turn=nothing, layer1=nothing,
                 stats=nothing, scale=nothing, norm=nothing, turn=nothing, residual=nothing, scale_rows=nothing, rows=nothing,
                 enter=nothing, leave=nothing):
        self.gate, self.up, self.down = gate, up, down
        self.build, self.sums, self.agg_turn, self.layer1 = build, sums, agg_turn, layer1
        self.stats, self.scale, self.norm, self.turn = stats, scale, norm, turn
        self.residual, self.scale_rows, self.rows = residual, scale_rows, rows
        self.enter, self.leave = enter, leave


def program(nc, x, src, dst, node_vec, W1, b1, gamma, beta, W2, b2, w_gate, w_up, w_down,
            alpha, Wg, bg, switch_w, switch_b, expert_w, expert_b, out):
    with ExitStack() as whole:
        def sb(ctx, name, shape, dt):
            return ctx.enter_context(nc.sbuf_tensor(name, shape, dt))

        def pb(ctx, name, shape, dt):
            return ctx.enter_context(nc.psum_tensor(name, shape, dt))

        stage_sems = []

        def sem(name):
            stage_sems.append(nc.alloc_semaphore(name=name))
            return stage_sems[-1]

        def next_stage():
            nc.clear_and_free_semaphores(stage_sems)
            stage_sems.clear()
            nc.all_engine_barrier()

        def dram(name, shape, dt):
            return nc.dram_tensor(name, shape, dt, kind="Internal").ap()

        whole.enter_context(nc.allow_non_contiguous_dma(reason="small vectors and tables"))

        extremes = dram("extremes", (2, C), F32)
        units_row = dram("units_row", (1, 3, CQ), I32)
        lasts = dram("lasts", (1, NT), F32)
        expert_rows = dram("expert_rows", (SLOTS + P, D), F32)
        y_rows = dram("y_rows", (SLOTS, D), F32)
        z_rows = dram("z_rows", (NT * P, D), F32)
        hid1_rows = dram("hid1_rows", (NT * P, H3), BF16)
        hid2_rows = dram("hid2_rows", (NT * P, H3), BF16)
        x2_rows = dram("x2_rows", (NT * P, D), F32)
        xn2_rows = dram("xn2_rows", (NT * P, 2 * D), F16)
        wd_rows = dram("wd_rows", (FB, P, 2, D), F32)

        ident = sb(whole, "ident", [P, P], F32)
        identb = sb(whole, "identb", [P, P], BF16)
        iota = sb(whole, "iota", [P, P], F32)
        srcT = sb(whole, "srcT", [P, C], I16)
        dstT = sb(whole, "dstT", [P, CX], I16)
        ranges = sb(whole, "ranges", [1, 4, NT], I32)
        dinv = sb(whole, "dinv", [P, NT], F32)
        invdeg = sb(whole, "invdeg", [P, NT], F32)
        hid = sb(whole, "hid", [P, NT, H3], BF16)
        zerob = sb(whole, "zerob", [P, H3], BF16)

        s = {n: sem("a_" + n) for n in (
            "ext_out const cleared src_in dst_in w1_in stats xn xT_ps xT h_ps h_used "
            "dve lists_f lists_ps lists_used lo_hi ol oh hist_used hist "
            "span var std degs degs_std fence span_ps spanr row_ps ranges pool hid1 stored ".split())}
        x_in = [sem(f"a_x_in{k}") for k in range(G)]
        with ExitStack() as ctx:
            src_em = sb(ctx, "src_em", [EP, EB * P], I32)
            dst_em = sb(ctx, "dst_em", [EP, EB * P], I32)
            src_f = sb(ctx, "src_f", [EP, EB * P], F32)
            dst_f = sb(ctx, "dst_f", [EP, EB * P], F32)
            hi_i = sb(ctx, "hi_i", [EP, EB * P], I32)
            hi_f = sb(ctx, "hi_f", [EP, EB, P], F32)
            lohi_i = sb(ctx, "lohi_i", [P, 3, C], I32)
            lo_f = sb(ctx, "lo_f", [P, C], F32)
            hiT_f = sb(ctx, "hiT_f", [P, C], F32)
            mm = sb(ctx, "mm", [EP, 2, EB], F32)
            pres = sb(ctx, "pres", [EP, 3, EB, NT], F32)
            cid = sb(ctx, "cid", [EP, 2, EB], F32)
            span = sb(ctx, "span", [EP, 2, NT], F32)
            spanr = sb(ctx, "spanr", [2 * NT, 1], F32)
            row = sb(ctx, "row", [1, 8, NT], F32)
            rowi = sb(ctx, "rowi", [1, 3, NT], I32)
            w1 = sb(ctx, "w1", [P, DK, H], F32)
            xt = sb(ctx, "xt", [P, G, D], F32)
            st = sb(ctx, "st", [P, G, 6], F32)
            sig = sb(ctx, "sig", [P, 8], F32)
            zeros = sb(ctx, "azeros", [P, NT], BF16)
            var = sb(ctx, "var", [P, G], F32)
            nw = sb(ctx, "nw", [P, G], F32)
            degs = sb(ctx, "degs", [P, NT], F32)
            nwd = sb(ctx, "nwd", [P, NT], F32)
            mv = sb(ctx, "mv", [P, G, 2], F32)
            rs = sb(ctx, "rs", [P, G, 2], F32)
            xT = sb(ctx, "xT", [P, 2, D], F32)
            h1 = sb(ctx, "h1", [P, NT, H], F32)
            r1 = sb(ctx, "r1", [P, 2, NT * H], F32)
            HU = 14
            HG = C // (G * HU)
            ol = sb(ctx, "ol", [P, 2, HU, P], BF16)
            oh = sb(ctx, "oh", [P, 2, HU, NT], BF16)
            pT = [pb(ctx, f"pT{i}", [P, D], F32) for i in range(2)]
            pH = pb(ctx, "pH", [P, 512], F32)
            pD = pb(ctx, "pD", [P, 512], F32)
            pL = [pb(ctx, f"pL{i}", [P, 512], F32) for i in range(2)]
            block = ctx.enter_context(nc.Block())

            @block.sync
            def _(sp):
                sp.dma_start(w1[:], W1.rearrange("(k p) h -> p k h", p=P)).then_inc(s["w1_in"], 16)
                sp.wait_ge(s["cleared"], 2)
                full = (EP - 1) * EB * P
                for lst, em, done in ((src, src_em, "src_in"), (dst, dst_em, "dst_in")):
                    sp.dma_start(em[0:EP - 1, :], lst[0:full].rearrange("(p c) -> p c", p=EP - 1)).then_inc(s[done], 16)
                    sp.dma_start(em[EP - 1:EP, 0:E - full], lst[full:E].rearrange("(p c) -> p c", p=1)).then_inc(s[done], 16)

                def load(i, k, rows=P):
                    sp.dma_start(xt[0:rows, k, :], x[ds((i * G + k) * P, rows), :]).then_inc(x_in[k], 16)

                for k in range(G):
                    load(0, k)
                with sp.Fori(1, G - 1) as i:
                    for k in range(G):
                        sp.wait_ge(s["xT_ps"], (i - 1) * G + (k + 1))
                        load(i, k)
                for k in range(G):
                    sp.wait_ge(s["xT_ps"], (G - 2) * G + k + 1)
                    load(G - 1, k, P if k < G - 1 else LAST)
                sp.wait_ge(s["row_ps"], 1)
                sp.dma_start(extremes.rearrange("m (p b) -> p m b", p=EP), mm[:]).then_inc(s["ext_out"], 16)
                sp.wait_ge(s["ranges"], 1)
                sp.dma_start(lasts, row[0:1, 0, :]).then_inc(s["ext_out"], 16)
                sp.wait_ge(s["ext_out"], 32)
                sp.wait_ge(s["hid1"], 1)
                sp.dma_start(hid1_rows.rearrange("(t p) f -> p t f", p=P), hid[:]).then_inc(s["stored"], 16)
                sp.wait_ge(s["stored"], 16)

            @block.gpsimd
            def _(pool):
                own = Steps(pool, s["pool"])
                own.step(nc.gpsimd.memset(ident[:], 0.0))
                own.step(nc.gpsimd.affine_select(out=ident[:], in_=ident[:], compare_op=ALU.not_equal, fill=1.0,
                                                 base=0, pattern=[[-1, P]], channel_multiplier=1))
                nc.gpsimd.tensor_copy(identb[:], ident[:])
                nc.gpsimd.memset(zerob[:], 0.0)
                nc.gpsimd.memset(zeros[:], 0.0)
                nc.gpsimd.iota(iota[:], [[1, P]], base=0, channel_multiplier=0,
                               allow_small_or_imprecise_dtypes=True)
                nc.gpsimd.iota(cid[:, 0, :], [[1, EB]], base=1, channel_multiplier=EB,
                               allow_small_or_imprecise_dtypes=True)
                nc.gpsimd.iota(cid[:, 1, :], [[-1, EB]], base=1000, channel_multiplier=-EB,
                               allow_small_or_imprecise_dtypes=True)
                nc.gpsimd.memset(dstT[:, C:CX], FAR).then_inc(s["const"], 1)

            @block.vector
            def _(dve):
                own = Steps(dve, s["dve"])
                nc.vector.memset(src_em[:], 0).then_inc(s["cleared"], 1)
                nc.vector.memset(dst_em[:], FAR).then_inc(s["cleared"], 1)
                dve.wait_ge(s["dst_in"], 32)
                nc.vector.tensor_copy(dst_f[:], dst_em[:]).then_inc(s["lists_f"], 1)
                dve.wait_ge(s["src_in"], 32)
                nc.vector.tensor_copy(src_f[:], src_em[:]).then_inc(s["lists_f"], 1)
                own.step(nc.vector.tensor_single_scalar(hi_i[:], dst_em[:], 7, ALU.arith_shift_right))
                own.step(nc.vector.tensor_copy(hi_f[:].rearrange("p a b -> p (a b)"), hi_i[:]))
                own.step(nc.vector.tensor_reduce(mm[:, 0, :], hi_f[:], AX, ALU.min))
                own.step(nc.vector.tensor_reduce(mm[:, 1, :], hi_f[:], AX, ALU.max))
                dve.wait_ge(s["const"], 1)
                full = (EP, EB, NT)
                tiles = bc(iota[0:EP, 0:NT].unsqueeze(1), full)
                own.step(nc.vector.tensor_tensor(pres[:, 0], bc(mm[:, 0, :].unsqueeze(2), full), tiles, ALU.is_le))
                own.step(nc.vector.tensor_tensor(pres[:, 1], bc(mm[:, 1, :].unsqueeze(2), full), tiles, ALU.is_ge))
                own.step(nc.vector.tensor_tensor(pres[:, 2], pres[:, 0], pres[:, 1], ALU.mult))
                for j in range(2):
                    own.step(nc.vector.tensor_tensor(pres[:, 0], pres[:, 2], bc(cid[:, j, :].unsqueeze(2), full), ALU.mult))
                    own.step(nc.vector.tensor_reduce(span[:, j, :], pres[:, 0].rearrange("p e t -> p t e"), AX, ALU.max))
                nc.vector.tensor_copy(pres[:, 1, 0, 0:1], pres[:, 0, 0, 0:1]).then_inc(s["span"], 1)
                for j in range(2 * EB):
                    lst, b = (dstT[:, 0:C], j) if j < EB else (srcT[:, 0:C], j - EB)
                    dve.wait_ge(s["lists_ps"], j + 1)
                    nc.vector.tensor_copy(lst.rearrange("q (p b) -> q b p", b=EB)[:, b, :],
                                          pL[j % 2][:, 0:EP]).then_inc(s["lists_used"], 1)
                dve.wait_ge(s["lists_used"], 2 * EB)
                own.step(nc.vector.tensor_copy(lohi_i[:, 0, :], dstT[:, 0:C]))
                own.step(nc.vector.tensor_single_scalar(lohi_i[:, 1, :], lohi_i[:, 0, :], P - 1, ALU.bitwise_and))
                own.step(nc.vector.tensor_single_scalar(lohi_i[:, 2, :], lohi_i[:, 0, :], 7, ALU.arith_shift_right))
                own.step(nc.vector.tensor_copy(lo_f[:], lohi_i[:, 1, :]))
                nc.vector.tensor_copy(hiT_f[:], lohi_i[:, 2, :]).then_inc(s["lo_hi"], 1)
                dve.wait_ge(s["span_ps"], 1)
                nc.vector.tensor_reduce(spanr[:], pL[0][0:2 * NT, 0:EP], AX, ALU.max).then_inc(s["spanr"], 1)
                dve.wait_ge(s["row_ps"], 1)
                r = [row[0:1, j, :] for j in range(8)]
                own.step(nc.vector.tensor_copy(row[0:1, 0:2, :].rearrange("p a b -> p (a b)"), pL[1][0:1, 0:2 * NT]))
                own.step(nc.vector.tensor_scalar(r[2], r[1], -1.0, 1000.0, ALU.mult, ALU.add))
                own.step(nc.vector.tensor_scalar_min(r[2], r[2], float(C - 1)))
                own.step(nc.vector.tensor_sub(r[3], r[0], r[2]))
                own.step(nc.vector.tensor_scalar(r[3], r[3], 1.0, float(U - 1), ALU.max, ALU.add))
                own.step(nc.vector.tensor_scalar_add(r[4], r[2], float(U + V - 1)))
                own.step(nc.vector.tensor_copy(ranges[0:1, 0, :], r[2]))
                own.step(nc.vector.tensor_copy(rowi[0:1, 0:2, :], row[0:1, 3:5, :]))
                for j, size in ((0, U), (1, V)):
                    own.step(nc.vector.tensor_single_scalar(ranges[0:1, 1 + j, :], rowi[0:1, j, :], size.bit_length() - 1,
                                                            ALU.arith_shift_right))
                own.step(nc.vector.tensor_copy(r[5], ranges[0:1, 1, :]))
                own.step(nc.vector.tensor_copy(r[7], r[5]))
                a, b = 5, 6
                d = 1
                while d < NT:
                    own.step(nc.vector.tensor_copy(r[b], r[a]))
                    own.step(nc.vector.tensor_add(r[b][:, d:NT], r[a][:, d:NT], r[a][:, 0:NT - d]))
                    a, b, d = b, a, 2 * d
                own.step(nc.vector.tensor_sub(r[b], r[a], r[7]))
                own.step(nc.vector.tensor_copy(ranges[0:1, 3, :], r[b]))
                dve.sem_inc(s["ranges"], 1)
                def histogram(i, m):
                    n, h = i * HG + m, m % 2
                    dve.wait_ge(s["hist_used"], n + 1)
                    nc.vector.tensor_tensor(
                        ol[:, h, :, :], bc(iota[:].unsqueeze(1), (P, HU, P)),
                        bc(lo_f[:, ds(n * HU, HU)].unsqueeze(2), (P, HU, P)), ALU.is_equal).then_inc(s["ol"], 1)
                    nc.vector.tensor_tensor(
                        oh[:, h, :, :], bc(iota[:, 0:NT].unsqueeze(1), (P, HU, NT)),
                        bc(hiT_f[:, ds(n * HU, HU)].unsqueeze(2), (P, HU, NT)), ALU.is_equal).then_inc(s["oh"], 1)

                with dve.Fori(0, G) as i:
                    own.body(i, 3 + NEWTON)
                    dve.wait_ge(s["xn"], i * G + G)
                    for k in range(G):
                        dve.wait_ge(x_in[k], (i + 1) * 16)
                        last = nc.vector.bn_stats(st[:, k, :], xt[:, k, :])
                    own.step(last)
                    dve.sem_inc(s["fence"], 1)
                    for k in range(G):
                        last = nc.vector.bn_aggr(mv[:, k, :], st[:, k, :])
                    own.step(last)
                    own.step(nc.vector.tensor_scalar_add(var[:], mv[:, :, 1], EPS))
                    nc.vector.tensor_copy(sig[:, 0:1], var[:, 0:1]).then_inc(s["var"], 1)
                    for m in range(2):
                        histogram(i, m)
                    dve.wait_ge(s["std"], i + 1)
                    newton(nc, own, rs[:, :, 0], var[:], nw[:])
                    nc.vector.scalar_tensor_tensor(rs[:, :, 1], mv[:, :, 0], -1.0, rs[:, :, 0],
                                                   ALU.mult, ALU.mult).then_inc(s["stats"], 1)
                    for m in range(2, HG):
                        histogram(i, m)
                own.end(G)
                dve.wait_ge(s["hist"], 1)
                own.step(nc.vector.tensor_scalar_add(degs[:], pD[:, 0:NT], 1.0))
                nc.vector.tensor_copy(sig[:, 0:1], degs[:, 0:1]).then_inc(s["degs"], 1)
                dve.wait_ge(s["degs_std"], 1)
                newton(nc, own, dinv[:], degs[:], nwd[:])
                own.step(nc.vector.tensor_scalar_max(invdeg[:], pD[:, 0:NT], 1.0))
                own.step(nc.vector.reciprocal(invdeg[:], invdeg[:]))
                dve.wait_ge(s["h_used"], G + 1)
                own.step(nc.vector.tensor_tensor(h1[:], h1[:], bc(dinv[:].unsqueeze(2), (P, NT, H)), ALU.mult))
                split3(nc, own, hid, h1, r1)
                nc.vector.tensor_copy(sig[:, 0:1], r1[:, 0, 0:1]).then_inc(s["hid1"], 1)

            @block.scalar
            def _(act):
                act.sem_inc(s["xn"], G)
                act.sem_inc(s["h_used"], 1)

                def norm(k):
                    nc.scalar.activation(xt[:, k, :], xt[:, k, :], ACT.Identity,
                                         bias=rs[:, k, 1:2], scale=rs[:, k, 0:1]).then_inc(s["xn"], 1)

                with act.Fori(0, G) as i:
                    act.wait_ge(s["var"], i + 1)
                    nc.scalar.activation(rs[:, :, 0], var[:], ACT.Sqrt).then_inc(s["std"], 1)
                    act.wait_ge(s["stats"], i + 1)
                    norm(0)
                    norm(1)
                    for k in range(G):
                        T = i * G + k
                        act.wait_ge(s["xT_ps"], T + 1)
                        act.wait_ge(s["h_ps"], T if k else T + 1)
                        nc.scalar.copy(xT[:, k % 2, :], pT[k % 2][:]).then_inc(s["xT"], 1)
                        if k + 2 < G:
                            norm(k + 2)
                    act.wait_ge(s["h_ps"], i * G + (G + 1))
                    nc.scalar.copy(h1[:, ds(i * G, G), :].rearrange("p a b -> p (a b)"), pH[:, 0:G * H]).then_inc(s["h_used"], 1)
                act.wait_ge(s["degs"], 1)
                nc.scalar.activation(dinv[:], degs[:], ACT.Sqrt).then_inc(s["degs_std"], 1)

            @block.tensor
            def _(pe):
                pe.wait_ge(s["const"], 1)
                pe.sem_inc(s["hist_used"], 2)
                pe.sem_inc(s["h_ps"], 1)
                for j in range(2 * EB):
                    lst, b = (dst_f, j) if j < EB else (src_f, j - EB)
                    pe.wait_ge(s["lists_f"], j // EB + 1)
                    if j >= 2:
                        pe.wait_ge(s["lists_used"], j - 1)
                    nc.tensor.transpose(pL[j % 2][:, 0:EP], lst[:, b * P:(b + 1) * P], ident[0:EP, 0:EP]).then_inc(s["lists_ps"], 1)
                pe.wait_ge(s["span"], 1)
                pe.wait_ge(s["lists_used"], 2 * EB)
                nc.tensor.transpose(pL[0][0:2 * NT, 0:EP], span[:].rearrange("p a b -> p (a b)"),
                                    ident[0:EP, 0:EP]).then_inc(s["span_ps"], 1)
                pe.wait_ge(s["spanr"], 1)
                nc.tensor.transpose(pL[1][0:1, 0:2 * NT], spanr[:], ident[0:2 * NT, 0:2 * NT]).then_inc(s["row_ps"], 1)
                pe.wait_ge(s["w1_in"], 16)
                nc.tensor.matmul(pD[:, 0:NT], identb[:], zeros[:], start=True, stop=False)

                def turn(i, k):
                    pe.wait_ge(s["xn"], i * G + (k + G + 1))
                    for c in range(DK):
                        last = nc.tensor.transpose(pT[k % 2][:, c * P:(c + 1) * P], xt[:, k, c * P:(c + 1) * P], ident[:])
                    last.then_inc(s["xT_ps"], 1)

                def layer1(i, k):
                    if k == 0:
                        pe.wait_ge(s["h_used"], i + 1)
                    pe.wait_ge(s["xT"], i * G + (k + 1))
                    for c in range(DK):
                        last = nc.tensor.matmul(pH[:, k * H:(k + 1) * H], xT[:, k % 2, c * P:(c + 1) * P], w1[:, c, :],
                                                start=(c == 0), stop=(c == DK - 1))
                    last.then_inc(s["h_ps"], 1)

                def histogram(i, m):
                    pe.wait_ge(s["ol"], i * HG + (m + 1))
                    pe.wait_ge(s["oh"], i * HG + (m + 1))
                    for c in range(HU):
                        last = nc.tensor.matmul(pD[:, 0:NT], ol[:, m % 2, c, :], oh[:, m % 2, c, :], start=False, stop=False)
                    last.then_inc(s["hist_used"], 1)

                with pe.Fori(0, G) as i:
                    histogram(i, 0)
                    histogram(i, 1)
                    turn(i, 0)
                    for k in range(G):
                        if k + 1 < G:
                            turn(i, k + 1)
                        layer1(i, k)
                        if k % 2 == 0:
                            histogram(i, 2 + k // 2)
                    for m in range(2 + -(-G // 2), HG):
                        histogram(i, m)
                nc.tensor.matmul(pD[:, 0:NT], identb[:], zeros[:], start=False, stop=True).then_inc(s["hist"], 1)


        ffn = whole.enter_context(ExitStack())
        wgu = [sb(ffn, f"wgu_{n}", [P, 2 * FB, DK, P], F32R) for n in ("hi", "lo")]
        msg = sb(ffn, "msg", [P, CX, H3], BF16)
        onehot = sb(ffn, "onehot", [P, 2, U // 2, P], BF16)
        tiota = sb(ffn, "tiota", [P, P], F32)
        idx = sb(ffn, "idx", [P, 2, V], I32)
        stage = sb(ffn, "stage", [P, 2, V, H3], BF16)
        next_stage()
        s = {n: sem("b_" + n) for n in (
            "tables tables_out zero zeroed ext_in fence fence_sp small_in wq ps hi lo_done dve idx msg onehot used agg agg_used var std hid2 stored "
            "d_wq d_ps d_hi d_lo d_out".split())}
        w_in = [sem(f"b_w_in{j}") for j in range(2)]
        wd_in = sem("b_wd_in")
        landed = [[sem(f"b_landed{h}_{k}") for k in range(V)] for h in range(2)]
        with ExitStack() as ctx:
            wraw = sb(ctx, "wraw", [P, 2, DK, P], F32)
            wq = sb(ctx, "wq", [P, 2, 2, DK, P], F32)
            wdraw = sb(ctx, "wdraw", [P, FB, P], F32)
            wdq = sb(ctx, "wdq", [P, 2, FB, P], F32)
            wdT = sb(ctx, "wdT", [P, 2, FB, P], F32R)
            sc = sb(ctx, "sc", [P, 3, FB], F32)
            vec = sb(ctx, "vec", [P, 3, H], F32)
            agg = sb(ctx, "agg", [P, NT, H], F32)
            sq = sb(ctx, "sq", [P, NT, H], F32)
            mean = sb(ctx, "mean", [P, NT], F32)
            var = sb(ctx, "bvar", [P, NT], F32)
            rstd = sb(ctx, "rstd", [P, NT], F32)
            nw = sb(ctx, "bnw", [P, NT], F32)
            rest = sb(ctx, "rest", [P, 2, NT * H], F32)
            sig = sb(ctx, "bsig", [P, 1], F32)
            zeros = sb(ctx, "zeros", [P, D], F32)
            units = sb(ctx, "units", [1, 3, CQ], I32)
            ext = sb(ctx, "ext", [1, 2, C], F32)
            ur = sb(ctx, "ur", [1, 5, CQ], F32)
            tr = sb(ctx, "tr", [1, 6, NT], F32)
            ti = sb(ctx, "ti", [1, 2, NT], I32)
            pW = [pb(ctx, f"pW{i}", [P, DK, P], F32) for i in range(2)]
            pA = pb(ctx, "pA", [P, 512], F32)
            acc = pA[:, 0:H3]
            block = ctx.enter_context(nc.Block())

            @block.sync
            def _(sp):
                sp.wait_ge(s["zero"], 1)
                with sp.Fori(0, (SLOTS + P) // P) as i:
                    sp.dma_start(expert_rows[ds(i * P, P), :], zeros[:]).then_inc(s["zeroed"], 16)
                rest_rows = (SLOTS + P) % P
                sp.dma_start(expert_rows[SLOTS + P - rest_rows:SLOTS + P, :], zeros[0:rest_rows, :]).then_inc(s["zeroed"], 16)
                sp.dma_start(ext[0:1, :, :], extremes.rearrange("(a m) c -> a m c", a=1)).then_inc(s["ext_in"], 16)
                sp.dma_start(tr[0:1, 0, :], lasts).then_inc(s["ext_in"], 16)
                for j, v in enumerate((b1, gamma, beta)):
                    sp.dma_start(vec[:, j, :], v.partition_broadcast(P)).then_inc(s["small_in"], 16)
                with sp.Fori(0, FB) as i:
                    for j, w in enumerate((w_gate, w_up)):
                        wait_alone(sp, s["wq"], i * 2 + (j + 1), s["fence_sp"])
                        sp.dma_start(wraw[:, j, :, :].rearrange("p a b -> p (a b)"), w[ds(i * P, P), :]).then_inc(w_in[j], 16)
                with sp.Fori(0, DK) as i:
                    wait_alone(sp, s["d_wq"], i + 1, s["fence_sp"])
                    sp.dma_start(wdraw[:].rearrange("p a b -> p (a b)"), w_down[ds(i * P, P), :]).then_inc(wd_in, 16)
                    wait_alone(sp, s["d_lo"], (i + 1) * 3 + 1, s["fence_sp"])
                    for j in range(2):
                        sp.dma_start(wd_rows[:, :, j, ds(i * P, P)].rearrange("b f o -> f b o"),
                                     wdT[:, j, :, :].bitcast(F32)).then_inc(s["d_out"], 16)
                    wait_alone(sp, s["d_out"], (i + 1) * 32, s["fence_sp"])
                sp.wait_ge(s["tables"], 1)
                sp.dma_start(units_row, units[:]).then_inc(s["tables_out"], 16)
                sp.wait_ge(s["tables_out"], 16)
                sp.wait_ge(s["zeroed"], ((SLOTS + P) // P + 1) * 16)
                sp.wait_ge(s["hid2"], 1)
                sp.dma_start(hid2_rows.rearrange("(t p) f -> p t f", p=P), hid[:]).then_inc(s["stored"], 16)
                sp.wait_ge(s["stored"], 16)

            @block.gpsimd
            def _(pool):
                nc.gpsimd.memset(msg[:, C:CX, :], 0.0)
                gather_units(nc, pool, hid1_rows, srcT, idx, stage, msg, landed, s["idx"], s["msg"], s["fence"])
                pool.sem_inc(s["msg"], U // V)

            @block.vector
            def _(dve):
                own = Steps(dve, s["dve"])
                own.step(nc.vector.memset(zeros[:], 0.0))
                dve.sem_inc(s["zero"], 1)
                dve.sem_inc(s["wq"], 2)
                dve.sem_inc(s["d_wq"], 1)

                def quantize(w, q, n):
                    full = (P, n, P)
                    scale, over, under = (sc[:, j, 0:n] for j in range(3))
                    own.step(nc.vector.tensor_reduce(scale, w, AX, ALU.add, apply_absolute_value=True))
                    own.step(nc.vector.tensor_scalar(scale, scale, 1.0 / P, EPS, ALU.mult, ALU.add))
                    own.step(nc.vector.tensor_scalar_mul(over, scale, 0.5))
                    own.step(nc.vector.tensor_scalar_mul(under, scale, -0.5))
                    own.step(nc.vector.tensor_tensor(q[0], w, bc(over.unsqueeze(2), full), ALU.is_gt))
                    own.step(nc.vector.tensor_tensor(q[1], w, bc(under.unsqueeze(2), full), ALU.is_lt))
                    own.step(nc.vector.tensor_tensor(q[0], q[0], q[1], ALU.subtract))
                    return nc.vector.tensor_tensor(q[0], q[0], bc(scale.unsqueeze(2), full), ALU.mult)

                with dve.Fori(0, FB) as i:
                    own.body(i, 14)
                    for j in range(2):
                        dve.wait_ge(w_in[j], (i + 1) * 16)
                        quantize(wraw[:, j], [wq[:, j, 0], wq[:, j, 1]], DK).then_inc(s["wq"], 1)
                        dve.wait_ge(s["wq"], i * 2 + (j + 3))
                    for j in range(2):
                        dve.wait_ge(s["hi"], i * 2 + (j + 1))
                        at = wgu[1][:, ds(i + j * FB, 1)].rearrange("p a b c -> p (a b) c")
                        hi = wgu[0][:, ds(i + j * FB, 1)].rearrange("p a b c -> p (a b) c").bitcast(F32)
                        nc.vector.tensor_tensor(at, pW[j][:], hi, ALU.subtract).then_inc(s["lo_done"], 1)
                own.end(FB)
                with dve.Fori(0, DK) as i:
                    own.body(i, 7)
                    dve.wait_ge(wd_in, (i + 1) * 16)
                    quantize(wdraw[:], [wdq[:, 0], wdq[:, 1]], FB).then_inc(s["d_wq"], 1)
                    dve.wait_ge(s["d_wq"], i + 2)
                    for m in range(3):
                        g = slice(4 * m, min(4 * m + 4, FB))
                        dve.wait_ge(s["d_hi"], i * 3 + (m + 1))
                        nc.vector.tensor_tensor(wdT[:, 1, g, :], pW[m % 2][:, 0:g.stop - g.start, :],
                                                wdT[:, 0, g, :].bitcast(F32), ALU.subtract).then_inc(s["d_lo"], 1)
                own.end(DK)
                dve.wait_ge(s["ext_in"], 32)
                u = [ur[0:1, j, :] for j in range(5)]
                own.step(nc.vector.memset(ur[:], float(NT - 1)))
                own.step(nc.vector.tensor_reduce(u[0][:, 0:CQ], ext[0:1, 0, :].rearrange("a (u q) -> a u q", q=Q), AX, ALU.min))
                own.step(nc.vector.tensor_reduce(u[1][:, 0:CQ], ext[0:1, 1, :].rearrange("a (u q) -> a u q", q=Q), AX, ALU.max))
                own.step(nc.vector.tensor_scalar_min(ur[0:1, 0:2, :], ur[0:1, 0:2, :], float(NT - 1)))
                own.step(nc.vector.tensor_sub(u[1], u[1], u[0]))
                own.step(nc.vector.tensor_scalar_add(u[1], u[1], 1.0))
                own.step(nc.vector.tensor_copy(units[0:1, 0:2, :], ur[0:1, 0:2, :]))
                own.step(nc.vector.tensor_copy(u[2], u[1]))
                a, b = scan(nc, own, u, 2, 3, CQ, ALU.add)
                own.step(nc.vector.tensor_sub(u[b], u[a], u[1]))
                own.step(nc.vector.tensor_copy(units[0:1, 2, :], u[b]))
                dve.sem_inc(s["tables"], 1)
                own.step(nc.vector.tensor_copy(tiota[:], iota[:]))
                with dve.Fori(0, NT) as t:
                    own.body(t, 1)
                    build_onehots(nc, dve, t, ranges, dstT, tiota, onehot, s["onehot"], s["used"])
                    dve.wait_ge(s["agg"], t + 1)
                    own.step(nc.vector.tensor_scalar_add(tiota[:], tiota[:], float(P)))
                    nc.vector.tensor_reduce(agg[:, ds(t, 1), :].rearrange("p a b -> p (a b)"),
                                            acc.rearrange("p (a f) -> p f a", f=H), AX, ALU.add).then_inc(s["agg_used"], 1)
                own.end(NT)
                dve.wait_ge(s["agg_used"], NT + 1)
                dve.wait_ge(s["small_in"], 48)
                full = (P, NT, H)
                b1_, gamma_, beta_ = (bc(vec[:, j, :].unsqueeze(1), full) for j in range(3))

                def tt(o, a, b, op):
                    own.step(nc.vector.tensor_tensor(o, a, b, op))

                per_node = lambda v: bc(v[:].unsqueeze(2), full)
                tt(agg[:], agg[:], per_node(dinv), ALU.mult)
                tt(agg[:], agg[:], b1_, ALU.add)
                own.step(nc.vector.tensor_reduce(mean[:], agg[:], AX, ALU.add))
                own.step(nc.vector.tensor_scalar_mul(mean[:], mean[:], 1.0 / H))
                tt(agg[:], agg[:], per_node(mean), ALU.subtract)
                tt(sq[:], agg[:], agg[:], ALU.mult)
                own.step(nc.vector.tensor_reduce(var[:], sq[:], AX, ALU.add))
                own.step(nc.vector.tensor_scalar(var[:], var[:], 1.0 / H, EPS, ALU.mult, ALU.add))
                nc.vector.memset(sig[:], 0.0).then_inc(s["var"], 1)
                dve.wait_ge(s["std"], 1)
                newton(nc, own, rstd[:], var[:], nw[:])
                tt(agg[:], agg[:], per_node(rstd), ALU.mult)
                tt(agg[:], agg[:], gamma_, ALU.mult)
                tt(agg[:], agg[:], beta_, ALU.add)
                own.step(nc.vector.tensor_scalar_max(agg[:], agg[:], 0.0))
                tt(agg[:], agg[:], per_node(dinv), ALU.mult)
                split3(nc, own, hid, agg, rest)
                nc.vector.memset(sig[:], 0.0).then_inc(s["hid2"], 1)

            @block.scalar
            def _(act):
                with act.Fori(0, FB) as i:
                    for j in range(2):
                        act.wait_ge(s["ps"], i * 2 + (j + 1))
                        nc.scalar.copy(wgu[0][:, ds(i + j * FB, 1)].rearrange("p a b c -> p (a b) c"), pW[j][:]).then_inc(s["hi"], 1)
                with act.Fori(0, DK) as i:
                    act.wait_ge(s["d_wq"], i + 2)
                    for m in range(3):
                        g = slice(4 * m, min(4 * m + 4, FB))
                        act.wait_ge(s["d_ps"], i * 3 + (m + 1))
                        nc.scalar.copy(wdT[:, 0, g, :], pW[m % 2][:, 0:g.stop - g.start, :]).then_inc(s["d_hi"], 1)
                act.wait_ge(s["var"], 1)
                nc.scalar.activation(rstd[:], var[:], ACT.Sqrt).then_inc(s["std"], 1)

            @block.tensor
            def _(pe):
                pe.sem_inc(s["used"], 2)
                pe.sem_inc(s["agg_used"], 1)
                pe.sem_inc(s["lo_done"], 2)
                with pe.Fori(0, FB) as i:
                    for j in range(2):
                        pe.wait_ge(s["wq"], i * 2 + (j + 3))
                        pe.wait_ge(s["lo_done"], i * 2 + (j + 1))
                        for k in range(DK):
                            last = nc.tensor.transpose(pW[j][:, k, :], wq[:, j, 0, k, :], ident[:])
                        last.then_inc(s["ps"], 1)
                pe.wait_ge(s["lo_done"], 2 * FB + 2)
                pe.sem_inc(s["d_lo"], 1)
                with pe.Fori(0, DK) as i:
                    pe.wait_ge(s["d_wq"], i + 2)
                    for m in range(3):
                        pe.wait_ge(s["d_lo"], i * 3 + (1 if m < 2 else 2))
                        for k in range(4 * m, min(4 * m + 4, FB)):
                            last = nc.tensor.transpose(pW[m % 2][:, k - 4 * m, :], wdq[:, 0, k, :], ident[:])
                        last.then_inc(s["d_ps"], 1)
                with pe.Fori(0, NT) as t:
                    pe.wait_ge(s["agg_used"], t + 1)
                    sum_messages(nc, pe, t, ranges, hid, msg, identb, zerob, acc, onehot,
                                 s["onehot"], s["used"], s["msg"]).then_inc(s["agg"], 1)


        next_stage()
        s = {n: sem("c_" + n) for n in (
            "small_in nv_clear idx msg fence fence_sp fence_pe fence_dve onehot used agg agg_used aggd aggT_ps aggT conv relu "
            "x1 var std rs xn xT_ps xT_hi xT_lo gate_ps up_ps silu hmul h_hi h_lo down x2 var2 std2 rs2 "
            "xn2 row_hi row_lo row_stored dve".split())}
        landed = [[sem(f"c_landed{h}_{k}") for k in range(V)] for h in range(2)]
        x_in = [sem(f"c_x_in{k}") for k in range(G)]
        x2_out = [sem(f"c_x2_out{k}") for k in range(G)]
        row_out = sem("c_row_out")
        wd_in = [sem(f"c_wd_in{j}") for j in range(2)]
        with ExitStack() as ctx:
            xr = sb(ctx, "xr", [P, G, D], F32)
            xn = sb(ctx, "xn", [P, 2, D], F32)
            xT = [sb(ctx, f"xT{g}", [P, 2, DK, len(ks) * P], F32R) for g, ks in enumerate(GROUPS)]
            hT = sb(ctx, "hT", [P, 2, 2, 4 * P], F32R)
            sil = sb(ctx, "sil", [P, 4 * P], F32)
            wd = sb(ctx, "wd", [P, 2, 2, D], F32R)
            w2b = sb(ctx, "w2b", [H + 1, D], F32)
            small = sb(ctx, "small", [P, NT + 4 * (H + 1) + H + 4 * 16], F32)
            taken = [0]

            def part(name, *shape):
                n = 1
                for size in shape:
                    n *= size
                at = small[:, taken[0]:taken[0] + n]
                taken[0] += n
                names = "abc"[:len(shape)]
                return at.rearrange(f"p ({' '.join(names)}) -> p {' '.join(names)}", **dict(zip(names, shape))) if len(shape) > 1 else at

            nv = part("node_vec", NT)
            pair = sb(ctx, "pair", [P, 2, D], F16)
            sums8 = part("sums", H)
            aggd = part("their rows and a 1", 4, H + 1)
            aggT = sb(ctx, "aggT", [H + 1, P], F32)
            st = part("statistics", 4, 6)
            mv = part("mean and variance", 2, 4, 2)
            var = part("variance", 2, 4)
            rs = part("scale and bias", 2, 4, 2)
            acc4 = [pb(ctx, f"acc{j}", [P, D], F32) for j in range(4)]
            pG = pb(ctx, "pG", [P, 4 * P], F32)
            pU = pb(ctx, "pU", [P, 4 * P], F32)
            pA = pb(ctx, "pAc", [P, 512], F32)
            pB = pb(ctx, "pB", [P, DK, P], F32)
            pB_flat = pB[:].rearrange("p a b -> p (a b)")
            acc = pA[:, 0:H3]
            pAT = pA[0:H + 1, 0:P]
            block = ctx.enter_context(nc.Block())

            def steps_before(i, g, f):
                return i * (2 * FB) + (g * FB + f)

            @block.gpsimd
            def _(pool):
                gather_units(nc, pool, hid2_rows, srcT, idx, stage, msg, landed, s["idx"], s["msg"], s["fence"])
                pool.sem_inc(s["msg"], U // V)

            @block.sync
            def _(sp):
                def load_x(i, k):
                    last = isinstance(i, int) and i * G + k == NT - 1
                    rows = LAST if last else P
                    sp.dma_start(xr[0:rows, k, :], x[ds((i * G + k) * P, rows), :]).then_inc(x_in[k], 16)

                sp.dma_start(w2b[0:H, :], W2).then_inc(s["small_in"], 16)
                sp.dma_start(w2b[H:H + 1, :], b2.rearrange("(a n) -> a n", a=1)).then_inc(s["small_in"], 16)
                full = (NT - 1) * P
                sp.wait_ge(s["nv_clear"], 1)
                sp.dma_start(nv[:, 0:NT - 1], node_vec[0:full, :].rearrange("(t p) a -> p (t a)", p=P)).then_inc(s["small_in"], 16)
                sp.dma_start(nv[0:LAST, NT - 1:NT], node_vec[full:N, :]).then_inc(s["small_in"], 16)
                for k in range(G):
                    load_x(0, k)

                def gate(i, g, f):
                    step, slot = steps_before(i, g, f), (g * FB + f) % 2
                    wait_alone(sp, s["down"], step + 1, s["fence_sp"])
                    sp.dma_start(wd[:, slot, :, :].bitcast(F32), wd_rows[f]).then_inc(wd_in[slot], 16)

                def rows(i, k, j):
                    T = i * G + k
                    wait_alone(sp, s["x2"], T + 2, s["fence_sp"])
                    sp.dma_start(x2_rows[ds(T * P, P), :], xr[:, k, :]).then_inc(x2_out[k], 16)
                    wait_alone(sp, s["row_lo"], T + 2, s["fence_sp"])
                    sp.dma_start(xn2_rows[ds(T * P, P), :], pair[:].rearrange("p a b -> p (a b)")).then_inc(row_out, 16)
                    wait_alone(sp, row_out, T * 16 + 16, s["fence_sp"])
                    sp.sem_inc(s["row_stored"], 1)
                    if not isinstance(i, int) or i < G - 1:
                        wait_alone(sp, x2_out[k], (i + 1) * 16, s["fence_sp"])
                        load_x(i + 1, k)

                groups(sp.Fori, Part(gate=gate, rows=rows))
                for k in range(G):
                    sp.wait_ge(x2_out[k], G * 16)

            @block.tensor
            def _(pe):
                pe.sem_inc(s["used"], 2)
                for n in ("agg_used", "silu", "hmul", "xT_lo"):
                    pe.sem_inc(s[n], 1)
                pe.sem_inc(s["down"], 2)
                pe.wait_ge(s["small_in"], 64)

                def sums(i, k, j):
                    T = i * G + k
                    wait_alone(pe, s["agg_used"], T + 1, s["fence_pe"])
                    if j == 0 and not (isinstance(i, int) and i == 0 and k == 0):
                        wait_alone(pe, s["aggT"], T, s["fence_pe"])
                    sum_messages(nc, pe, T, ranges, hid, msg, identb, zerob, acc, onehot,
                                 s["onehot"], s["used"], s["msg"]).then_inc(s["agg"], 1)

                def agg_turn(i, k, j):
                    T, g = i * G + k, int(k >= 4)
                    if j == 0:
                        wait_alone(pe, s["aggd"], i * G + (GROUPS[g][-1] + 1), s["fence_pe"])
                    else:
                        wait_alone(pe, s["aggT"], T, s["fence_pe"])
                    nc.tensor.transpose(pAT, aggd[:, j, :], ident[:]).then_inc(s["aggT_ps"], 1)

                def layer1(i, k, j):
                    T = i * G + k
                    wait_alone(pe, s["relu"] if j else s["xT_lo"], T if j else T + 1, s["fence_pe"])
                    wait_alone(pe, s["aggT"], T + 1, s["fence_pe"])
                    nc.tensor.matmul(pB_flat, aggT[:], w2b[:], start=True, stop=True).then_inc(s["conv"], 1)

                def turn(i, k, j):
                    T = i * G + k
                    wait_alone(pe, s["xn"], T + 1, s["fence_pe"])
                    wait_alone(pe, s["xT_lo"], T + 1, s["fence_pe"])
                    for c in range(DK):
                        last = nc.tensor.transpose(pB[:, c, :], xn[:, j % 2, c * P:(c + 1) * P], ident[:])
                    last.then_inc(s["xT_ps"], 1)

                def hidden(ps, i, g, f, which):
                    hi, lo = (w[:, which * FB + f] for w in wgu)
                    x_hi, x_lo = xT[g][:, 0], xT[g][:, 1]
                    n = len(GROUPS[g]) * P
                    terms = [(w, v, c) for c in range(DK) for w, v in ((hi, x_hi), (hi, x_lo), (lo, x_hi))]
                    for m, (w, v, c) in enumerate(terms):
                        last = nc.tensor.matmul(ps[:, 0:n], w[:, c, :], v[:, c, :], start=(m == 0), stop=(m == len(terms) - 1))
                    return last

                def gate(i, g, f):
                    if f == 0:
                        wait_alone(pe, s["xT_lo"], i * G + (GROUPS[g][-1] + 2), s["fence_pe"])
                    wait_alone(pe, s["silu"], steps_before(i, g, f) + 1, s["fence_pe"])
                    hidden(pG, i, g, f, 0).then_inc(s["gate_ps"], 1)

                def up(i, g, f):
                    wait_alone(pe, s["hmul"], steps_before(i, g, f) + 1, s["fence_pe"])
                    hidden(pU, i, g, f, 1).then_inc(s["up_ps"], 1)

                def down(i, g, f):
                    step = steps_before(i, g, f)
                    slot = (g * FB + f) % 2
                    if f == 0:
                        wait_alone(pe, s["x2"], i * G + GROUPS[g][0] + 1, s["fence_pe"])
                    wait_alone(pe, wd_in[slot], (i * FB + ((g * FB + f) // 2 + 1)) * 16, s["fence_pe"])
                    wait_alone(pe, s["h_lo"], step + 2, s["fence_pe"])
                    for j in range(len(GROUPS[g])):
                        h_hi, h_lo = (hT[:, slot, m, j * P:(j + 1) * P] for m in range(2))
                        for m, (h, w) in enumerate(((h_hi, 0), (h_hi, 1), (h_lo, 0))):
                            last = nc.tensor.matmul(acc4[j][:], h, wd[:, slot, w, :], start=(f == 0 and m == 0),
                                                    stop=(f == FB - 1 and m == 2))
                    last.then_inc(s["down"], 1)

                groups(pe.Fori, Part(sums=sums, agg_turn=agg_turn, layer1=layer1, turn=turn, gate=gate, up=up, down=down))

            @block.scalar
            def _(act):
                act.sem_inc(s["h_lo"], 1)
                act.sem_inc(s["x2"], 1)
                act.sem_inc(s["row_stored"], 1)
                act.sem_inc(s["row_lo"], 1)

                def agg_turn(i, k, j):
                    T = i * G + k
                    act.wait_ge(s["aggT_ps"], T + 1)
                    nc.scalar.copy(aggT[:], pAT).then_inc(s["aggT"], 1)

                def layer1(i, k, j):
                    T = i * G + k
                    act.wait_ge(s["conv"], T + 1)
                    if j >= 2:
                        act.wait_ge(s["x1"], T - 1)
                    elif not (isinstance(i, int) and i == 0 and k < 4):
                        act.wait_ge(s["row_lo"], T - j - (2 if k < 4 else 3))
                    nc.scalar.activation(xn[:, j % 2, :], pB_flat, ACT.Relu).then_inc(s["relu"], 1)

                def scale(i, g):
                    n = len(GROUPS[g])
                    act.wait_ge(s["var"], i * 2 + (g + 1))
                    nc.scalar.activation(rs[:, 0, 0:n, 0], var[:, 0, 0:n], ACT.Sqrt).then_inc(s["std"], 1)

                def norm(i, k, j):
                    T, g = i * G + k, int(k >= 4)
                    act.wait_ge(s["rs"], i * 2 + (g + 1))
                    if j >= 2:
                        act.wait_ge(s["xT_ps"], T - 1)
                    nc.scalar.activation(xn[:, j % 2, :], xr[:, k, :], ACT.Identity, bias=rs[:, 0, j, 1:2],
                                         scale=rs[:, 0, j, 0:1]).then_inc(s["xn"], 1)

                def turn(i, k, j):
                    T, g = i * G + k, int(k >= 4)
                    act.wait_ge(s["xT_ps"], T + 1)
                    nc.scalar.copy(xT[g][:, 0, :, j * P:(j + 1) * P], pB[:]).then_inc(s["xT_hi"], 1)

                def gate(i, g, f):
                    step, n = steps_before(i, g, f), len(GROUPS[g]) * P
                    act.wait_ge(s["h_lo"], step + 1)
                    act.wait_ge(s["gate_ps"], step + 1)
                    nc.scalar.activation(sil[:, 0:n], pG[:, 0:n], ACT.Silu).then_inc(s["silu"], 1)

                def up(i, g, f):
                    step, n, slot = steps_before(i, g, f), len(GROUPS[g]) * P, (g * FB + f) % 2
                    act.wait_ge(s["hmul"], step + 2)
                    act.wait_ge(s["down"], step + 1)
                    nc.scalar.copy(hT[:, slot, 0, 0:n], sil[:, 0:n]).then_inc(s["h_hi"], 1)

                def scale_rows(i, g):
                    n = len(GROUPS[g])
                    act.wait_ge(s["var2"], i * 2 + (g + 1))
                    nc.scalar.activation(rs[:, 1, 0:n, 0], var[:, 1, 0:n], ACT.Sqrt).then_inc(s["std2"], 1)

                def rows(i, k, j):
                    T, g = i * G + k, int(k >= 4)
                    act.wait_ge(s["rs2"], i * 2 + (g + 1))
                    act.wait_ge(s["row_lo"], T + 1)
                    act.wait_ge(s["row_stored"], T + 1)
                    nc.scalar.activation(xn[:, j % 2, :], xr[:, k, :], ACT.Identity, bias=rs[:, 1, j, 1:2],
                                         scale=rs[:, 1, j, 0:1]).then_inc(s["xn2"], 1)
                    act.wait_ge(s["xn2"], T + 1)
                    nc.scalar.copy(pair[:, 0, :], xn[:, j % 2, :]).then_inc(s["row_hi"], 1)

                groups(act.Fori, Part(agg_turn=agg_turn, layer1=layer1, scale=scale, norm=norm, turn=turn, gate=gate, up=up,
                                      scale_rows=scale_rows, rows=rows))

            @block.vector
            def _(dve):
                own = Steps(dve, s["dve"])
                own.step(nc.vector.tensor_copy(tiota[:], iota[:]))
                own.step(nc.vector.memset(aggd[:], 1.0))
                nc.vector.memset(nv[:], 0.0).then_inc(s["nv_clear"], 1)

                def build(i, k, j):
                    build_onehots(nc, dve, i * G + k, ranges, dstT, tiota, onehot, s["onehot"], s["used"])

                def sums(i, k, j):
                    T = i * G + k
                    dve.wait_ge(s["agg"], T + 1)
                    own.step(nc.vector.tensor_scalar_add(tiota[:], tiota[:], float(P)))
                    own.step(nc.vector.tensor_reduce(sums8[:], acc.rearrange("p (a f) -> p f a", f=H), AX, ALU.add))
                    dve.sem_inc(s["agg_used"], 1)
                    nc.vector.tensor_scalar(aggd[:, j, 0:H], sums8[:], dinv[:, ds(T, 1)], None, ALU.mult).then_inc(s["aggd"], 1)
                    dve.wait_ge(s["aggd"], T + 1)

                def layer1(i, k, j):
                    T = i * G + k
                    if isinstance(i, int) and i == 0:
                        dve.wait_ge(s["small_in"], 64)
                    dve.wait_ge(s["relu"], T + 1)
                    dve.wait_ge(x_in[k], (i + 1) * 16)
                    nc.vector.scalar_tensor_tensor(xr[:, k, :], xn[:, j % 2, :], nv[:, ds(T, 1)], xr[:, k, :],
                                                   ALU.mult, ALU.add).then_inc(s["x1"], 1)

                def stats_of(g, m, ready):
                    ks = GROUPS[g]
                    for j, k in enumerate(ks):
                        last = nc.vector.bn_stats(st[:, j, :], xr[:, k, :])
                    own.step(last)
                    dve.sem_inc(s["fence_dve"], 1)
                    for j, k in enumerate(ks):
                        last = nc.vector.bn_aggr(mv[:, m, j, :], st[:, j, :])
                    own.step(last)
                    own.step(nc.vector.tensor_scalar_add(var[:, m, 0:len(ks)], mv[:, m, 0:len(ks), 1], EPS))
                    dve.sem_inc(ready, 1)

                def scales_of(g, m, done):
                    n = len(GROUPS[g])
                    newton(nc, own, rs[:, m, 0:n, 0], var[:, m, 0:n], sums8[:, 0:n])
                    own.step(nc.vector.scalar_tensor_tensor(rs[:, m, 0:n, 1], mv[:, m, 0:n, 0], -1.0, rs[:, m, 0:n, 0],
                                                            ALU.mult, ALU.mult))
                    dve.sem_inc(done, 1)

                def stats(i, g):
                    dve.wait_ge(s["x1"], i * G + (GROUPS[g][-1] + 1))
                    dve.wait_ge(s["xT_lo"], i * G + (GROUPS[g][0] + 1))
                    stats_of(g, 0, s["var"])

                def scale(i, g):
                    dve.wait_ge(s["std"], i * 2 + (g + 1))
                    scales_of(g, 0, s["rs"])

                def turn(i, k, j):
                    T, g = i * G + k, int(k >= 4)
                    dve.wait_ge(s["xT_hi"], T + 1)
                    nc.vector.tensor_tensor(xT[g][:, 1, :, j * P:(j + 1) * P], pB[:],
                                            xT[g][:, 0, :, j * P:(j + 1) * P].bitcast(F32), ALU.subtract).then_inc(s["xT_lo"], 1)

                def up(i, g, f):
                    step, n, slot = steps_before(i, g, f), len(GROUPS[g]) * P, (g * FB + f) % 2
                    dve.wait_ge(s["silu"], step + 2)
                    dve.wait_ge(s["up_ps"], step + 1)
                    nc.vector.tensor_tensor(sil[:, 0:n], pU[:, 0:n], sil[:, 0:n], ALU.mult).then_inc(s["hmul"], 1)
                    dve.wait_ge(s["hmul"], step + 2)
                    dve.wait_ge(s["h_hi"], step + 1)
                    nc.vector.tensor_tensor(hT[:, slot, 1, 0:n], sil[:, 0:n], hT[:, slot, 0, 0:n].bitcast(F32),
                                            ALU.subtract).then_inc(s["h_lo"], 1)

                def residual(i, g):
                    dve.wait_ge(s["down"], steps_before(i, g, FB) + 2)
                    for j, k in enumerate(GROUPS[g]):
                        last = nc.vector.tensor_tensor(xr[:, k, :], xr[:, k, :], acc4[j][:], ALU.add).then_inc(s["x2"], 1)
                    dve.wait_ge(s["x2"], i * G + (GROUPS[g][-1] + 2))
                    stats_of(g, 1, s["var2"])

                def scale_rows(i, g):
                    dve.wait_ge(s["std2"], i * 2 + (g + 1))
                    scales_of(g, 1, s["rs2"])

                def rows(i, k, j):
                    T = i * G + k
                    dve.wait_ge(s["row_hi"], T + 1)
                    nc.vector.tensor_tensor(pair[:, 1, :], xn[:, j % 2, :], pair[:, 0, :], ALU.subtract).then_inc(s["row_lo"], 1)

                groups(dve.Fori, Part(build=build, sums=sums, layer1=layer1, stats=stats, scale=scale, turn=turn, up=up,
                                      residual=residual, scale_rows=scale_rows, rows=rows,
                                      enter=lambda i: own.body(i, 2 * (3 + 6) * 2 + 2 * G, 1),
                                      leave=lambda: own.end(G - 2)))

        ffn.close()

        next_stage()
        s = {n: sem("d_" + n) for n in (
            "tables_in w_in small_in idx fence fence_sp fence_pe fence_dve fence_act rows_ready rows_used oh_ready mm_done added loaded loads "
            "const wT_ps wT scaled aT_ps aT conv x3 var std rs xf xT_ps xT logits lg_done lg expd onehot cum placed "
            "z normed scatter scattered stores stored dve pool".split())}
        landed = [[sem(f"d_landed{h}_{k}") for k in range(Q)] for h in range(4)]
        route = whole.enter_context(ExitStack())
        gidx = sb(route, "gidx", [P, NT], I32)
        pkeep = sb(route, "pkeep", [P, NT], F32)
        with ExitStack() as ctx:
            agg = sb(ctx, "agg3", [P, NT + 1, D], F32)
            rows = sb(ctx, "rows", [P, 4, Q, 2 * D], F16)
            units = sb(ctx, "units3", [1, 3, CQ], I32)
            idx = sb(ctx, "idx3", [P, 4, Q], I32)
            oh = sb(ctx, "oh3", [P, 2, Q, P], F16)
            iotah = sb(ctx, "iotah", [P, P], F16)
            bases = sb(ctx, "bases", [P, NT], F32)
            dstF = sb(ctx, "dstF", [P, C], F32)
            zeroh = sb(ctx, "zeroh", [P, D], F16)
            wg = sb(ctx, "wg", [P, DK, D], F32)
            wgT = sb(ctx, "wgT", [P, DK, D], F32)
            bgb = sb(ctx, "bgb", [P, D], F32)
            alp = sb(ctx, "alp", [P, 1], F32)
            sw = sb(ctx, "sw", [NX, D], F32)
            swT = sb(ctx, "swT", [P, DK, NX], F32)
            swb = sb(ctx, "swb", [P, NX], F32)
            tri = sb(ctx, "tri", [P, 2, P], BF16)
            trash = sb(ctx, "trash", [P, 1], F32)
            scaled = wg[:, 0:2, :]
            aT = sb(ctx, "aT", [P, 2, DK, P], F32)
            xf = sb(ctx, "xf", [P, 2, D], F32)
            xfT = sb(ctx, "xfT", [P, 2, DK, P], F32)
            zb = sb(ctx, "zb", [P, 2, D], F32)
            x2l = sb(ctx, "x2l", [P, 3, D], F32)
            pl = sb(ctx, "pl", [P, 3, 2 * D], F16)
            res = sb(ctx, "res", [P, D], F32)
            st = sb(ctx, "dst", [P, G, 6], F32)
            mv = sb(ctx, "dmv", [P, G, 2], F32)
            var = sb(ctx, "dvar", [P, G], F32)
            rs = sb(ctx, "drs", [P, 2, G], F32)
            nw = sb(ctx, "dnw", [P, G], F32)
            lg = sb(ctx, "lg", [P, G, NX], F32)
            ex = sb(ctx, "ex", [P, G, NX], F32)
            other = sb(ctx, "other", [P, G, NX], F32)
            top = sb(ctx, "top", [P, G], F32)
            rt = sb(ctx, "rt", [P, G], F32)
            oh16 = sb(ctx, "oh16", [P, G, NX], F32)
            oh16b = sb(ctx, "oh16b", [P, G, NX], BF16)
            base = sb(ctx, "base", [P, G + 1, NX], F32)
            w16 = sb(ctx, "w16", [P, G, NX], F32)
            col = sb(ctx, "col", [P, 8, G], F32)
            sidx = sb(ctx, "sidx", [P, G], I32)
            fin = sb(ctx, "fin", [P, 4, G], F32)
            normal = rows[:, 0, 0:2, :].bitcast(F32)
            pV = pb(ctx, "pV", [P, 2, D], F32)
            pT = [pb(ctx, f"pT3{j}", [P, DK, P], F32) for j in range(2)]
            pX = [pb(ctx, f"pX3{j}", [P, DK, P], F32) for j in range(2)]
            pW = [pb(ctx, f"pW3{j}", [P, D], F32) for j in range(2)]
            pR = pV[:, 0, 0:G * NX]
            pC = pV[:, 1, 0:2 * G * NX]
            block = ctx.enter_context(nc.Block())

            def unit_at(eng, u, which):
                within_ = ((0, NT - 1), (1, NT), (0, CQ * NT))
                return [eng.value_load(units[0:1, j, ds(u, 1)], min_val=within_[j][0], max_val=within_[j][1]) for j in which]

            def value(eng, register):
                return nc.s_assert_within(eng.snap(register), 1, CQ * NT + 3,
                                          skip_runtime_bounds_check_because="set to 1 or to a sum of 2 and more")

            def agg_at(t):
                return agg[:, ds(t, 1), :].rearrange("p a b -> p (a b)")

            def third(loop, tile, early, late, enter, leave):
                def steps(i, ahead, place):
                    for k, step in ahead.get(place, ()):
                        step(i, k)

                def body(i):
                    fixed = isinstance(i, int)
                    for k in range(G):
                        place = 0
                        for d, step in tile:
                            if step is not None:
                                i_, k_ = i + (k + d) // G, (k + d) % G
                                if not fixed or 0 <= i_ * G + k_ < NT:
                                    step(i_, k_)
                                continue
                            if not fixed or 0 <= i - 2 < G:
                                steps(i - 2, late, (k, place))
                            if not fixed or 0 <= i - 1 < G:
                                steps(i - 1, early, (k, place))
                            place += 1
                if tile and tile[0][0] > 0:
                    for k in range(tile[0][0]):
                        tile[0][1](0, k)
                body(0)
                body(1)
                with loop(2, G - 1) as i:
                    enter(i)
                    body(i)
                leave()
                for i in range(G - 1, G + 2):
                    body(i)

            def plan(**step):
                def table(places):
                    return {place: [(k, step[n]) for n, k in names if n in step] for place, names in places.items()}
                early = table({
                    (1, 0): (("stats", 0),),
                    (1, 1): (("scales", 0),),
                    (2, 0): (("norm", 0), ("norm", 1)),
                    (2, 1): (("turn", 0),),
                    (3, 0): (("turn", 1), ("norm", 2)),
                    (3, 1): (("logits", 0), ("turn", 2), ("norm", 3)),
                    (4, 0): (("logits", 1), ("turn", 3), ("norm", 4)),
                    (4, 1): (("logits", 2), ("turn", 4), ("norm", 5)),
                    (5, 0): (("logits", 3), ("turn", 5), ("norm", 6)),
                    (5, 1): (("logits", 4), ("turn", 6)),
                    (6, 0): (("logits", 5),),
                    (6, 1): (("logits", 6), ("routes", 0))})
                late = table({
                    (0, 1): (("cumulate", 0),),
                    (1, 0): (("place", 0),),
                    (1, 1): (("finish", 0),), (2, 0): (("finish", 1),),
                    (2, 1): (("finish", 2),), (3, 1): (("finish", 3),),
                    (4, 1): (("finish", 4),), (5, 1): (("finish", 5),),
                    (6, 0): (("finish", 6),)})
                return early, late

            def before(k):
                return FREE + 1 - lag(k)

            @block.gpsimd
            def _(pool):
                own = Steps(pool, s["pool"])
                nc.gpsimd.iota(iotah[:], [[1, P]], base=0, channel_multiplier=0, allow_small_or_imprecise_dtypes=True)
                nc.gpsimd.iota(bases[:], [[P, NT]], base=0, channel_multiplier=0, allow_small_or_imprecise_dtypes=True)
                nc.gpsimd.iota(trash[:], [[0, 1]], base=SLOTS, channel_multiplier=1, allow_small_or_imprecise_dtypes=True)
                nc.gpsimd.memset(zeroh[:], 0.0)
                own.step(nc.gpsimd.memset(tri[:], 1.0))
                nc.gpsimd.affine_select(out=tri[:, 0, :], in_=tri[:, 0, :], compare_op=ALU.is_ge, fill=0.0,
                                        base=0, pattern=[[1, P]], channel_multiplier=-1).then_inc(s["const"], 1)

                def issue(u, h):
                    wait_alone(pool, s["rows_used"], u + 1, s["fence"])
                    nc.gpsimd.tensor_copy(idx[:, h, :], srcT[:, ds(u * Q, Q)]).then_inc(s["idx"], 1)
                    wait_alone(pool, s["idx"], u + 1, s["fence"])
                    for k in range(Q):
                        nc.gpsimd.indirect_dma_start(
                            rows[:, h, k, :], None, xn2_rows,
                            bass.IndirectOffsetOnAxis(ap=idx[:, h, k:k + 1], axis=0)).then_inc(landed[h][k], 16)

                def drain(h, times):
                    for k in range(Q):
                        pool.wait_ge(landed[h][k], times * 16)
                    pool.sem_inc(s["rows_ready"], 1)

                issue(0, 0)
                issue(1, 1)
                with pool.Fori(0, CQ // 4 - 1) as i:
                    for h in range(4):
                        issue(i * 4 + (h + 2), (h + 2) % 4)
                        drain(h, i + 1)
                for h in range(4):
                    if h < 2:
                        issue(CQ - 2 + h, h + 2)
                    drain(h, CQ // 4)

                def finish(i, k):
                    T = i * G + k
                    wait_alone(pool, s["normed"], T + 1, s["fence"])
                    nc.gpsimd.indirect_dma_start(expert_rows, bass.IndirectOffsetOnAxis(ap=sidx[:, k:k + 1], axis=0),
                                                 normal[:, k % 2, :], None).then_inc(s["scatter"], 16)
                    wait_alone(pool, s["scatter"], T * 16 + 16, s["scattered"])

                third(pool.Fori, ((0, None), (0, None)), *plan(finish=finish), lambda i: None, lambda: None)

            @block.sync
            def _(sp):
                sp.dma_start(units[:], units_row).then_inc(s["tables_in"], 16)
                sp.dma_start(wg[:], Wg.rearrange("(m p) d -> p m d", p=P)).then_inc(s["w_in"], 16)
                sp.dma_start(bgb[:], bg.partition_broadcast(P)).then_inc(s["small_in"], 16)
                sp.dma_start(alp[:], alpha.partition_broadcast(P)).then_inc(s["small_in"], 16)
                sp.dma_start(sw[:], switch_w).then_inc(s["small_in"], 16)
                sp.dma_start(swb[:], switch_b.partition_broadcast(P)).then_inc(s["small_in"], 16)

                def load(i, k):
                    T = i * G + k
                    wait_alone(sp, s["x3"], T + 1, s["fence_sp"])
                    sp.dma_start(x2l[:, ds(T % 3, 1), :].rearrange("p a b -> p (a b)"), x2_rows[ds(T * P, P), :]).then_inc(s["loads"], 16)
                    sp.dma_start(pl[:, ds(T % 3, 1), :].rearrange("p a b -> p (a b)"), xn2_rows[ds(T * P, P), :]).then_inc(s["loads"], 16)
                    wait_alone(sp, s["loads"], T * 32 + 32, s["loaded"])

                def finish(i, k):
                    T = i * G + k
                    wait_alone(sp, s["z"], T + 1, s["fence_sp"])
                    sp.dma_start(z_rows[ds(T * P, P), :], zb[:, k % 2, :]).then_inc(s["stores"], 16)
                    wait_alone(sp, s["stores"], T * 16 + 16, s["stored"])

                third(sp.Fori, ((1, load), (0, None), (0, None)), *plan(finish=finish), lambda i: None, lambda: None)

            @block.tensor
            def _(pe):
                pe.wait_ge(s["w_in"], 16)
                for c in range(DK):
                    if c > 0:
                        pe.wait_ge(s["wT"], c)
                    for m in range(DK):
                        last = nc.tensor.transpose(pW[0][:, m * P:(m + 1) * P], wg[:, m, c * P:(c + 1) * P], ident[:])
                    last.then_inc(s["wT_ps"], 1)
                pe.wait_ge(s["small_in"], 64)
                for c in range(DK):
                    last = nc.tensor.transpose(pW[1][:, c * NX:(c + 1) * NX], sw[:, c * P:(c + 1) * P], ident[0:NX, 0:NX])
                last.then_inc(s["wT_ps"], 1)
                pe.wait_ge(s["wT"], DK + 1)
                pe.wait_ge(s["const"], 1)
                pe.wait_ge(s["tables_in"], 16)
                for n in ("aT_ps", "conv", "xT_ps", "logits"):
                    pe.sem_inc(s[n], FREE)
                nc.tensor.matmul(pV[:, 1, :], zeroh[:, 0:P], zeroh[:], start=True, stop=True).then_inc(s["mm_done"], 1)

                def visit(h):
                    for c in range(Q):
                        for m in range(2):
                            last = nc.tensor.matmul(pV[:, h % 2, :], oh[:, h % 2, c, :], rows[:, h, c, m * D:(m + 1) * D],
                                                    start=(c == 0 and m == 0), stop=(c == Q - 1 and m == 1))
                    last.then_inc(s["mm_done"], 1)

                free = pe.alloc_register("free")
                with pe.Fori(0, CQ // 4) as i:
                    for h in range(4):
                        u = i * 4 + h
                        tiles, visits = unit_at(pe, u, (1, 2))
                        pe.reg_mov(free, 1)
                        wait_alone(pe, s["rows_ready"], u + 1, s["fence_pe"])
                        with pe.Fori(0, tiles) as k:
                            wait_alone(pe, s["oh_ready"], visits + k + 1, s["fence_pe"])
                            wait_alone(pe, s["added"], value(pe, free), s["fence_pe"])
                            visit(h)
                            pe.reg_mov(free, visits + k + 3)

                def turn_sums(i, k):
                    T = i * G + k
                    wait_alone(pe, s["scaled"], T + 1, s["fence_pe"])
                    wait_alone(pe, s["aT"], T + before(k), s["fence_pe"])
                    for c in range(DK):
                        last = nc.tensor.transpose(pT[k % 2][:, c, :], scaled[:, k % 2, c * P:(c + 1) * P], ident[:])
                    last.then_inc(s["aT_ps"], 1)

                def convolve(i, k):
                    T = i * G + k
                    wait_alone(pe, s["aT"], T + (1 + FREE), s["fence_pe"])
                    wait_alone(pe, s["x3"], T + before(k), s["fence_pe"])
                    for c in range(DK):
                        last = nc.tensor.matmul(pW[k % 2][:], aT[:, k % 2, c, :], wgT[:, c, :], start=(c == 0), stop=(c == DK - 1))
                    last.then_inc(s["conv"], 1)

                def turn(i, k):
                    T = i * G + k
                    wait_alone(pe, s["xf"], T + 1, s["fence_pe"])
                    wait_alone(pe, s["xT"], T + before(k), s["fence_pe"])
                    for c in range(DK):
                        last = nc.tensor.transpose(pX[k % 2][:, c, :], xf[:, k % 2, c * P:(c + 1) * P], ident[:])
                    last.then_inc(s["xT_ps"], 1)

                def logits(i, k):
                    T = i * G + k
                    wait_alone(pe, s["xT"], T + (1 + FREE), s["fence_pe"])
                    if k == 0:
                        wait_alone(pe, s["lg"], i + 1, s["fence_pe"])
                    for c in range(DK):
                        last = nc.tensor.matmul(pR[:, k * NX:(k + 1) * NX], xfT[:, k % 2, c, :], swT[:, c, :],
                                                start=(c == 0), stop=(c == DK - 1))
                    last.then_inc(s["logits"], 1)

                def cumulate(i, _):
                    wait_alone(pe, s["onehot"], i + 1, s["fence_pe"])
                    for m in range(2):
                        last = nc.tensor.matmul(pC[:, m * G * NX:(m + 1) * G * NX], tri[:, m, :],
                                                oh16b[:].rearrange("p a b -> p (a b)"), start=True, stop=True)
                    last.then_inc(s["cum"], 1)

                third(pe.Fori, ((0, turn_sums), (0, None), (-1, convolve), (0, None)),
                      *plan(turn=turn, logits=logits, cumulate=cumulate), lambda i: None, lambda: None)

            @block.scalar
            def _(act):
                for c in range(DK):
                    act.wait_ge(s["wT_ps"], c + 1)
                    nc.scalar.copy(wgT[:, c, :], pW[0][:]).then_inc(s["wT"], 1)
                act.wait_ge(s["wT_ps"], DK + 1)
                nc.scalar.copy(swT[:].rearrange("p a b -> p (a b)"), pW[1][:, 0:DK * NX]).then_inc(s["wT"], 1)
                for n in ("aT", "xT"):
                    act.sem_inc(s[n], FREE)

                def sums_out(i, k):
                    T = i * G + k
                    act.wait_ge(s["aT_ps"], T + (1 + FREE))
                    act.wait_ge(s["conv"], T + before(k))
                    nc.scalar.copy(aT[:, k % 2], pT[k % 2][:]).then_inc(s["aT"], 1)

                def stats(i, _):
                    act.wait_ge(s["var"], i + 1)
                    nc.scalar.activation(rs[:, 0, :], var[:], ACT.Sqrt).then_inc(s["std"], 1)

                def norm(i, k):
                    T = i * G + k
                    act.wait_ge(s["rs"], i + 1)
                    wait_alone(act, s["xT_ps"], T + before(k), s["fence_act"])
                    nc.scalar.activation(xf[:, k % 2, :], agg_at(T), ACT.Identity, bias=rs[:, 1, k:k + 1],
                                         scale=rs[:, 0, k:k + 1]).then_inc(s["xf"], 1)

                def turn(i, k):
                    T = i * G + k
                    act.wait_ge(s["xT_ps"], T + (1 + FREE))
                    act.wait_ge(s["logits"], T + before(k))
                    nc.scalar.copy(xfT[:, k % 2], pX[k % 2][:]).then_inc(s["xT"], 1)

                def routes(i, _):
                    act.wait_ge(s["lg_done"], i + 1)
                    nc.scalar.activation(ex[:].rearrange("p a b -> p (a b)"), lg[:].rearrange("p a b -> p (a b)"),
                                         ACT.Exp).then_inc(s["expd"], 1)

                def finish(i, k):
                    T = i * G + k
                    act.wait_ge(s["placed"], i + 1)
                    wait_alone(act, s["stored"], T + before(k), s["fence_act"])
                    nc.scalar.activation(zb[:, k % 2, :], agg_at(T), ACT.Identity, bias=fin[:, 3, k:k + 1],
                                         scale=fin[:, 2, k:k + 1]).then_inc(s["z"], 1)
                    wait_alone(act, s["scattered"], T + before(k), s["fence_act"])
                    nc.scalar.activation(normal[:, k % 2, :], agg_at(T), ACT.Identity, bias=fin[:, 1, k:k + 1],
                                         scale=fin[:, 0, k:k + 1]).then_inc(s["normed"], 1)

                third(act.Fori, ((0, sums_out), (0, None), (0, None)),
                      *plan(stats=stats, norm=norm, turn=turn, routes=routes, finish=finish), lambda i: None, lambda: None)

            @block.vector
            def _(dve):
                own = Steps(dve, s["dve"])
                dve.sem_inc(s["rows_used"], 3)
                dve.sem_inc(s["x3"], FREE)
                dve.sem_inc(s["lg"], 1)
                dve.sem_inc(s["stored"], FREE)
                dve.sem_inc(s["scattered"], FREE)
                own.step(nc.vector.memset(base[:], 0.0))
                own.step(nc.vector.tensor_copy(dstF[:], dstT[:, 0:C]))
                own.step(nc.vector.memset(agg[:], 0.0))
                dve.sem_inc(s["added"], 1)
                dve.wait_ge(s["small_in"], 64)
                own.step(nc.vector.tensor_scalar(bgb[:], bgb[:], alp[:], None, ALU.mult))
                dve.wait_ge(s["const"], 1)
                dve.wait_ge(s["tables_in"], 16)
                pending = dve.alloc_register("pending")
                dve.reg_mov(pending, NT)

                bank = dve.alloc_register("bank")
                made = dve.alloc_register("made")
                dve.reg_mov(bank, 1)

                def within(tile, top_):
                    return nc.s_assert_within(tile, 0, top_, skip_runtime_bounds_check_because="block B's tables, NT, or a bank")

                def add_pending(v):
                    wait_alone(dve, s["mm_done"], v + 2, s["fence_dve"])
                    wait_alone(dve, s["added"], v + 2, s["fence_dve"])
                    at = agg_at(within(dve.snap(pending), NT))
                    nc.vector.tensor_tensor(at, at, pV[:, ds(within(dve.snap(bank), 1), 1), :].rearrange("p a b -> p (a b)"),
                                            ALU.add).then_inc(s["added"], 1)

                with dve.Fori(0, CQ // 4) as i:
                    for h in range(4):
                        u = i * 4 + h
                        first, tiles, visits = unit_at(dve, u, (0, 1, 2))
                        dve.reg_mov(made, 1)
                        with dve.Fori(0, tiles) as k:
                            tile = within(first + k, NT - 1)
                            wait_alone(dve, s["mm_done"], value(dve, made), s["fence_dve"])
                            nc.vector.scalar_tensor_tensor(
                                oh[:, h % 2], bc(iotah[:].unsqueeze(1), (P, Q, P)), bases[:, ds(tile, 1)],
                                bc(dstF[:, ds(u * Q, Q)].unsqueeze(2), (P, Q, P)), ALU.add, ALU.is_equal).then_inc(s["oh_ready"], 1)
                            add_pending(visits + k - 1)
                            dve.reg_mov(pending, tile)
                            dve.reg_mov(bank, h % 2)
                            dve.reg_mov(made, visits + k + 2)
                        dve.sem_inc(s["rows_used"], 1)
                tiles, visits = unit_at(dve, CQ - 1, (1, 2))
                add_pending(visits + tiles - 1)
                wait_alone(dve, s["added"], visits + tiles + 2, s["fence_dve"])

                def scale(i, k):
                    T = i * G + k
                    wait_alone(dve, s["aT_ps"], T + before(k), s["fence_dve"])
                    nc.vector.tensor_scalar(scaled[:, k % 2, :], agg_at(T), invdeg[:, ds(T, 1)], None,
                                            ALU.mult).then_inc(s["scaled"], 1)

                def residual(i, k):
                    T = i * G + k
                    wait_alone(dve, s["loaded"], T + 1, s["fence_dve"])
                    parts = pl[:, ds(T % 3, 1), :].rearrange("p a (m d) -> p (a m) d", m=2)
                    own.step(nc.vector.tensor_tensor(res[:], parts[:, 0, :], parts[:, 1, :], ALU.add))
                    own.step(nc.vector.tensor_tensor(res[:], res[:], x2l[:, ds(T % 3, 1), :].rearrange("p a b -> p (a b)"), ALU.add))
                    own.step(nc.vector.tensor_tensor(res[:], res[:], bgb[:], ALU.add))
                    wait_alone(dve, s["conv"], T + (1 + FREE), s["fence_dve"])
                    own.step(nc.vector.scalar_tensor_tensor(agg_at(T), pW[k % 2][:], alp[:], res[:], ALU.mult, ALU.add))
                    dve.sem_inc(s["x3"], 1)
                    own.step(nc.vector.bn_stats(st[:, k, :], agg_at(T)))

                def stats(i, _):
                    dve.sem_inc(s["fence_dve"], 1)
                    for k in range(G):
                        last = nc.vector.bn_aggr(mv[:, k, :], st[:, k, :])
                    own.step(last)
                    own.step(nc.vector.tensor_scalar_add(var[:], mv[:, :, 1], EPS))
                    dve.sem_inc(s["var"], 1)

                def scales(i, _):
                    wait_alone(dve, s["std"], i + 1, s["fence_dve"])
                    newton(nc, own, rs[:, 0, :], var[:], nw[:])
                    own.step(nc.vector.scalar_tensor_tensor(rs[:, 1, :], mv[:, :, 0], -1.0, rs[:, 0, :], ALU.mult, ALU.mult))
                    dve.sem_inc(s["rs"], 1)

                full = (P, G, NX)
                routes_of = bc(iota[:, 0:NX].unsqueeze(1), full)

                def routes(i, _):
                    wait_alone(dve, s["logits"], i * G + (G + FREE), s["fence_dve"])
                    own.step(nc.vector.tensor_tensor(lg[:], pR.rearrange("p (a b) -> p a b", b=NX), bc(swb[:].unsqueeze(1), full), ALU.add))
                    dve.sem_inc(s["lg"], 1)
                    own.step(nc.vector.tensor_reduce(top[:], lg[:], AX, ALU.max))
                    own.step(nc.vector.tensor_tensor(lg[:], lg[:], bc(top[:].unsqueeze(2), full), ALU.subtract))
                    dve.sem_inc(s["lg_done"], 1)
                    own.step(nc.vector.tensor_scalar(other[:], lg[:], 0.0, float(NX), ALU.is_lt, ALU.mult))
                    own.step(nc.vector.tensor_tensor(other[:], other[:], routes_of, ALU.add))
                    own.step(nc.vector.tensor_reduce(rt[:], other[:], AX, ALU.min))
                    own.step(nc.vector.tensor_tensor(oh16[:], routes_of, bc(rt[:].unsqueeze(2), full), ALU.is_equal))
                    own.step(nc.vector.tensor_copy(oh16b[:], oh16[:]))
                    dve.sem_inc(s["onehot"], 1)

                def place(i, _):
                    c = [col[:, j, :] for j in range(8)]
                    at = ds(i * G, G)
                    wait_alone(dve, s["cum"], i + 1, s["fence_dve"])
                    wait_alone(dve, s["scattered"], i * G + FREE, s["fence_dve"])
                    for k in range(G):
                        own.step(nc.vector.tensor_tensor(base[:, k + 1, :], pC[:, (G + k) * NX:(G + k + 1) * NX], base[:, k, :], ALU.add))
                    own.step(nc.vector.tensor_tensor(w16[:], pC[:, 0:G * NX].rearrange("p (a b) -> p a b", b=NX), base[:, 0:G, :], ALU.add))
                    nc.vector.tensor_copy(base[:, 0, :], base[:, G, :])
                    own.step(nc.vector.tensor_tensor(w16[:], w16[:], oh16[:], ALU.mult))
                    own.step(nc.vector.tensor_reduce(c[0], w16[:], AX, ALU.add))
                    own.step(nc.vector.tensor_scalar(c[1], c[0], float(CAP), None, ALU.is_le))
                    own.step(nc.vector.scalar_tensor_tensor(c[2], rt[:], float(CAP), c[0], ALU.mult, ALU.add))
                    own.step(nc.vector.tensor_scalar_add(c[2], c[2], -1.0))
                    nc.vector.tensor_tensor(gidx[:, at], c[2], c[1], ALU.mult)
                    own.step(nc.vector.tensor_scalar(c[3], c[2], trash[:], None, ALU.subtract))
                    own.step(nc.vector.tensor_tensor(c[3], c[3], c[1], ALU.mult))
                    nc.vector.tensor_scalar(sidx[:], c[3], trash[:], None, ALU.add)
                    wait_alone(dve, s["expd"], i + 1, s["fence_dve"])
                    own.step(nc.vector.tensor_reduce(c[4], ex[:], AX, ALU.add))
                    own.step(nc.vector.reciprocal(c[4], c[4]))
                    own.step(nc.vector.tensor_mul(c[5], c[4], c[1]))
                    nc.vector.tensor_copy(pkeep[:, at], c[5])
                    own.step(nc.vector.tensor_sub(c[6], c[4], c[5]))
                    own.step(nc.vector.tensor_mul(c[7], c[6], rs[:, 0, :]))
                    nc.vector.tensor_copy(fin[:, 0:2, :], rs[:])
                    nc.vector.tensor_scalar_add(fin[:, 2, :], c[7], 1.0)
                    own.step(nc.vector.tensor_mul(fin[:, 3, :], c[6], rs[:, 1, :]))
                    dve.sem_inc(s["placed"], 1)

                third(dve.Fori, ((1, scale), (0, None), (-1, residual), (0, None)),
                      *plan(stats=stats, scales=scales, routes=routes, place=place),
                      lambda i: own.body(i, G * 5 + 2 + 6 + 8 + (G + 8 + 4 + 2), 2), lambda: own.end(G - 3))

        next_stage()
        s = {n: sem("e_" + n) for n in (
            "y_free y_stored wT_ps wT xT_ps xT y y_ps fence_sp fence_pe fence_dve".split())}
        w_in = [sem(f"e_w_in{j}") for j in range(2)]
        b_in = [sem(f"e_b_in{j}") for j in range(2)]
        r_in = [sem(f"e_r_in{j}") for j in range(ET)]
        y_out = [sem(f"e_y_out{j}") for j in range(ET)]
        with ExitStack() as ctx:
            we = sb(ctx, "we", [P, 2, DK, D], F32)
            weT = sb(ctx, "weT", [P, DK, D], F32)
            be = sb(ctx, "be", [P, 2, D], F32)
            er = sb(ctx, "er", [P, ET, D], F32)
            erT = sb(ctx, "erT", [P, 2, DK, P], F32)
            ye = sb(ctx, "ye", [P, ET, D], F32)
            pWT = [pb(ctx, f"pWT{j}", [P, DK, P], F32) for j in range(2)]
            pXT = [pb(ctx, f"pXT{j}", [P, DK, P], F32) for j in range(2)]
            pY = [pb(ctx, f"pY{j}", [P, D], F32) for j in range(2)]
            block = ctx.enter_context(nc.Block())
            sizes = [min(P, CAP - j * P) for j in range(ET)]

            @block.sync
            def _(sp):
                def load_w(e, j):
                    sp.dma_start(we[:, j, :, :], expert_w[ds(e, 1), :, :].rearrange("a (m p) d -> p (a m) d", p=P)).then_inc(w_in[j], 16)
                    sp.dma_start(be[:, j, :], expert_b[ds(e, 1), :].rearrange("a b -> (a b)").partition_broadcast(P)).then_inc(b_in[j], 16)

                sp.sem_inc(s["y_stored"], ET)
                def load_rows(e, m):
                    sp.dma_start(er[0:sizes[m], m, :], expert_rows[ds(e * CAP + m * P, sizes[m]), :]).then_inc(r_in[m], 16)

                load_w(0, 0)
                for m in range(ET):
                    load_rows(0, m)
                load_w(1, 1)
                with sp.Fori(0, NX // 2) as i:
                    for j in range(2):
                        e = i * 2 + j
                        for m, n in enumerate(sizes):
                            wait_alone(sp, s["xT_ps"], e * ET + (ET + m + 1), s["fence_sp"])
                            load_rows((e + 1) % NX, m)
                            wait_alone(sp, s["y"], e * ET + (m + 3), s["fence_sp"])
                            sp.dma_start(y_rows[ds(e * CAP + m * P, n), :], ye[0:n, m, :]).then_inc(y_out[m], 16)
                        for m in range(ET):
                            wait_alone(sp, y_out[m], (e + 1) * 16, s["y_stored"])
                        nxt = (e + 2) % NX
                        load_w(nxt, j)
                for j in range(2):
                    sp.wait_ge(w_in[j], (NX // 2 + 1) * 16)
                    sp.wait_ge(b_in[j], (NX // 2 + 1) * 16)
                for m in range(ET):
                    sp.wait_ge(r_in[m], (NX + 1) * 16)
                    sp.wait_ge(y_out[m], NX * 16)

            @block.tensor
            def _(pe):
                pe.sem_inc(s["xT_ps"], ET)
                pe.sem_inc(s["wT"], 2)
                pe.sem_inc(s["xT"], 2)
                pe.sem_inc(s["y"], 2)
                with pe.Fori(0, NX // 2) as i:
                    for j in range(2):
                        e = i * 2 + j
                        wait_alone(pe, w_in[j], (i + 1) * 16, s["fence_pe"])
                        for c in range(DK):
                            wait_alone(pe, s["wT"], e * DK + (c + 1), s["fence_pe"])
                            for m in range(DK):
                                last = nc.tensor.transpose(pWT[c % 2][:, m, :], we[:, j, m, c * P:(c + 1) * P], ident[:])
                            last.then_inc(s["wT_ps"], 1)

                        def product(m):
                            n = sizes[m]
                            wait_alone(pe, s["xT"], e * ET + (m + 3), s["fence_pe"])
                            if m == 0:
                                wait_alone(pe, s["wT"], e * DK + (DK + 2), s["fence_pe"])
                            wait_alone(pe, s["y"], e * ET + (m + 1), s["fence_pe"])
                            for c in range(DK):
                                last = nc.tensor.matmul(pY[m % 2][0:n, :], erT[:, m % 2, c, 0:n], weT[:, c, :],
                                                        start=(c == 0), stop=(c == DK - 1))
                            last.then_inc(s["y_ps"], 1)

                        for m, n in enumerate(sizes):
                            wait_alone(pe, r_in[m], (e + 1) * 16, s["fence_pe"])
                            wait_alone(pe, s["xT"], e * ET + (m + 1), s["fence_pe"])
                            for c in range(DK):
                                last = nc.tensor.transpose(pXT[m % 2][:, c, 0:n], er[0:n, m, c * P:(c + 1) * P], ident[0:n, 0:n])
                            last.then_inc(s["xT_ps"], 1)
                            if m > 0:
                                product(m - 1)
                        product(ET - 1)

            @block.scalar
            def _(act):
                act.sem_inc(s["y_free"], 1)
                with act.Fori(0, NX // 2) as i:
                    for j in range(2):
                        e = i * 2 + j
                        for c in range(DK):
                            act.wait_ge(s["wT_ps"], e * DK + (c + 1))
                            act.wait_ge(s["y_free"], e * ET + 1)
                            nc.scalar.copy(weT[:, c, :], pWT[c % 2][:].rearrange("p a b -> p (a b)")).then_inc(s["wT"], 1)
                        for m, n in enumerate(sizes):
                            act.wait_ge(s["xT_ps"], e * ET + (m + 1 + ET))
                            if m >= 2:
                                act.wait_ge(s["y_ps"], e * ET + (m - 1))
                            nc.scalar.copy(erT[:, m % 2, :, 0:n], pXT[m % 2][:, :, 0:n]).then_inc(s["xT"], 1)

            @block.vector
            def _(dve):
                with dve.Fori(0, NX // 2) as i:
                    for j in range(2):
                        e = i * 2 + j
                        wait_alone(dve, b_in[j], (i + 1) * 16, s["fence_dve"])
                        for m, n in enumerate(sizes):
                            wait_alone(dve, s["y_ps"], e * ET + (m + 1), s["fence_dve"])
                            dve.sem_inc(s["y_free"], 1)
                            wait_alone(dve, s["y_stored"], e * ET + (m + 1), s["fence_dve"])
                            nc.vector.tensor_tensor(ye[0:n, m, :], pY[m % 2][0:n, :], be[0:n, j, :], ALU.add).then_inc(s["y"], 1)

        next_stage()
        s = {n: sem("f_" + n) for n in "idx fence fence_sp fence_dve done out_free".split()}
        y_in, z_in, o_out = ([sem(f"f_{n}{k}") for k in range(G)] for n in ("y_in", "z_in", "o_out"))
        with ExitStack() as ctx:
            idx = sb(ctx, "idx4", [P, G], I32)
            yl = sb(ctx, "yl", [P, G, D], F32)
            zl = sb(ctx, "zl", [P, G, D], F32)
            ol = sb(ctx, "ol4", [P, G, D], F32)
            block = ctx.enter_context(nc.Block())

            @block.gpsimd
            def _(pool):
                with pool.Fori(0, G) as i:
                    wait_alone(pool, s["done"], i * G + 1, s["fence"])
                    nc.gpsimd.tensor_copy(idx[:], gidx[:, ds(i * G, G)]).then_inc(s["idx"], 1)
                    wait_alone(pool, s["idx"], i + 1, s["fence"])
                    for k in range(G):
                        nc.gpsimd.indirect_dma_start(yl[:, k, :], None, y_rows,
                                                     bass.IndirectOffsetOnAxis(ap=idx[:, k:k + 1], axis=0)).then_inc(y_in[k], 16)

            @block.sync
            def _(sp):
                def load(i, k):
                    sp.dma_start(zl[:, k, :], z_rows[ds((i * G + k) * P, P), :]).then_inc(z_in[k], 16)

                def store(i, k, rows=P):
                    wait_alone(sp, s["done"], i * G + (k + 2), s["fence_sp"])
                    sp.dma_start(out[ds((i * G + k) * P, rows), :], ol[0:rows, k, :]).then_inc(o_out[k], 16)

                for k in range(G):
                    load(0, k)
                with sp.Fori(0, G - 1) as i:
                    for k in range(G):
                        store(i, k)
                        load(i + 1, k)
                    for k in range(G):
                        wait_alone(sp, o_out[k], (i + 1) * 16, s["out_free"])
                for k in range(G):
                    store(G - 1, k, P if k < G - 1 else LAST)
                for k in range(G):
                    sp.wait_ge(o_out[k], G * 16)

            @block.vector
            def _(dve):
                dve.sem_inc(s["done"], 1)
                dve.sem_inc(s["out_free"], G)
                with dve.Fori(0, G) as i:
                    for k in range(G):
                        T = i * G + k
                        wait_alone(dve, y_in[k], (i + 1) * 16, s["fence_dve"])
                        wait_alone(dve, z_in[k], (i + 1) * 16, s["fence_dve"])
                        wait_alone(dve, s["out_free"], T + 1, s["fence_dve"])
                        nc.vector.scalar_tensor_tensor(ol[:, k, :], yl[:, k, :], pkeep[:, ds(T, 1)], zl[:, k, :],
                                                       ALU.mult, ALU.add).then_inc(s["done"], 1)
        route.close()


def scan(nc, own, rows, a, b, n, op):
    d = 1
    while d < n:
        own.step(nc.vector.tensor_copy(rows[b], rows[a]))
        own.step(nc.vector.tensor_tensor(rows[b][:, d:n], rows[a][:, d:n], rows[a][:, 0:n - d], op))
        a, b, d = b, a, 2 * d
    return a, b


NEWTON = 5


def newton(nc, own, r, v, t):
    own.step(nc.vector.reciprocal(r, r))
    own.step(nc.vector.tensor_mul(t, v, r))
    own.step(nc.vector.tensor_mul(t, t, r))
    own.step(nc.vector.tensor_scalar(t, t, -0.5, 1.5, ALU.mult, ALU.add))
    own.step(nc.vector.tensor_mul(r, r, t))


def split3(nc, own, out3, val, rest):
    parts = [out3[:, :, j * H:(j + 1) * H] for j in range(3)]
    r = [rest[:, j, :].rearrange("p (t f) -> p t f", f=H) for j in range(2)]
    own.step(nc.vector.tensor_copy(parts[0], val[:]))
    own.step(nc.vector.tensor_tensor(r[0], val[:], parts[0], ALU.subtract))
    own.step(nc.vector.tensor_copy(parts[1], r[0]))
    own.step(nc.vector.tensor_tensor(r[1], r[0], parts[1], ALU.subtract))
    own.step(nc.vector.tensor_copy(parts[2], r[1]))


_INS = ['x', 'src', 'dst', 'node_vec1', 'L0_gnn_W1', 'L0_gnn_b1', 'L0_gnn_gamma', 'L0_gnn_beta', 'L0_gnn_W2',
        'L0_gnn_b2', 'L0_ffn_w_gate', 'L0_ffn_w_up', 'L0_ffn_w_down', 'L1_gnn_alpha', 'L1_gnn_W', 'L1_gnn_b',
        'L1_ffn_switch_w', 'L1_ffn_switch_b', 'L1_ffn_expert_w', 'L1_ffn_expert_b']


def kernel(**inputs):
    import numpy as np
    import concourse.bacc as bacc
    from concourse.bass_utils import run_bass_kernel_spmd

    nc = bacc.Bacc("TRN2", target_bir_lowering=False, num_devices=1)
    arrays, args = {}, []
    for name in _INS:
        a = np.ascontiguousarray(inputs[name])
        if a.ndim == 0:
            a = a.reshape(1)
        arrays[f"in_{name}"] = a
        args.append(nc.dram_tensor(f"in_{name}", a.shape, mybir.dt.from_np(a.dtype), kind="ExternalInput").ap())
    args.append(nc.dram_tensor("out_0", (N, D), F32, kind="ExternalOutput").ap())
    program(nc, *args)
    r = run_bass_kernel_spmd(nc, [arrays], core_ids=[0])
    return r.results[0]["out_0"]
```
